# Optimizing a Trainium2 kernel written in Bass

```python
import numpy as np
import jax
import jax.numpy as jnp

def _softmax(x, axis=-1):
    return jax.nn.softmax(x, axis=axis)

def _gelu(x):
    return jax.nn.gelu(x, approximate=True)

def _silu(x):
    return jax.nn.silu(x)

def _sigmoid(x):
    return jax.nn.sigmoid(x)

def _layernorm(x, axis=-1, eps=1e-05):
    m = jnp.mean(x, axis=axis, keepdims=True)
    v = jnp.var(x, axis=axis, keepdims=True)
    return (x - m) / jnp.sqrt(v + eps)

def _scatter_add(tgt, idx, src, axis=0):
    return tgt.at[idx].add(src)

def _segment_sum(src, seg, n):
    return jax.ops.segment_sum(src, seg, n)
kernel_name = 'mk_early_fusion_embed_d2_tok_img768_r4_3f057c'

def setup_inputs(seed: int=0):
    np.random.seed(seed)
    _w = jnp.asarray

    def _rec_inputs():
        import jax
        import jax.numpy as jnp
        _rk = jax.random.key(seed)
        x = -0.00016672 + 0.999947 * jax.random.normal(jax.random.fold_in(_rk, 1), (32, 3, 96, 96), jnp.float32)
        x_txt = jax.random.randint(jax.random.fold_in(_rk, 51), (32, 77), 0, 31993, jnp.int32)
        return (x, x_txt)
    x, x_txt = _rec_inputs()

    def _L0_tok_setup():
        import jax, jax.numpy as jnp
        import numpy as np
        P = 16
        EPS = 1e-05
        key = jax.random.key(seed)
        ks = jax.random.split(key, 6)
        B, C, H = (64, 3, 96)
        E = 192
        L = (H // P) ** 2
        patch_dim = C * P * P
        return {'x': jax.random.normal(ks[0], (B, C, H, H), dtype=jnp.float32), 'ln_w': jnp.ones((C, H, H), dtype=jnp.float32), 'ln_b': jnp.zeros((C, H, H), dtype=jnp.float32), 'conv_w': jax.random.normal(ks[1], (C, C, 1, 1), dtype=jnp.float32) * 0.1, 'conv_b': jax.random.normal(ks[2], (C,), dtype=jnp.float32) * 0.1, 'proj_w': jax.random.normal(ks[3], (E, patch_dim), dtype=jnp.float32) * 0.02, 'proj_b': jax.random.normal(ks[4], (E,), dtype=jnp.float32) * 0.02, 'pos_emb': jax.random.normal(ks[5], (1, L, E), dtype=jnp.float32) * 0.02}
    _L0_tok_all = _L0_tok_setup()
    _L0_tok_in = {k: v for k, v in _L0_tok_all.items() if k in ('ln_w', 'ln_b', 'conv_w', 'conv_b', 'proj_w', 'proj_b', 'pos_emb')}
    del _L0_tok_all

    def _L0_txt_setup():
        import jax, jax.numpy as jnp
        import numpy as np
        VOCAB = 8000
        key = jax.random.key(seed)
        k1, k2 = jax.random.split(key)
        input_ids = jax.random.randint(k1, (4, 512), 0, VOCAB, dtype=jnp.int64 if jax.config.jax_enable_x64 else jnp.int32)
        weight = jax.random.normal(k2, (VOCAB, 192), dtype=jnp.float32)
        return {'input_ids': input_ids, 'weight': weight}
    _L0_txt_all = _L0_txt_setup()
    _L0_txt_in = {k: v for k, v in _L0_txt_all.items() if k in ('weight',)}
    del _L0_txt_all

    def _L0_attn_setup():
        import jax, jax.numpy as jnp
        import numpy as np
        B, N, C = (32, 256, 192)
        H = 12
        E = C // H
        SCALE = E ** (-0.5)
        EPS = 1e-06
        key = jax.random.key(seed)
        k1, k2, k3 = jax.random.split(key, 3)
        x = jax.random.normal(k1, (B, N, C), dtype=jnp.float32)
        qkv_w = jax.random.normal(k2, (3 * C, C), dtype=jnp.float32) * C ** (-0.5)
        proj_w = jax.random.normal(k3, (C, C), dtype=jnp.float32) * C ** (-0.5)
        proj_b = jnp.zeros((C,), dtype=jnp.float32)
        return {'x': x, 'qkv_w': qkv_w, 'proj_w': proj_w, 'proj_b': proj_b}
    _L0_attn_all = _L0_attn_setup()
    _L0_attn_in = {k: v for k, v in _L0_attn_all.items() if k in ('qkv_w', 'proj_w', 'proj_b')}
    del _L0_attn_all

    def _L0_ffn_setup():
        import jax, jax.numpy as jnp
        import numpy as np
        B, T, H, F, E = (128, 32, 192, 768, 3)
        key = jax.random.key(seed)
        ks = jax.random.split(key, 4)
        s = 0.02
        return {'x': jax.random.normal(ks[0], (B, T, H), jnp.float32), 'Wg': jax.random.normal(ks[1], (E, H), jnp.float32) * s, 'W1': jax.random.normal(ks[2], (E, H, F), jnp.float32) * s, 'b1': jnp.zeros((E, F), jnp.float32), 'W2': jax.random.normal(ks[3], (E, F, H), jnp.float32) * s, 'b2': jnp.zeros((E, H), jnp.float32)}
    _L0_ffn_all = _L0_ffn_setup()
    _L0_ffn_in = {k: v for k, v in _L0_ffn_all.items() if k in ('Wg', 'W1', 'b1', 'W2', 'b2')}
    del _L0_ffn_all

    def _L1_attn_setup():
        import jax, jax.numpy as jnp
        import numpy as np
        DIM = 192
        H = 12
        HD = DIM // H
        TTT_BASE_LR = 1.0
        EPS = 1e-06

        def ln_fwd(x, gamma, beta):
            mu = jnp.mean(x, axis=-1, keepdims=True)
            var = jnp.mean((x - mu) ** 2, axis=-1, keepdims=True)
            x_hat = (x - mu) / jnp.sqrt(var + EPS)
            return gamma * x_hat + beta

        def ln_fused_l2_bwd(x, l2_target, gamma, beta):
            D = x.shape[-1]
            mu = jnp.mean(x, axis=-1, keepdims=True)
            var = jnp.mean((x - mu) ** 2, axis=-1, keepdims=True)
            std = jnp.sqrt(var + EPS)
            x_hat = (x - mu) / std
            y = gamma * x_hat + beta
            grad_out = y - l2_target
            g = grad_out * gamma
            z = (D * g - jnp.sum(g, -1, keepdims=True) - x_hat * jnp.sum(g * x_hat, -1, keepdims=True)) / (D * std)
            return z
        key = jax.random.key(seed)
        ks = jax.random.split(key, 10)
        B, N, C = (16, 256, DIM)
        return {'x': jax.random.normal(ks[0], (B, N, C), jnp.float32), 'qkv_weight': jax.random.normal(ks[1], (3 * C, C), jnp.float32) * 0.02, 'q_bias': jnp.zeros((C,), jnp.float32), 'v_bias': jnp.zeros((C,), jnp.float32), 'proj_weight': jax.random.normal(ks[2], (C, C), jnp.float32) * 0.02, 'proj_bias': jnp.zeros((C,), jnp.float32), 'ttt_lr_weight': jax.random.normal(ks[3], (H, 1, C), jnp.float32) * 0.02, 'ttt_lr_bias': jnp.zeros((H, 1), jnp.float32), 'ttt_norm_weight': jnp.ones((H, HD), jnp.float32), 'ttt_norm_bias': jnp.zeros((H, HD), jnp.float32), 'W1': jax.random.normal(ks[4], (H, HD, HD), jnp.float32) * 0.02, 'b1': jnp.zeros((H, 1, HD), jnp.float32)}
    _L1_attn_all = _L1_attn_setup()
    _L1_attn_in = {k: v for k, v in _L1_attn_all.items() if k in ('qkv_weight', 'q_bias', 'v_bias', 'proj_weight', 'proj_bias', 'ttt_lr_weight', 'ttt_lr_bias', 'ttt_norm_weight', 'ttt_norm_bias', 'W1', 'b1')}
    del _L1_attn_all

    def _L1_ffn_setup():
        import jax, jax.numpy as jnp
        import numpy as np
        B, S, H = (2, 256, 192)
        E, K, I = (16, 4, 192)
        ALPHA, LIMIT, EPS = (1.702, 7.0, 1e-05)

        def _swiglu(h):
            x_glu, x_lin = jnp.split(h, 2, axis=-1)
            x_glu = jnp.minimum(x_glu, LIMIT)
            x_lin = jnp.clip(x_lin, -LIMIT, LIMIT)
            return x_glu * jax.nn.sigmoid(ALPHA * x_glu) * (x_lin + 1.0)
        key = jax.random.key(seed)
        ks = jax.random.split(key, 7)
        x = jax.random.normal(ks[0], (B, S, H), dtype=jnp.float32)
        scale = jnp.ones((H,), jnp.float32)
        gate_w = jax.random.normal(ks[1], (E, H), jnp.float32) * 0.02
        gate_b = jnp.zeros((E,), jnp.float32)
        w1 = jax.random.normal(ks[2], (E, H, 2 * I), jnp.float32) * 0.02
        b1 = jax.random.normal(ks[3], (E, 2 * I), jnp.float32) * 0.02
        w2 = jax.random.normal(ks[4], (E, I, H), jnp.float32) * 0.02
        b2 = jax.random.normal(ks[5], (E, H), jnp.float32) * 0.02
        return {'x': x, 'scale': scale, 'gate_w': gate_w, 'gate_b': gate_b, 'w1': w1, 'b1': b1, 'w2': w2, 'b2': b2}
    _L1_ffn_all = _L1_ffn_setup()
    _L1_ffn_in = {k: v for k, v in _L1_ffn_all.items() if k in ('scale', 'gate_w', 'gate_b', 'w1', 'b1', 'w2', 'b2')}
    del _L1_ffn_all
    return {'x': x, 'x_txt': x_txt, 'L0_tok_ln_w': _L0_tok_in['ln_w'], 'L0_tok_ln_b': _L0_tok_in['ln_b'], 'L0_tok_conv_w': _L0_tok_in['conv_w'], 'L0_tok_conv_b': _L0_tok_in['conv_b'], 'L0_tok_proj_w': _L0_tok_in['proj_w'], 'L0_tok_proj_b': _L0_tok_in['proj_b'], 'L0_tok_pos_emb': _L0_tok_in['pos_emb'], 'L0_txt_weight': _L0_txt_in['weight'], 'L0_attn_qkv_w': _L0_attn_in['qkv_w'], 'L0_attn_proj_w': _L0_attn_in['proj_w'], 'L0_attn_proj_b': _L0_attn_in['proj_b'], 'L0_ffn_Wg': _L0_ffn_in['Wg'], 'L0_ffn_W1': _L0_ffn_in['W1'], 'L0_ffn_b1': _L0_ffn_in['b1'], 'L0_ffn_W2': _L0_ffn_in['W2'], 'L0_ffn_b2': _L0_ffn_in['b2'], 'L1_attn_qkv_weight': _L1_attn_in['qkv_weight'], 'L1_attn_q_bias': _L1_attn_in['q_bias'], 'L1_attn_v_bias': _L1_attn_in['v_bias'], 'L1_attn_proj_weight': _L1_attn_in['proj_weight'], 'L1_attn_proj_bias': _L1_attn_in['proj_bias'], 'L1_attn_ttt_lr_weight': _L1_attn_in['ttt_lr_weight'], 'L1_attn_ttt_lr_bias': _L1_attn_in['ttt_lr_bias'], 'L1_attn_ttt_norm_weight': _L1_attn_in['ttt_norm_weight'], 'L1_attn_ttt_norm_bias': _L1_attn_in['ttt_norm_bias'], 'L1_attn_W1': _L1_attn_in['W1'], 'L1_attn_b1': _L1_attn_in['b1'], 'L1_ffn_scale': _L1_ffn_in['scale'], 'L1_ffn_gate_w': _L1_ffn_in['gate_w'], 'L1_ffn_gate_b': _L1_ffn_in['gate_b'], 'L1_ffn_w1': _L1_ffn_in['w1'], 'L1_ffn_b1': _L1_ffn_in['b1'], 'L1_ffn_w2': _L1_ffn_in['w2'], 'L1_ffn_b2': _L1_ffn_in['b2']}

def reference(x, x_txt, L0_tok_ln_w, L0_tok_ln_b, L0_tok_conv_w, L0_tok_conv_b, L0_tok_proj_w, L0_tok_proj_b, L0_tok_pos_emb, L0_txt_weight, L0_attn_qkv_w, L0_attn_proj_w, L0_attn_proj_b, L0_ffn_Wg, L0_ffn_W1, L0_ffn_b1, L0_ffn_W2, L0_ffn_b2, L1_attn_qkv_weight, L1_attn_q_bias, L1_attn_v_bias, L1_attn_proj_weight, L1_attn_proj_bias, L1_attn_ttt_lr_weight, L1_attn_ttt_lr_bias, L1_attn_ttt_norm_weight, L1_attn_ttt_norm_bias, L1_attn_W1, L1_attn_b1, L1_ffn_scale, L1_ffn_gate_w, L1_ffn_gate_b, L1_ffn_w1, L1_ffn_b1, L1_ffn_w2, L1_ffn_b2):
    import jax
    import jax.numpy as jnp

    def _L0_tok_ref(x, ln_w, ln_b, conv_w, conv_b, proj_w, proj_b, pos_emb):
        import jax, jax.numpy as jnp
        import numpy as np
        P = 16
        EPS = 1e-05
        B, C, H, W = x.shape
        mu = jnp.mean(x, axis=(1, 2, 3), keepdims=True)
        var = jnp.var(x, axis=(1, 2, 3), keepdims=True)
        xn = (x - mu) * jax.lax.rsqrt(var + EPS) * ln_w + ln_b
        w = conv_w[:, :, 0, 0]
        xc = jnp.einsum('bchw,oc->bohw', xn, w) + conv_b[None, :, None, None]
        hp, wp = (H // P, W // P)
        patches = xc.reshape(B, C, hp, P, wp, P)
        patches = patches.transpose(0, 2, 4, 1, 3, 5).reshape(B, hp * wp, C * P * P)
        tokens = jnp.einsum('bld,ed->ble', patches, proj_w) + proj_b
        return tokens + pos_emb

    def _L0_txt_ref(input_ids, weight):
        import jax, jax.numpy as jnp
        import numpy as np
        VOCAB = 8000
        one_hot = jax.nn.one_hot(input_ids, VOCAB, dtype=weight.dtype)
        return jnp.einsum('bsv,vd->bsd', one_hot, weight)

    def _L0_attn_ref(x, qkv_w, proj_w, proj_b):
        import jax, jax.numpy as jnp
        import numpy as np
        B, N, C = (32, 256, 192)
        H = 12
        E = C // H
        SCALE = E ** (-0.5)
        EPS = 1e-06
        b, n, c = x.shape
        qkv = jnp.einsum('bnc,dc->bnd', x, qkv_w).reshape(b, n, 3, H, E)
        q = qkv[:, :, 0]
        k = qkv[:, :, 1]
        v = qkv[:, :, 2]
        q_ = jax.nn.relu(q) + SCALE
        k_ = jax.nn.relu(k) + SCALE
        kv = jnp.einsum('bnhe,bnhd->bhed', k_, v)
        k_sum = jnp.sum(k_, axis=1)
        z = 1.0 / (jnp.einsum('bnhe,bhe->bnh', q_, k_sum) + EPS)
        out = jnp.einsum('bnhe,bhed->bnhd', q_, kv) * z[..., None]
        out = out.reshape(b, n, c)
        return jnp.einsum('bnc,dc->bnd', out, proj_w) + proj_b

    def _L0_ffn_ref(x, Wg, W1, b1, W2, b2):
        import jax, jax.numpy as jnp
        import numpy as np
        B, T, H, F, E = (128, 32, 192, 768, 3)
        scores = jax.nn.softmax(jnp.mean(x, axis=1) @ Wg.T, axis=-1)
        _, idx = jax.lax.top_k(scores, 1)
        sel = idx[:, 0]
        h = jax.nn.gelu(jnp.einsum('bth,ehf->betf', x, W1) + b1[None, :, None, :], approximate=False)
        y = jnp.einsum('betf,efh->beth', h, W2) + b2[None, :, None, :]
        w = scores * jax.nn.one_hot(sel, E, dtype=scores.dtype)
        out = jnp.einsum('beth,be->bth', y, w)
        return out

    def _L1_attn_ref(x, qkv_weight, q_bias, v_bias, proj_weight, proj_bias, ttt_lr_weight, ttt_lr_bias, ttt_norm_weight, ttt_norm_bias, W1, b1):
        import jax, jax.numpy as jnp
        import numpy as np
        DIM = 192
        H = 12
        HD = DIM // H
        TTT_BASE_LR = 1.0
        EPS = 1e-06

        def ln_fwd(x, gamma, beta):
            mu = jnp.mean(x, axis=-1, keepdims=True)
            var = jnp.mean((x - mu) ** 2, axis=-1, keepdims=True)
            x_hat = (x - mu) / jnp.sqrt(var + EPS)
            return gamma * x_hat + beta

        def ln_fused_l2_bwd(x, l2_target, gamma, beta):
            D = x.shape[-1]
            mu = jnp.mean(x, axis=-1, keepdims=True)
            var = jnp.mean((x - mu) ** 2, axis=-1, keepdims=True)
            std = jnp.sqrt(var + EPS)
            x_hat = (x - mu) / std
            y = gamma * x_hat + beta
            grad_out = y - l2_target
            g = grad_out * gamma
            z = (D * g - jnp.sum(g, -1, keepdims=True) - x_hat * jnp.sum(g * x_hat, -1, keepdims=True)) / (D * std)
            return z
        B, N, C = x.shape
        num_mini_batch = 1
        m = N // num_mini_batch
        qkv_bias = jnp.concatenate([q_bias, jnp.zeros_like(q_bias), v_bias])
        qkv = x @ qkv_weight.T + qkv_bias
        qkv = qkv.reshape(B, N, 3, H, HD).transpose(2, 0, 3, 1, 4)
        q, k, v = (qkv[0], qkv[1], qkv[2])
        ttt_lr = jnp.einsum('bnc,hdc->bhnd', x, ttt_lr_weight) + ttt_lr_bias.reshape(1, H, 1, 1)
        ttt_lr_eta = TTT_BASE_LR * jax.nn.sigmoid(ttt_lr) / HD
        gamma = ttt_norm_weight.reshape(H, 1, HD)
        beta = ttt_norm_bias.reshape(H, 1, HD)

        def compute_mini_batch(carry, inp):
            W1c, b1c = carry
            XQ, XK, XV, eta = inp
            Z1 = XK @ W1c + b1c
            g = ln_fused_l2_bwd(Z1, XV - XK, gamma, beta)
            g = g * eta / m
            grad_W1 = jnp.einsum('bhmd,bhme->bhde', XK, g)
            grad_b1 = jnp.sum(g, axis=2, keepdims=True)
            W1n = W1c - grad_W1
            b1n = b1c - grad_b1
            Z1_bar = ln_fwd(XQ @ W1n + b1n, gamma, beta)
            return ((W1n, b1n), XQ + Z1_bar)

        def to_scan(t):
            return t.reshape(B, H, num_mini_batch, m, t.shape[-1]).transpose(2, 0, 1, 3, 4)
        xs = (to_scan(q), to_scan(k), to_scan(v), to_scan(ttt_lr_eta))
        init = (jnp.broadcast_to(W1, (B, H, HD, HD)), jnp.broadcast_to(b1, (B, H, 1, HD)))
        _, XQW = jax.lax.scan(compute_mini_batch, init, xs)
        out = XQW.transpose(1, 2, 0, 3, 4).reshape(B, H, N, HD)
        out = out.transpose(0, 2, 1, 3).reshape(B, N, C)
        out = out @ proj_weight.T + proj_bias
        return out

    def _L1_ffn_ref(x, scale, gate_w, gate_b, w1, b1, w2, b2):
        import jax, jax.numpy as jnp
        import numpy as np
        B, S, H = (2, 256, 192)
        E, K, I = (16, 4, 192)
        ALPHA, LIMIT, EPS = (1.702, 7.0, 1e-05)

        def _swiglu(h):
            x_glu, x_lin = jnp.split(h, 2, axis=-1)
            x_glu = jnp.minimum(x_glu, LIMIT)
            x_lin = jnp.clip(x_lin, -LIMIT, LIMIT)
            return x_glu * jax.nn.sigmoid(ALPHA * x_glu) * (x_lin + 1.0)
        Bx, Sx, Hx = x.shape
        xf = x.astype(jnp.float32)
        t = xf * jax.lax.rsqrt(jnp.mean(xf * xf, axis=-1, keepdims=True) + EPS) * scale
        t = t.reshape(-1, Hx)
        T = t.shape[0]
        g = t @ gate_w.T + gate_b
        vals, idx = jax.lax.top_k(g, K)
        w = jax.nn.softmax(vals, axis=-1) / K
        full_w = jnp.zeros((T, E), jnp.float32).at[jnp.arange(T)[:, None], idx].set(w)
        h = jnp.einsum('th,ehf->tef', t, w1) + b1
        h = _swiglu(h)
        y = jnp.einsum('tei,eih->teh', h, w2) + b2
        out = jnp.einsum('teh,te->th', y, full_w) * K
        return x + out.astype(x.dtype).reshape(Bx, Sx, Hx)
    h = _L0_tok_ref(x, L0_tok_ln_w, L0_tok_ln_b, L0_tok_conv_w, L0_tok_conv_b, L0_tok_proj_w, L0_tok_proj_b, L0_tok_pos_emb)
    h = jnp.concatenate([h, _L0_txt_ref(x_txt, L0_txt_weight)], axis=1)
    h = h + _L0_attn_ref(_layernorm(h, axis=-1), L0_attn_qkv_w, L0_attn_proj_w, L0_attn_proj_b)
    h = h + _L0_ffn_ref(_layernorm(h, axis=-1), L0_ffn_Wg, L0_ffn_W1, L0_ffn_b1, L0_ffn_W2, L0_ffn_b2)
    h = h + _L1_attn_ref(_layernorm(h, axis=-1), L1_attn_qkv_weight, L1_attn_q_bias, L1_attn_v_bias, L1_attn_proj_weight, L1_attn_proj_bias, L1_attn_ttt_lr_weight, L1_attn_ttt_lr_bias, L1_attn_ttt_norm_weight, L1_attn_ttt_norm_bias, L1_attn_W1, L1_attn_b1)
    h = h + _L1_ffn_ref(_layernorm(h, axis=-1), L1_ffn_scale, L1_ffn_gate_w, L1_ffn_gate_b, L1_ffn_w1, L1_ffn_b1, L1_ffn_w2, L1_ffn_b2)
    return h

_drawn_inputs = setup_inputs


def setup_inputs(seed=0):
    import zlib

    import numpy as np

    out = dict(_drawn_inputs(seed))
    spreads = {'L0_tok_ln_w': (1.0, 0.2),
     'L0_tok_ln_b': (0.0, 0.346),
     'L0_attn_proj_b': (0.0, 0.1),
     'L0_ffn_b1': (0.0, 0.273),
     'L0_ffn_b2': (0.0, 0.1),
     'L1_attn_q_bias': (0.0, 0.1),
     'L1_attn_v_bias': (0.0, 0.1),
     'L1_attn_proj_bias': (0.0, 0.1),
     'L1_attn_ttt_lr_bias': (0.0, 0.568),
     'L1_attn_ttt_norm_weight': (1.0, 0.2),
     'L1_attn_ttt_norm_bias': (0.0, 0.1),
     'L1_attn_b1': (0.0, 0.1),
     'L1_ffn_scale': (1.0, 0.6),
     'L1_ffn_gate_b': (0.0, 0.8)}
    factors = {'L1_ffn_gate_w': 3.665,
     'L1_ffn_w1': 3.43,
     'L1_ffn_b1': 8.0,
     'L1_ffn_w2': 3.703,
     'L1_ffn_b2': 8.0}
    for name, (base, spread) in spreads.items():
        noise = np.random.default_rng([zlib.crc32(name.encode()), seed]).standard_normal(out[name].shape)
        drawn = base * np.exp(spread * noise) if base else spread * noise
        out[name] = jnp.asarray(drawn.astype(out[name].dtype))
    for name, factor in factors.items():
        out[name] = (out[name] * factor).astype(out[name].dtype)
    return out
```

```python
from contextlib import ExitStack

import numpy as np

import concourse.bass as bass
from concourse import mybir

F32 = mybir.dt.float32
I32 = mybir.dt.int32
U32 = mybir.dt.uint32
ALU = mybir.AluOpType
ACT = mybir.ActivationFunctionType
AX_X = mybir.AxisListType.X

B = 32
NI, NW = 36, 77
N = NI + NW
C = 192
HC = C // 2
KA = HC + 1
PAIRS = B // 2
HEADS, HD = 12, 16
HH = HEADS // 2
F0 = 768
E0 = 3
FT = F0 // 128
E1, TOPK = 16, 4
I1 = 192
VOCAB = 8000
CHUNKS = 6
XW = CHUNKS * NI
GRP = 3
ROWS = GRP * NI
BLOCKS = (TOPK * N * B + E1 * 127) // 128
SLOTS = BLOCKS * 128
RW = C + 2
DUMP = TOPK * N * B
WTOK = 3 * C + HEADS
LN_EPS = 1e-5
TTT_EPS = 1e-6
RMS_EPS = 1e-5
ALPHA, LIMIT = 1.702, 7.0

SEMS = """load_x load_tok load_idx load_att load_ffn load_ttt load_moe const_ready dve_chain gathered tok_piece0 tok_piece1
tok_stat tok_dev tok_mean tok_devavg tok_varsum tok_eps tok_rstd tok_norm tok_xg tok_mm tok_sum tok_w tok_bias_mm
tok_bias0 tok_bias clipped mask_lo mask_hi masked ln0_stat ln_e ln_rstd att_xn att_xT att_xTs att_q att_kv att_qs
att_ks att_vs att_prod att_ksm att_frac att_rden att_on att_oTp att_oT att_out att_h att_stat gate0_xn gate0_mean
gate0_prod gate0_logit gate0_step gate0_exp gate0_ready ffn_xn ffn_xT ffn_xTs ffn_hid ffn_gelu ffn_hT ffn_hTv
ffn_hTa ffn_y ffn_h ffn_stat tw_cent tw_comp tw_done ttt_xn ttt_xT ttt_xTs ttt_q ttt_qs ttt_tok ttt_sq ttt_kA ttt_dl
ttt_sig ttt_v ttt_rstd ttt_xh ttt_t1 ttt_g ttt_p ttt_s ttt_r ttt_gr ttt_xs ttt_zz ttt_grad ttt_gm ttt_w ttt_zb
ttt_zm ttt_zc ttt_zsq ttt_zv ttt_zr ttt_zh ttt_zT ttt_oT ttt_out ttt_h ttt_stat pool_inner pool_outer rt_rms rt_xn
rt_t rt_tT rt_tTs rt_row rt_logit rt_gs rt_max rt_idx rt_top rt_mask rt_pre rt_exp rt_done filled row_t row_meta
dispatched0 dispatched1 going moe_x0 moe_x1 moe_meta moe_xT moe_xTs moe_h moe_al moe_sig moe_p moe_act moe_aT moe_aTs moe_y moe_ys
moe_out0 moe_out1 fin_y0 fin_y1 fin_a fin_b fin_c stored0 stored1""".split()


def when(eng, sem, n):
    if not isinstance(n, int) or n > 0:
        eng.wait_ge(sem, n)


def over_pairs(eng, step, unroll=2):
    step(0, 0)
    step(1, 1)
    with eng.Fori(0, (PAIRS - 4) // unroll) as turn:
        for j in range(unroll):
            step(turn * unroll + (2 + j), (2 + j) % unroll)
    step(PAIRS - 2, (PAIRS - 2) % unroll)
    step(PAIRS - 1, (PAIRS - 1) % unroll)


def over_some(eng, step, count):
    step(0, 0, 0)
    step(1, 1, 0)
    with eng.Fori(1, count // 2 - 1) as turn:
        step(turn * 2, 0, turn)
        step(turn * 2 + 1, 1, turn)
    step(count - 2, 0, count // 2 - 1)
    step(count - 1, 1, count // 2 - 1)


def over_blocks(eng, step):
    over_some(eng, step, BLOCKS)


def over_images(eng, step):
    over_some(eng, step, B)


def before(n, slot, half):
    return n - 1, 1 - slot, half - 1 if slot == 0 else half


def after(n, slot, half):
    return n + 1, 1 - slot, half if slot == 0 else half + 1


def first(n):
    return isinstance(n, int) and n == 0


def last(n, count):
    return isinstance(n, int) and n == count - 1


def build(nc, x_d, ids_d, idsm_d, lnwb_d, convb_d, projT_d, projb_d, pos_d, table_d, att_d, attp_d, gate0_d,
          f1_d, f2_d, fb2_d, tq_d, tk_d, tv_d, tkn_d, tg_d, tgc_d, tw_d, tp_d, scale_d, gate1_d, m1_d, m2_d,
          ident_d, mask_d, tri_d, iotae_d, iotab_d, target_d, dump_d, out_d):
    ctx = ExitStack()
    with ctx:
        def sb(name, shape, dt=F32):
            return ctx.enter_context(nc.sbuf_tensor(name, shape, dt))

        S = {n: ctx.enter_context(nc.semaphore(n)) for n in SEMS}
        bank = [ctx.enter_context(nc.psum_tensor(f"bank{i}", [128, 512], F32)) for i in range(4)]
        wide = [ctx.enter_context(nc.psum_tensor(f"wide{i}", [128, 2, 512], F32)) for i in range(2)]

        slots_d = nc.dram_tensor("slots", [SLOTS, RW], F32, kind="Internal").ap()
        ycomb_d = nc.dram_tensor("ycomb", [DUMP + 256, C], F32, kind="Internal").ap()

        h = sb("h", [N, B, C])
        stats = sb("stats", [N, B, 6])
        mean = sb("mean", [N, B])
        rstd = sb("rstd", [N, B])
        lns = sb("lns", [N, 4, B])
        ident = sb("ident", [128, 128])
        mask = sb("mask", [KA, HC])
        ones = sb("ones", [128, 128])
        avg128 = sb("avg128", [128, 128])
        avgN = sb("avgN", [128, 1])
        mhalf = sb("mhalf", [128, 32])
        xn = sb("xn", [N, 2, 2, C])
        xT = sb("xT", [KA, 2, 2, 2, N])

        def carver(name, size):
            place, taken = sb(name, [128, size]), [0]

            def carve(shape, again=False):
                if again:
                    taken[0] = 0
                n = int(np.prod(shape[1:]))
                at = taken[0]
                taken[0] += n
                assert taken[0] <= size, (name, taken[0])
                v = place[0:shape[0], at:at + n]
                names = " ".join(f"d{i}" for i in range(1, len(shape)))
                sizes = {f"d{i}": shape[i] for i in range(2, len(shape))}
                return v.rearrange(f"p ({names}) -> p {names}", **sizes) if len(shape) > 2 else v

            return carve

        rows = carver("rows", E0 * 2 * F0 + E0 * FT * C)
        X = rows([128, B, XW])
        w1 = rows([KA, E0, 2, F0], again=True)
        w2 = rows([128, E0, FT, C])
        t_all = rows([N, B, C], again=True)
        early = carver("early", E1 * 2 * (2 * I1 + C))
        inner = carver("inner", 12320)

        idx = sb("idx", [NW, B], I32)
        idxc = sb("idxc", [NW, B], I32)
        idxm = sb("idxm", [N, B], I32)
        dump = sb("dump", [128, 2])
        keep = sb("keep", [N, 2, B])
        lnwb = early([128, 2, XW])
        convb = sb("convb", [128, 12])
        projT = early([128, 3, 2, C])
        convT = early([128, 3, 2, C])
        projb = early([ROWS, C])
        pos = early([ROWS, C])
        tokb = early([ROWS, C])
        tstat = early([128, B, 6])
        tsmall = early([128, 6, B])
        xg = early([128, 2, CHUNKS, ROWS])
        tok = early([ROWS, 2, C])

        watt = early([KA, 2, 3 * C])
        wattp = early([KA, 2, C])
        qT = sb("qT", [KA, 4, 2, 2 * N])
        kS = early([N, 2, 2, 2, KA])
        vS = early([N, 2, 2, 2, KA])
        kvm = early([HC, 2, 2, 2, HC])
        ksm = early([KA, 2, 2, 2, HH])
        rden = early([N, 2 * HEADS])
        on = early([N, 2, 2, 2, HC])
        oT = sb("oT", [KA, 2, 2, 2, N])

        wg0 = early([HC, 2, E0])
        wb2 = sb("wb2", [1, E0, C])
        gm = early([HC, 2, B])
        gprod = early([HC, 2, B, E0])
        gsm = early([128, 2, B, E0])
        gone = sb("gone", [128, 5, B])
        sel = sb("sel", [1, B], I32)
        hid = early([N, 2, F0])
        hT = early([128, 2, FT, N])

        wq = inner([KA, 2, C])
        wtok = inner([KA, 2, WTOK])
        wv = inner([KA, 2, C])
        wkn = inner([HC, 2, C])
        gam = inner([N, C])
        gam2 = inner([N, 2, C])
        gcol = inner([HC, 4])
        w1b = inner([KA, 2, HC])
        w1c = inner([KA, 2, HC])
        w1m = inner([KA, HEADS])
        wp = inner([KA, 2, C])
        kA = inner([N, 2, 2, 4, KA])
        dl = inner([N, 2, 2, C + HEADS])
        sig = inner([N, 2, 2 * HEADS])
        sm = inner([N, 2, 8, 2 * HEADS])
        tc = inner([N, 3, 2 * HEADS])
        sq = inner([N, 2 * C])
        xh = inner([N, 2 * C])
        t1 = inner([N, 2 * C])
        gg = inner([N, 2 * C])
        pp = inner([N, 2 * C])
        xs = inner([N, 2 * C])
        zz = inner([N, 2, 2 * C])
        gmk = inner([KA, 4 * HC])
        wn = inner([KA, 2, 2, 2, HC])
        zc = inner([N, 2 * C])
        zsq = inner([N, 2 * C])
        zh = inner([N, 2, 2 * C])

        m1 = early([KA, E1, 2, 2 * I1], again=True)
        m2 = early([KA, E1, 2, C])
        chosen = inner([N, TOPK, B, E1], again=True)
        work = inner([N, 4, B * E1])
        scale = sb("scale", [N, C])
        gate1 = sb("gate1", [KA, 2, E1])
        tri = sb("tri", [N, N])
        rr = inner([N, B])
        ts = inner([N, 2, 2, C])
        gs = inner([N, 2, 2, E1])
        m8 = inner([N, 2, 2, 8])
        i8 = sb("i8", [N, 2, 2, 8], U32)
        topv = inner([N, B, TOPK])
        topi = inner([N, B, TOPK])
        wtop = inner([N, B, TOPK])
        wsum = inner([N, B])
        iota_e = sb("iota_e", [N, E1])
        iota_b = sb("iota_b", [1, BLOCKS])
        per_e = inner([N, 6, E1])
        per_ei = sb("per_ei", [N, 2, E1], I32)
        slot_of = inner([N, B, TOPK])
        slot_i = sb("slot_i", [N, B, TOPK], I32)
        slot_s = sb("slot_s", [N, 2, TOPK], I32)
        target = sb("target", [N, B, TOPK])
        etab = sb("etab", [1, BLOCKS], I32)
        rowbuf = inner([N, 2, TOPK, RW])
        fill = sb("fill", [128, 2, RW])
        xb = inner([128, 2, RW])
        weight = inner([128, 2, 1])
        al = inner([128, 2, 2 * I1])
        sg = inner([128, 2, I1])
        pr = inner([128, 2, I1])
        ac = inner([128, 2, I1])
        aT = inner([KA, 2, 2, 128])
        xTm = inner([KA, 2, 2, 128])
        ys = inner([128, 2, C])
        yc = inner([N, 2, TOPK * C], again=True)
        ya = inner([N, 2 * C])
        yb = inner([N, C])
        yo = inner([N, 2, C])
        dest = sb("dest", [128, 2, 1], I32)

        block = ctx.enter_context(nc.Block())

        @block.sync
        def _(sp):
            sp.dma_start(idx[:, :], ids_d).then_inc(S["load_idx"], 16)
            sp.dma_start(idxm[:, :], idsm_d).then_inc(S["load_idx"], 16)
            sp.dma_start(dump[:, :], dump_d).then_inc(S["load_idx"], 16)
            for q in range(4):
                sp.dma_start(X[:, 8 * q:8 * q + 8, :], x_d[:, 8 * q:8 * q + 8, :]).then_inc(S["load_x"], 16)
            for dst, src in ((convb[:], convb_d), (projT, projT_d), (lnwb, lnwb_d), (projb, projb_d), (pos, pos_d)):
                sp.dma_start(dst, src).then_inc(S["load_tok"], 16)
            for dst, src in ((ident[:], ident_d), (mask[:], mask_d), (watt, att_d), (wattp, attp_d)):
                sp.dma_start(dst, src).then_inc(S["load_att"], 16)

            for dst, src in ((wq, tq_d), (wtok, tk_d), (wv, tv_d), (wkn, tkn_d), (gam, tg_d), (gcol, tgc_d), (w1b, tw_d),
                             (wp, tp_d)):
                sp.dma_start(dst, src).then_inc(S["load_ttt"], 16)

            def put(g, slot, count):
                sp.wait_ge(S["tok_sum"], g + 1)
                for j in range(count):
                    sp.dma_start(h[0:NI, bass.ds(g * GRP + j, 1), :], tok[NI * j:NI * j + NI, slot, :])\
                      .then_inc(S[f"tok_piece{slot}"], 16)

            with sp.Fori(0, 5) as turn:
                put(turn * 2, 0, GRP)
                put(turn * 2 + 1, 1, GRP)
            put(10, 0, 2)
            sp.wait_ge(S["tok_xg"], 11)
            for dst, src in ((wg0, gate0_d), (w1, f1_d), (w2, f2_d), (wb2[:], fb2_d)):
                sp.dma_start(dst, src).then_inc(S["load_ffn"], 16)
            sp.wait_ge(S["filled"], 1)
            with sp.Fori(0, BLOCKS // 2) as turn:
                sp.dma_start(slots_d[bass.ds(turn * 256, 256), :].rearrange("(j p) w -> p j w", p=128), fill[:, :, :])\
                  .then_inc(S["filled"], 16)
            sp.wait_ge(S["ffn_stat"], B)
            for dst, src in ((m1, m1_d), (m2, m2_d), (scale[:], scale_d), (gate1[:], gate1_d), (tri[:], tri_d),
                             (iota_e[:], iotae_d), (iota_b[:], iotab_d), (target[:], target_d)):
                sp.dma_start(dst, src).then_inc(S["load_moe"], 16)

            sp.wait_ge(S["dispatched0"], 16 * TOPK * B // 2)
            sp.wait_ge(S["dispatched1"], 16 * TOPK * B // 2)

            def load_block(j, slot, half):
                when(sp, S["moe_xT"], j - 1)
                when(sp, S["moe_meta"], j - 1)
                sp.dma_start(xb[:, slot, :], slots_d[bass.ds(j * 128, 128), :]).then_inc(S[f"moe_x{slot}"], 16)

            over_blocks(sp, load_block)

            sp.wait_ge(S["moe_out0"], 16 * BLOCKS // 2)
            sp.wait_ge(S["moe_out1"], 16 * BLOCKS // 2)

            def load_choices(b, slot, half):
                when(sp, S["fin_a"], b - 1)
                sp.dma_start(yc[:, slot, :], ycomb_d[bass.ds(b * (N * TOPK), N * TOPK), :].rearrange("(p k) c -> p (k c)", k=TOPK))\
                  .then_inc(S[f"fin_y{slot}"], 16)

            def store(b, slot, half):
                sp.wait_ge(S["fin_c"], b + 1)
                sp.dma_start(out_d[bass.ds(b, 1), :, :].rearrange("a n c -> n (a c)"), yo[:, slot, :])\
                  .then_inc(S[f"stored{slot}"], 16)

            def final(b, slot, half):
                if not last(b, B):
                    load_choices(*after(b, slot, half))
                store(b, slot, half)

            load_choices(0, 0, 0)
            over_images(sp, final)
            sp.wait_ge(S["stored0"], 16 * B // 2)
            sp.wait_ge(S["stored1"], 16 * B // 2)

        @block.gpsimd
        def _(pool):
            pool.wait_ge(S["clipped"], 1)
            for b in range(B):
                nc.gpsimd.indirect_dma_start(
                    out=h[NI:N, b, :], out_offset=None, in_=table_d,
                    in_offset=bass.IndirectOffsetOnAxis(ap=idxc[:, b:b + 1], axis=0)).then_inc(S["gathered"], 16)
            pool.wait_ge(S["tok_eps"], 1)
            nc.gpsimd.tensor_tensor(tsmall[:, 5, :], tsmall[:, 4, :], mhalf[:, :], ALU.pow).then_inc(S["tok_rstd"], 1)
            def layer_rstd(k):
                pool.wait_ge(S["ln_e"], k + 1)
                nc.gpsimd.tensor_tensor(rstd[:, :], lns[:, 3, :], mhalf[0:N, :], ALU.pow).then_inc(S["ln_rstd"], 1)

            for k in range(3):
                layer_rstd(k)

            G = nc.gpsimd

            def rsqrt(dst, src, step, count):
                G.tensor_tensor(src, src, tc[:, 0, :], ALU.add).then_inc(step, 1)
                pool.wait_ge(step, count)
                return G.tensor_tensor(dst, src, mhalf[0:N, 0:2 * HEADS], ALU.pow)

            def heads(v):
                return v.rearrange("p (a d) -> p a d", d=HD)

            def per_head(v):
                return v.rearrange("p (a d) -> p a d", d=1).broadcast_to([N, 2 * HEADS, HD])

            def ttt(t, slot):
                s_ = sm[:, slot % 2]
                step = S["pool_inner"]
                pool.wait_ge(S["ttt_v"], t + 1)
                rsqrt(s_[:, 1, :], s_[:, 0, :], step, 4 * t + 1).then_inc(S["ttt_rstd"], 1)
                pool.wait_ge(S["ttt_sig"], t + 1)
                pool.wait_ge(S["ttt_rstd"], t + 1)
                G.tensor_tensor(s_[:, 2, :], s_[:, 1, :], tc[:, 1, :], ALU.mult).then_inc(step, 1)
                pool.wait_ge(step, 4 * t + 2)
                G.tensor_tensor(s_[:, 2, :], s_[:, 2, :], sig[:, slot % 2, :], ALU.mult).then_inc(S["ttt_r"], 1)
                pool.wait_ge(S["ttt_xh"], t + 1)
                G.tensor_tensor(t1[:, :], xh[:, :], gam2[:, :, :].rearrange("p i c -> p (i c)"), ALU.mult)\
                 .then_inc(S["ttt_t1"], 1)
                if not first(t):
                    ttt_outer(t - 1, slot - 1)
                pool.wait_ge(S["ttt_s"], t + 1)
                pool.wait_ge(S["ttt_r"], t + 1)
                G.tensor_tensor(s_[:, 3, :], s_[:, 3, :], tc[:, 2, :], ALU.mult).then_inc(step, 1)
                pool.wait_ge(step, 4 * t + 3)
                G.tensor_tensor(s_[:, 3, :], s_[:, 3, :], s_[:, 2, :], ALU.mult).then_inc(step, 1)
                pool.wait_ge(step, 4 * t + 4)
                when(pool, S["ttt_zz"], t)
                G.tensor_tensor(heads(xs[:, :]), heads(xh[:, :]), per_head(s_[:, 3, :]), ALU.mult)\
                 .then_inc(S["ttt_xs"], 1)

            def ttt_outer(t, slot):
                s_ = sm[:, slot % 2]
                pool.wait_ge(S["ttt_zv"], t + 1)
                rsqrt(s_[:, 6, :], s_[:, 5, :], S["pool_outer"], t + 1).then_inc(S["ttt_zr"], 1)

            over_pairs(pool, ttt, 4)
            ttt_outer(PAIRS - 1, 3)
            layer_rstd(3)
            pool.wait_ge(S["rt_rms"], 1)
            G.tensor_tensor(rr, lns[:, 1, :], mhalf[0:N, :], ALU.pow).then_inc(S["rt_rms"], 1)

            def dispatch(b, slot, half):
                pool.wait_ge(S["row_t"], b + 1)
                pool.wait_ge(S["row_meta"], b + 1)
                pool.sem_inc(S["going"], 1)
                for k in range(TOPK):
                    G.indirect_dma_start(
                        out=slots_d, out_offset=bass.IndirectOffsetOnAxis(ap=slot_s[:, slot, k:k + 1], axis=0),
                        in_=rowbuf[:, slot, k, :], in_offset=None).then_inc(S[f"dispatched{slot}"], 16)

            pool.wait_ge(S["filled"], 1 + 16 * (BLOCKS // 2))
            over_images(pool, dispatch)

            def send_back(j, slot, half):
                pool.wait_ge(S["moe_ys"], j + 1)
                pool.sem_inc(S["going"], 1)
                G.indirect_dma_start(
                    out=ycomb_d, out_offset=bass.IndirectOffsetOnAxis(ap=dest[:, slot, :], axis=0),
                    in_=ys[:, slot, :], in_offset=None).then_inc(S[f"moe_out{slot}"], 16)

            def moe(j, slot, half):
                pool.wait_ge(S["moe_p"], j + 1)
                pool.wait_ge(S["moe_sig"], j + 1)
                when(pool, S["moe_aT"], j - 1)
                G.tensor_tensor(ac[:, slot, :], pr[:, slot, :], sg[:, slot, :], ALU.mult).then_inc(S["moe_act"], 1)
                if not first(j):
                    send_back(*before(j, slot, half))

            over_blocks(pool, moe)
            send_back(BLOCKS - 1, 1, BLOCKS // 2 - 1)


        @block.scalar
        def _(act):
            act.wait_ge(S["const_ready"], 1)
            act.wait_ge(S["load_att"], 64)

            def attention(t, slot):
                act.wait_ge(S["att_xT"], t + 1)
                when(act, S["att_q"], t - 1)
                nc.scalar.copy(xT[0:HC, slot].rearrange("p h i n -> p (h i n)"), bank[0][0:HC, 0:4 * N])\
                    .then_inc(S["att_xTs"], 1)
                act.wait_ge(S["att_ks"], t + 1)
                when(act, S["att_prod"], t - 1)
                nc.scalar.copy(vS[:, slot, :, :, 0:HC].rearrange("p i h c -> p i h c"),
                               wide[0][0:N, :, C:2 * C].rearrange("p i (h c) -> p i h c", h=2))\
                    .then_inc(S["att_vs"], 1)

                if not first(t):
                    att_oT(t - 1, 1 - slot)

            def att_oT(t, slot):
                act.wait_ge(S["att_oTp"], t + 1)
                when(act, S["att_out"], t - 1)
                nc.scalar.copy(oT[0:HC, slot].rearrange("p h i n -> p (h i n)"), wide[1][0:HC, 1, 0:4 * N])\
                    .then_inc(S["att_oT"], 1)

            over_pairs(act, attention)
            att_oT(PAIRS - 1, 1)

            act.wait_ge(S["gate0_step"], 1)
            nc.scalar.activation(gsm[:, 1].rearrange("p b e -> p (b e)"), gsm[:, 0].rearrange("p b e -> p (b e)"),
                                 ACT.Exp).then_inc(S["gate0_exp"], 1)

            def ffn_xT(t, slot):
                act.wait_ge(S["ffn_xT"], t + 1)
                when(act, S["ffn_hid"], 2 * t - 2)
                nc.scalar.copy(xT[0:HC, slot].rearrange("p h i n -> p (h i n)"), bank[0][0:HC, 0:4 * N])\
                    .then_inc(S["ffn_xTs"], 1)

            def ffn_hT(u, i):
                act.wait_ge(S["ffn_hT"], u + 1)
                when(act, S["ffn_y"], u - 1)
                nc.scalar.copy(hT[:, i, 3:6, :], bank[2][:, 0:3 * N].rearrange("p (k n) -> p k n", k=3))\
                    .then_inc(S["ffn_hTa"], 1)

            def ffn(t, slot):
                for i in range(2):
                    u = t * 2 + i
                    if not first(u):
                        ffn_hT(u - 1, 1 - i)
                    act.wait_ge(S["ffn_hid"], u + 1)
                    when(act, S["ffn_hT"], u - 1)
                    for n in range(2):
                        ins = nc.scalar.activation(hid[:, i, 384 * n:384 * n + 384], wide[i][0:N, n, 0:384], ACT.Gelu)
                    ins.then_inc(S["ffn_gelu"], 1)
                    if i == 0 and not (isinstance(t, int) and t == PAIRS - 1):
                        ffn_xT(t + 1, 1 - slot)

            ffn_xT(0, 0)
            over_pairs(act, ffn)
            ffn_hT(B - 1, 1)

            def ttt_xT(t, slot):
                act.wait_ge(S["ttt_xT"], t + 1)
                when(act, S["ttt_tok"], t - 1)
                nc.scalar.copy(xT[0:HC, slot % 2].rearrange("p h i n -> p (h i n)"), bank[0][0:HC, 0:4 * N])\
                    .then_inc(S["ttt_xTs"], 1)

            def ttt_q(t, slot):
                act.wait_ge(S["ttt_q"], t + 1)
                when(act, S["ttt_oT"], t - 3)
                nc.scalar.copy(qT[0:HC, slot % 4].rearrange("p h n -> p (h n)"), bank[1][0:HC, 0:4 * N])\
                    .then_inc(S["ttt_qs"], 1)

            def ttt_tok(t, slot):
                act.wait_ge(S["ttt_tok"], t + 1)
                when(act, S["ttt_grad"], t - 1)
                when(act, S["ttt_xh"], t - 1)
                when(act, S["ttt_sq"], t - 1)
                nc.scalar.copy(kA[:, slot % 2, :, :, 0:HC], wide[0][0:N, :, 0:2 * C].rearrange("p i (a c) -> p i a c", a=4))\
                    .then_inc(S["ttt_kA"], 1)
                when(act, S["ttt_g"], t - 1)
                when(act, S["ttt_sig"], t - 1)
                nc.scalar.copy(dl[:, slot % 2], bank[3][0:N, 0:2 * (C + HEADS)].rearrange("p (i c) -> p i c", i=2))\
                    .then_inc(S["ttt_dl"], 1)
                act.wait_ge(S["ttt_kA"], t + 1)
                when(act, S["ttt_v"], t)
                nc.scalar.activation(sq[:, :].rearrange("p (i a c) -> p i a c", i=2, a=2), kA[:, slot % 2, :, 2:4, 0:HC],
                                     ACT.Square, scale=HD ** -0.5)\
                    .then_inc(S["ttt_sq"], 1)
                act.wait_ge(S["ttt_dl"], t + 1)
                when(act, S["ttt_r"], t - 1)
                nc.scalar.activation(sig[:, slot % 2, :].rearrange("p (i a) -> p i a", i=2),
                                     dl[:, slot % 2, :, C:C + HEADS], ACT.Sigmoid).then_inc(S["ttt_sig"], 1)

            def ttt_zsq(t):
                act.wait_ge(S["ttt_zc"], t + 1)
                when(act, S["ttt_zv"], t)
                nc.scalar.activation(zsq[:, :], zc[:, :], ACT.Square, scale=HD ** -0.5).then_inc(S["ttt_zsq"], 1)

            def ttt(t, slot):
                fixed = isinstance(t, int)
                if not (fixed and t == PAIRS - 1):
                    ttt_q(t + 1, slot + 1)
                if not (fixed and t == 0):
                    ttt_zsq(t - 1)
                if not (fixed and t == PAIRS - 1):
                    ttt_tok(t + 1, slot + 1)
                if not (fixed and t >= PAIRS - 2):
                    ttt_xT(t + 2, slot + 2)

            ttt_xT(0, 0)
            ttt_q(0, 0)
            ttt_tok(0, 0)
            ttt_xT(1, 1)
            over_pairs(act, ttt, 4)
            ttt_zsq(PAIRS - 1)

            def rt_copy(t, slot):
                act.wait_ge(S["rt_tT"], t + 1)
                when(act, S["rt_logit"], t - 1)
                nc.scalar.copy(xT[0:HC, slot].rearrange("p h i n -> p (h i n)"), bank[0][0:HC, 0:4 * N])\
                    .then_inc(S["rt_tTs"], 1)
                nc.scalar.copy(t_all[:, bass.ds(t * 2, 2), :], ts[:, slot]).then_inc(S["rt_row"], 1)

            over_pairs(act, rt_copy)
            act.wait_ge(S["rt_pre"], 1)
            nc.scalar.activation(wtop, topv, ACT.Exp).then_inc(S["rt_exp"], 1)
            act.wait_ge(S["rt_row"], PAIRS)

            def send(b, slot, half):
                when(act, S[f"dispatched{slot}"], 16 * TOPK * half)
                nc.scalar.copy(rowbuf[:, slot, :, 0:C], t_all[:, bass.ds(b, 1), :].broadcast_to([N, TOPK, C]))\
                    .then_inc(S["row_t"], 1)

            over_images(act, send)

            def moe_xTs(j, slot, half):
                act.wait_ge(S["moe_xT"], j + 1)
                when(act, S["moe_h"], j - 1)
                nc.scalar.copy(xTm[0:HC, slot].rearrange("p h n -> p (h n)"), bank[0][0:HC, 0:256])\
                    .then_inc(S["moe_xTs"], 1)

            def moe_sigmoid(j, slot, half):
                act.wait_ge(S["moe_al"], j + 1)
                when(act, S["moe_act"], j - 1)
                nc.scalar.activation(sg[:, slot, :], al[:, slot, 0:I1], ACT.Sigmoid, scale=ALPHA).then_inc(S["moe_sig"], 1)

            def moe_aTs(j, slot, half):
                act.wait_ge(S["moe_aT"], j + 1)
                when(act, S["moe_y"], j - 1)
                nc.scalar.copy(aT[0:HC, slot].rearrange("p h n -> p (h n)"), bank[2][0:HC, 0:256])\
                    .then_inc(S["moe_aTs"], 1)

            def moe(j, slot, half):
                moe_sigmoid(j, slot, half)
                if not first(j):
                    moe_aTs(*before(j, slot, half))
                if not last(j, BLOCKS):
                    moe_xTs(*after(j, slot, half))

            moe_xTs(0, 0, 0)
            over_blocks(act, moe)
            moe_aTs(BLOCKS - 1, 1, BLOCKS // 2 - 1)

        @block.tensor
        def _(pe):
            pe.wait_ge(S["const_ready"], 1)
            pe.wait_ge(S["tok_stat"], 1)
            pe.matmul(bank[0][:, 0:B], avg128[:, :], tsmall[:, 0, :], start=True, stop=True).then_inc(S["tok_mean"], 1)
            pe.wait_ge(S["tok_varsum"], 1)
            pe.matmul(bank[1][:, 0:B], avg128[:, :], tsmall[:, 3, :], start=True, stop=True).then_inc(S["tok_devavg"], 1)
            pe.wait_ge(S["tok_w"], 1)
            for k in range(CHUNKS):
                pe.matmul(bank[2][0:ROWS, 0:C], xg[:, 1, k, :], convT[:, k // 2, k % 2, :],
                          start=(k == 0), stop=False)
            for k in range(CHUNKS):
                ins = pe.matmul(bank[2][0:ROWS, 0:C], xg[:, 0, k, :], projT[:, k // 2, k % 2, :],
                                start=False, stop=(k == CHUNKS - 1))
            ins.then_inc(S["tok_bias_mm"], 1)

            def patches(g, slot, count):
                pe.wait_ge(S["tok_xg"], g + 1)
                when(pe, S["tok_sum"], g - 1)
                for k in range(CHUNKS):
                    ins = pe.matmul(bank[slot][0:NI * count, 0:C], xg[:, slot, k, 0:NI * count],
                                    convT[:, k // 2, k % 2, :], start=(k == 0), stop=(k == CHUNKS - 1))
                ins.then_inc(S["tok_mm"], 1)

            patches(0, 0, GRP)
            patches(1, 1, GRP)
            with pe.Fori(1, 5) as turn:
                patches(turn * 2, 0, GRP)
                patches(turn * 2 + 1, 1, GRP)
            patches(10, 0, 2)

            def turn_rows(slot, xn_ready, count, psum_free, n_free, done):
                pe.wait_ge(xn_ready, count)
                when(pe, psum_free, n_free)
                for i in range(2):
                    for k in range(2):
                        ins = pe.transpose(bank[0][0:HC, (2 * k + i) * N:(2 * k + i + 1) * N],
                                           xn[:, slot, i, k * HC:k * HC + HC], ident[0:N, 0:N])
                ins.then_inc(done, 1)

            pe.wait_ge(S["load_att"], 64)
            pe.wait_ge(S["tok_sum"], 11)

            def att_turn(t, slot):
                turn_rows(slot, S["att_xn"], t + 1, S["att_xTs"], t, S["att_xT"])

            def att_weights(t, slot):
                pe.wait_ge(S["att_xTs"], t + 1)
                when(pe, S["att_ks"], t)
                when(pe, S["att_vs"], t)
                for i in range(2):
                    for k in range(2):
                        ins = pe.matmul(wide[0][0:N, i, 0:2 * C], xT[0:HC, slot, k, i, :], watt[0:HC, k, C:3 * C],
                                        start=(k == 0), stop=(k == 1))
                ins.then_inc(S["att_kv"], 1)
                when(pe, S["att_qs"], t)
                for m in range(2):
                    for k in range(2):
                        ins = pe.matmul(bank[1][0:HC, m * 2 * N:(m + 1) * 2 * N], watt[0:HC, k, m * HC:m * HC + HC],
                                        xT[0:HC, slot, k].rearrange("p i n -> p (i n)"), start=(k == 0), stop=(k == 1))
                ins.then_inc(S["att_q"], 1)

            def att_product(t, slot):
                pe.wait_ge(S["att_ks"], t + 1)
                pe.wait_ge(S["att_vs"], t + 1)
                when(pe, S["att_ksm"], t)
                for i in range(2):
                    for k in range(2):
                        ins = pe.matmul(bank[2][0:HC, (2 * i + k) * KA:(2 * i + k + 1) * KA], kS[:, slot, i, k, 0:HC],
                                        vS[:, slot, i, k, :], start=True, stop=True)
                ins.then_inc(S["att_prod"], 1)

            def att_fraction(t, slot):
                pe.wait_ge(S["att_qs"], t + 1)
                pe.wait_ge(S["att_ksm"], t + 1)
                when(pe, S["att_on"], t)
                for i in range(2):
                    for k in range(2):
                        q = qT[:, slot, k, i * N:i * N + N]
                        a = 2 * i + k
                        pe.matmul(wide[1][0:N, 0, a * HC:a * HC + HC], q[0:HC], kvm[:, slot, i, k, :],
                                  start=True, stop=True)
                        ins = pe.matmul(wide[1][0:N, 0, 2 * C + a * HH:2 * C + a * HH + HH], q, ksm[:, slot, i, k, :],
                                        start=True, stop=True)
                ins.then_inc(S["att_frac"], 1)

            def att_turn_back(t, slot):
                pe.wait_ge(S["att_on"], t + 1)
                when(pe, S["att_oT"], t)
                for k in range(2):
                    for i in range(2):
                        ins = pe.transpose(wide[1][0:HC, 1, (2 * k + i) * N:(2 * k + i + 1) * N], on[:, slot, i, k, :],
                                           ident[0:N, 0:N])
                ins.then_inc(S["att_oTp"], 1)

            def att_project(t, slot):
                pe.wait_ge(S["att_oT"], t + 1)
                when(pe, S["att_h"], t)
                for i in range(2):
                    for k in range(2):
                        rows = KA if k == 0 else HC
                        ins = pe.matmul(bank[3][0:N, i * C:i * C + C], oT[0:rows, slot, k, i, :], wattp[0:rows, k, :],
                                        start=(k == 0), stop=(k == 1))
                ins.then_inc(S["att_out"], 1)

            def attention(t, slot):
                att_weights(t, slot)
                first = isinstance(t, int) and t == 0
                if not first:
                    att_fraction(t - 1, 1 - slot)
                if not last(t, PAIRS):
                    att_turn(t + 1, 1 - slot)
                att_product(t, slot)
                if not first:
                    att_turn_back(t - 1, 1 - slot)
                    att_project(t - 1, 1 - slot)

            att_turn(0, 0)
            over_pairs(pe, attention)
            att_fraction(PAIRS - 1, 1)
            att_turn_back(PAIRS - 1, 1)
            att_project(PAIRS - 1, 1)

            pe.wait_ge(S["att_h"], PAIRS)
            pe.wait_ge(S["att_qs"], PAIRS)

            def gate0(t, slot):
                pe.wait_ge(S["gate0_xn"], t + 1)
                for i in range(2):
                    for k in range(2):
                        ins = pe.matmul(bank[1][0:HC, bass.ds(t * 2 + (i + B * k), 1)],
                                        xn[:, slot, i, k * HC:k * HC + HC], avgN[0:N, :], start=True, stop=True)
                ins.then_inc(S["gate0_mean"], 1)

            over_pairs(pe, gate0)
            pe.wait_ge(S["gate0_prod"], 1)
            for k in range(2):
                ins = pe.matmul(bank[2][:, 0:B * E0], ones[0:HC, :], gprod[:, k].rearrange("p b e -> p (b e)"),
                                start=(k == 0), stop=(k == 1))
            ins.then_inc(S["gate0_logit"], 1)

            pe.wait_ge(S["load_ffn"], 64)
            pe.wait_ge(S["gate0_ready"], 1)

            def ffn_turn(t, slot):
                turn_rows(slot, S["ffn_xn"], t + 1, S["ffn_xTs"], t, S["ffn_xT"])

            def ffn_up(slot, i, n, e):
                for k in range(2):
                    rows = KA if k == 0 else HC
                    ins = pe.matmul(wide[i][0:N, n, 0:384], xT[0:rows, slot, k, i, :],
                                    w1[0:rows, bass.ds(e, 1), k, 384 * n:384 * n + 384], start=(k == 0), stop=(k == 1))
                return ins

            def ffn_transpose(u, i):
                pe.wait_ge(S["ffn_gelu"], u + 1)
                when(pe, S["ffn_hTv"], u)
                when(pe, S["ffn_hTa"], u)
                for k in range(FT):
                    ins = pe.transpose(bank[1 + k // 3][:, (k % 3) * N:(k % 3 + 1) * N], hid[:, i, 128 * k:128 * k + 128],
                                       ident[0:N, 0:N])
                ins.then_inc(S["ffn_hT"], 1)

            def ffn_down(u, i, e):
                pe.wait_ge(S["ffn_hTv"], u + 1)
                pe.wait_ge(S["ffn_hTa"], u + 1)
                when(pe, S["ffn_h"], u)
                for k in range(FT):
                    pe.matmul(bank[3][0:N, i * 256:i * 256 + C], hT[:, i, k, :], w2[:, bass.ds(e, 1), k, :],
                              start=(k == 0), stop=False)
                pe.matmul(bank[3][0:N, i * 256:i * 256 + C], ones[0:1, 0:N], wb2[0:1, bass.ds(e, 1), :],
                          start=False, stop=True).then_inc(S["ffn_y"], 1)

            def ffn(t, slot):
                pe.wait_ge(S["ffn_xTs"], t + 1)
                for i in range(2):
                    u = t * 2 + i
                    lag = not (isinstance(u, int) and u == 0)
                    e = pe.value_load(sel[0:1, bass.ds(u, 1)])
                    when(pe, S["ffn_gelu"], u - 1)
                    ffn_up(slot, i, 0, e)
                    if lag:
                        ffn_transpose(u - 1, 1 - i)
                    ffn_up(slot, i, 1, e).then_inc(S["ffn_hid"], 1)
                    if lag:
                        ffn_down(u - 1, 1 - i, pe.value_load(sel[0:1, bass.ds(u - 1, 1)]))
                    if i == 0 and not (isinstance(t, int) and t == PAIRS - 1):
                        ffn_turn(t + 1, 1 - slot)

            ffn_turn(0, 0)
            over_pairs(pe, ffn)
            ffn_transpose(B - 1, 1)
            ffn_down(B - 1, 1, pe.value_load(sel[0:1, B - 1:B]))

            pe.wait_ge(S["load_ttt"], 128)
            pe.wait_ge(S["tw_cent"], 1)
            for k in range(2):
                for m in range(2):
                    pe.matmul(bank[1][0:HC, (2 * k + m) * HC:(2 * k + m + 1) * HC], wkn[:, m, k * HC:k * HC + HC],
                              w1c[0:HC, m, :], start=True, stop=True)
            for k in range(2):
                ins = pe.matmul(bank[2][HC:KA, 0:C], gcol[:, 2 + k:3 + k], wp[0:HC, k, :], start=(k == 0), stop=(k == 1))
            ins.then_inc(S["tw_comp"], 1)
            pe.wait_ge(S["tw_done"], 1)

            def ttt_turn(t, slot):
                pe.wait_ge(S["ttt_xn"], t + 1)
                when(pe, S["ttt_oT"], t - 2)
                if isinstance(t, int) and t == 1:
                    pe.wait_ge(S["ttt_xTs"], 1)
                for i in range(2):
                    for k in range(2):
                        ins = pe.transpose(bank[0][0:HC, (2 * k + i) * N:(2 * k + i + 1) * N],
                                           xn[:, slot % 2, i, k * HC:k * HC + HC], ident[0:N, 0:N])
                ins.then_inc(S["ttt_xT"], 1)

            def ttt_query(t, slot):
                pe.wait_ge(S["ttt_xTs"], t + 1)
                when(pe, S["ttt_qs"], t)
                for m in range(2):
                    for k in range(2):
                        rows = KA if k == 0 else HC
                        ins = pe.matmul(bank[1][0:HC, m * 2 * N:(m + 1) * 2 * N], wq[0:rows, k, m * HC:m * HC + HC],
                                        xT[0:rows, slot % 2, k].rearrange("p i n -> p (i n)"),
                                        start=(k == 0), stop=(k == 1))
                ins.then_inc(S["ttt_q"], 1)

            def ttt_token(t, slot):
                when(pe, S["ttt_kA"], t)
                when(pe, S["ttt_dl"], t)
                for i in range(2):
                    for k in range(2):
                        rows = KA if k == 0 else HC
                        x_ = xT[0:rows, slot % 2, k, i, :]
                        pe.matmul(wide[0][0:N, i, 0:2 * C], x_, wtok[0:rows, k, 0:2 * C], start=(k == 0), stop=(k == 1))
                    for k in range(2):
                        rows = KA if k == 0 else HC
                        x_ = xT[0:rows, slot % 2, k, i, :]
                        ins = pe.matmul(bank[3][0:N, i * (C + HEADS):(i + 1) * (C + HEADS)], x_, wtok[0:rows, k, 2 * C:WTOK],
                                        start=(k == 0), stop=(k == 1))
                ins.then_inc(S["ttt_tok"], 1)

            def ttt_grad(t, slot):
                pe.wait_ge(S["ttt_zz"], t + 1)
                when(pe, S["ttt_gm"], t)
                for i in range(2):
                    for k in range(2):
                        a = 2 * i + k
                        ins = pe.matmul(bank[2][0:KA, a * HC:a * HC + HC], kA[:, slot % 2, i, k, :],
                                        zz[:, slot % 2, a * HC:a * HC + HC], start=True, stop=True)
                ins.then_inc(S["ttt_grad"], 1)

            def ttt_updated(t, slot):
                pe.wait_ge(S["ttt_w"], t + 1)
                pe.wait_ge(S["ttt_qs"], t + 1)
                when(pe, S["ttt_zc"], t)
                for i in range(2):
                    for k in range(2):
                        a = 2 * i + k
                        ins = pe.matmul(wide[1][0:N, 0, a * HC:a * HC + HC], qT[:, slot % 4, k, i * N:i * N + N],
                                        wn[:, slot % 2, i, k, :], start=True, stop=True)
                ins.then_inc(S["ttt_zb"], 1)

            def ttt_turn_back(t, slot):
                pe.wait_ge(S["ttt_zh"], t + 1)
                pe.wait_ge(S["ttt_xTs"], min(t + 3, PAIRS) if isinstance(t, int) else t + 3)
                for i in range(2):
                    for k in range(2):
                        a = 2 * i + k
                        ins = pe.transpose(bank[0][0:HC, (2 * k + i) * N:(2 * k + i + 1) * N],
                                           zh[:, slot % 2, a * HC:a * HC + HC], ident[0:N, 0:N])
                ins.then_inc(S["ttt_zT"], 1)

            def ttt_project(t, slot):
                pe.wait_ge(S["ttt_oT"], t + 1)
                when(pe, S["ttt_h"], t)
                for i in range(2):
                    for k in range(2):
                        rows = KA if k == 0 else HC
                        ins = pe.matmul(wide[1][0:N, 1, i * C:i * C + C], oT[0:rows, slot % 2, k, i, :], wp[0:rows, k, :],
                                        start=(k == 0), stop=(k == 1))
                ins.then_inc(S["ttt_out"], 1)

            def ttt(t, slot):
                fixed = isinstance(t, int)
                before, after = not (fixed and t == 0), not (fixed and t == PAIRS - 1)
                if before:
                    ttt_grad(t - 1, slot - 1)
                if after:
                    ttt_query(t + 1, slot + 1)
                if before:
                    ttt_updated(t - 1, slot - 1)
                if after:
                    ttt_token(t + 1, slot + 1)
                if before:
                    ttt_turn_back(t - 1, slot - 1)
                    ttt_project(t - 1, slot - 1)
                if not (fixed and t >= PAIRS - 2):
                    ttt_turn(t + 2, slot + 2)

            ttt_turn(0, 0)
            ttt_query(0, 0)
            ttt_token(0, 0)
            ttt_turn(1, 1)
            over_pairs(pe, ttt, 4)
            ttt_grad(PAIRS - 1, 3)
            ttt_updated(PAIRS - 1, 3)
            ttt_turn_back(PAIRS - 1, 3)
            ttt_project(PAIRS - 1, 3)

            pe.wait_ge(S["load_moe"], 128)
            pe.wait_ge(S["ttt_oT"], PAIRS)

            def rt_turn(t, slot):
                pe.wait_ge(S["rt_t"], t + 1)
                when(pe, S["rt_tTs"], t)
                for i in range(2):
                    for k in range(2):
                        ins = pe.transpose(bank[0][0:HC, (2 * k + i) * N:(2 * k + i + 1) * N],
                                           ts[:, slot, i, k * HC:k * HC + HC], ident[0:N, 0:N])
                ins.then_inc(S["rt_tT"], 1)

            def rt_logits(t, slot):
                pe.wait_ge(S["rt_tTs"], t + 1)
                when(pe, S["rt_gs"], t)
                for i in range(2):
                    for k in range(2):
                        nrow = KA if k == 0 else HC
                        ins = pe.matmul(bank[1][0:N, i * E1:i * E1 + E1], xT[0:nrow, slot, k, i, :], gate1[0:nrow, k, :],
                                        start=(k == 0), stop=(k == 1))
                ins.then_inc(S["rt_logit"], 1)

            def route(t, slot):
                if not last(t, PAIRS):
                    rt_turn(t + 1, 1 - slot)
                rt_logits(t, slot)

            rt_turn(0, 0)
            over_pairs(pe, route)
            pe.wait_ge(S["rt_mask"], 1)
            pe.matmul(bank[2][0:N, :], tri[:, :], work[:, 0, :], start=True, stop=True)
            pe.matmul(bank[3][0:N, :], ones[0:N, 0:N], work[:, 0, :], start=True, stop=True).then_inc(S["rt_max"], 1)

            def moe_turn(j, slot, half):
                pe.wait_ge(S[f"moe_x{slot}"], 16 * (half + 1))
                when(pe, S["moe_xTs"], j)
                for k in range(2):
                    ins = pe.transpose(bank[0][0:HC, k * 128:k * 128 + 128], xb[:, slot, k * HC:k * HC + HC], ident[:, :])
                ins.then_inc(S["moe_xT"], 1)

            def moe_up(j, slot, half, e):
                pe.wait_ge(S["moe_xTs"], j + 1)
                when(pe, S["moe_al"], j)
                for k in range(2):
                    nrow = KA if k == 0 else HC
                    ins = pe.matmul(bank[1][:, 0:2 * I1], xTm[0:nrow, slot, k, :], m1[0:nrow, bass.ds(e, 1), k, :],
                                    start=(k == 0), stop=(k == 1))
                ins.then_inc(S["moe_h"], 1)

            def moe_turn_back(j, slot, half):
                pe.wait_ge(S["moe_act"], j + 1)
                when(pe, S["moe_aTs"], j)
                for k in range(2):
                    ins = pe.transpose(bank[2][0:HC, k * 128:k * 128 + 128], ac[:, slot, k * HC:k * HC + HC], ident[:, :])
                ins.then_inc(S["moe_aT"], 1)

            def moe_down(j, slot, half, e):
                pe.wait_ge(S["moe_aTs"], j + 1)
                when(pe, S["moe_ys"], j)
                for k in range(2):
                    nrow = KA if k == 0 else HC
                    ins = pe.matmul(bank[3][:, 0:C], aT[0:nrow, slot, k, :], m2[0:nrow, bass.ds(e, 1), k, :],
                                    start=(k == 0), stop=(k == 1))
                ins.then_inc(S["moe_y"], 1)

            def moe(j, slot, half):
                moe_up(j, slot, half, pe.value_load(etab[0:1, bass.ds(j, 1)]))
                if not first(j):
                    moe_turn_back(*before(j, slot, half))
                if not last(j, BLOCKS):
                    moe_turn(*after(j, slot, half))
                if not first(j):
                    moe_down(*before(j, slot, half), pe.value_load(etab[0:1, bass.ds(j - 1, 1)]))

            pe.wait_ge(S["rt_done"], 1)
            moe_turn(0, 0, 0)
            over_blocks(pe, moe)
            moe_turn_back(BLOCKS - 1, 1, BLOCKS // 2 - 1)
            moe_down(BLOCKS - 1, 1, BLOCKS // 2 - 1, pe.value_load(etab[0:1, BLOCKS - 1:BLOCKS]))

        @block.vector
        def _(dve):
            V = nc.vector
            chained = [0]

            def link(ins):
                chained[0] += 1
                ins.then_inc(S["dve_chain"], 1)
                dve.wait_ge(S["dve_chain"], chained[0])

            V.memset(ones[:, :], 1.0)
            V.memset(avg128[:, :], 1.0 / 128)
            V.memset(avgN[:, :], 1.0 / N)
            V.memset(mhalf[:, :], -0.5)
            V.memset(xT[HC:KA, :, :, :, :], 1.0)
            V.memset(qT[HC:KA, :, :, :], 1.0)
            V.memset(oT[HC:KA, :, :, :, :], 1.0)
            V.memset(kS[:, :, :, :, HC:KA], 1.0)
            V.memset(vS[:, :, :, :, HC:KA], 1.0)
            V.memset(ksm[HC:KA, :, :, :, :], TTT_EPS).then_inc(S["const_ready"], 1)
            V.memset(fill[:, :, 0:C], 0.0)
            V.memset(fill[:, :, C + 1:RW], 0.0)
            dve.wait_ge(S["load_idx"], 48)
            V.tensor_copy(fill[:, :, C], dump[:, :]).then_inc(S["filled"], 1)
            dve.wait_ge(S["load_idx"], 48)
            V.tensor_scalar(idxc[:, :], idx[:, :], 0, VOCAB - 1, ALU.max, ALU.min).then_inc(S["clipped"], 1)
            V.tensor_scalar(keep[:, 0, :], idxm[:, :], 0, None, ALU.is_ge).then_inc(S["mask_lo"], 1)
            V.tensor_scalar(keep[:, 1, :], idxm[:, :], VOCAB - 1, None, ALU.is_le).then_inc(S["mask_hi"], 1)
            dve.wait_ge(S["mask_lo"], 1)
            dve.wait_ge(S["mask_hi"], 1)
            V.tensor_tensor(keep[:, 0, :], keep[:, 0, :], keep[:, 1, :], ALU.mult).then_inc(S["mask_lo"], 1)

            dve.wait_ge(S["load_x"], 64)
            with dve.Fori(0, B // 4) as turn:
                for j in range(4):
                    ins = V.bn_stats(tstat[:, bass.ds(turn * 4 + j, 1), :].rearrange("p a s -> p (a s)"),
                                     X[:, bass.ds(turn * 4 + j, 1), :].rearrange("p a w -> p (a w)"))
                ins.then_inc(S["tok_dev"], 1)
            dve.wait_ge(S["load_tok"], 80)
            for c in range(3):
                V.tensor_scalar(convT[:, c], projT[:, 0], convb[:, c:c + 1], None, ALU.mult).then_inc(S["tok_bias0"], 1)
            for o in (1, 2):
                for c in range(3):
                    dve.wait_ge(S["tok_bias0"], 3 * o + c - 2)
                    V.scalar_tensor_tensor(out=convT[:, c], in0=projT[:, o], scalar=convb[:, 3 * o + c:3 * o + c + 1],
                                           in1=convT[:, c], op0=ALU.mult, op1=ALU.add).then_inc(S["tok_bias0"], 1)
            dve.wait_ge(S["const_ready"], 1)
            for j in range(GRP):
                V.tensor_copy(xg[:, 1, :, j * NI:j * NI + NI], lnwb[:, 1, :].rearrange("p (k l) -> p k l", k=CHUNKS))
            for k in range(CHUNKS):
                ins = V.tensor_scalar(xg[:, 0, k, :], ones[:, 0:ROWS], convb[:, 9 + k // 2:10 + k // 2], None, ALU.mult)
            dve.wait_ge(S["tok_bias0"], 9)
            ins.then_inc(S["tok_w"], 1)
            dve.wait_ge(S["tok_dev"], B // 4)
            n_half = XW // 2
            T = tsmall
            link(V.tensor_tensor(T[:, 0, :], tstat[:, :, 1], tstat[:, :, 4], ALU.add))
            V.tensor_scalar(T[:, 0, :], T[:, 0, :], 0.5, None, ALU.mult).then_inc(S["tok_stat"], 1)
            dve.wait_ge(S["tok_mean"], 1)
            link(V.tensor_copy(T[:, 1, :], bank[0][:, 0:B]))
            for q, src in ((2, 1), (4, 4)):
                link(V.tensor_tensor(T[:, q, :], tstat[:, :, src], T[:, 1, :], ALU.subtract))
                link(V.tensor_tensor(T[:, q, :], T[:, q, :], T[:, q, :], ALU.mult))
            link(V.tensor_tensor(T[:, 2, :], T[:, 2, :], T[:, 4, :], ALU.add))
            link(V.tensor_tensor(T[:, 4, :], tstat[:, :, 2], tstat[:, :, 5], ALU.add))
            V.scalar_tensor_tensor(out=T[:, 3, :], in0=T[:, 4, :], scalar=1.0 / n_half, in1=T[:, 2, :],
                                   op0=ALU.mult, op1=ALU.add).then_inc(S["tok_varsum"], 1)
            dve.wait_ge(S["tok_devavg"], 1)
            V.tensor_scalar(T[:, 4, :], bank[1][:, 0:B], 0.5, LN_EPS, ALU.mult, ALU.add).then_inc(S["tok_eps"], 1)
            dve.wait_ge(S["tok_bias_mm"], 1)
            V.tensor_tensor(tokb[:, :], bank[2][0:ROWS, 0:C], projb[:, :], ALU.add).then_inc(S["tok_bias"], 1)
            dve.wait_ge(S["tok_bias"], 1)
            V.tensor_tensor(tokb[:, :], tokb[:, :], pos[:, :], ALU.add).then_inc(S["tok_bias"], 1)
            dve.wait_ge(S["tok_rstd"], 1)

            def patch_scale(g, slot, count):
                when(dve, S["tok_mm"], g - 1)
                for j in range(count):
                    b = g * GRP + j
                    ins = V.tensor_scalar(X[:, bass.ds(b, 1), :].rearrange("p a w -> p (a w)"),
                                          X[:, bass.ds(b, 1), :].rearrange("p a w -> p (a w)"),
                                          T[:, 1, bass.ds(b, 1)], T[:, 5, bass.ds(b, 1)], ALU.subtract, ALU.mult)
                ins.then_inc(S["tok_norm"], 1)
                dve.wait_ge(S["tok_norm"], g + 1)
                for j in range(count):
                    ins = V.tensor_tensor(xg[:, slot, :, j * NI:j * NI + NI],
                                          X[:, bass.ds(g * GRP + j, 1), :].rearrange("p a (k l) -> p (a k) l", k=CHUNKS),
                                          lnwb[:, 0, :].rearrange("p (k l) -> p k l", k=CHUNKS), ALU.mult)
                ins.then_inc(S["tok_xg"], 1)

            def patch_add(g, slot, count, uses):
                dve.wait_ge(S["tok_mm"], g + 1)
                dve.wait_ge(S["tok_bias"], 2)
                when(dve, S[f"tok_piece{slot}"], 16 * GRP * uses)
                rows = NI * count
                V.tensor_tensor(tok[0:rows, slot, :], bank[slot][0:rows, 0:C], tokb[0:rows, :], ALU.add)\
                 .then_inc(S["tok_sum"], 1)

            patch_scale(0, 0, GRP)
            patch_scale(1, 1, GRP)
            patch_add(0, 0, GRP, 0)
            patch_scale(2, 0, GRP)
            patch_add(1, 1, GRP, 0)
            patch_scale(3, 1, GRP)
            with dve.Fori(1, 4) as turn:
                patch_add(turn * 2, 0, GRP, turn)
                patch_scale(turn * 2 + 2, 0, GRP)
                patch_add(turn * 2 + 1, 1, GRP, turn)
                patch_scale(turn * 2 + 3, 1, GRP)
            patch_add(8, 0, GRP, 4)
            patch_scale(10, 0, 2)
            patch_add(9, 1, GRP, 4)
            patch_add(10, 0, 2, 5)

            dve.wait_ge(S["mask_lo"], 2)
            dve.wait_ge(S["tok_piece0"], 16 * (5 * GRP + 2))
            dve.wait_ge(S["tok_piece1"], 16 * 5 * GRP)
            dve.wait_ge(S["gathered"], 16 * B)

            def image(t_, b, i=1):
                return t_[:, bass.ds(b, 1), :].rearrange("p a c -> p (a c)")

            with dve.Fori(0, B // 4) as turn:
                for j in range(4):
                    b = turn * 4 + j
                    ins = V.tensor_scalar(image(h, b), image(h, b), keep[:, 0, bass.ds(b, 1)], None, ALU.mult)
                ins.then_inc(S["masked"], 1)
                dve.wait_ge(S["masked"], turn + 1)
                for j in range(4):
                    ins = V.bn_stats(image(stats, turn * 4 + j), image(h, turn * 4 + j))
                ins.then_inc(S["ln0_stat"], 1)

            def finish_stats(k, sem, count):
                dve.wait_ge(sem, count)
                V.tensor_tensor(lns[:, 0, :], stats[:, :, 1], stats[:, :, 4], ALU.add)
                V.tensor_tensor(lns[:, 1, :], stats[:, :, 1], stats[:, :, 4], ALU.subtract)
                link(V.tensor_tensor(lns[:, 2, :], stats[:, :, 2], stats[:, :, 5], ALU.add))
                V.tensor_scalar(mean[:, :], lns[:, 0, :], 0.5, None, ALU.mult)
                link(V.scalar_tensor_tensor(out=lns[:, 3, :], in0=lns[:, 1, :], scalar=0.25, in1=lns[:, 1, :],
                                            op0=ALU.mult, op1=ALU.mult))
                link(V.scalar_tensor_tensor(out=lns[:, 0, :], in0=lns[:, 2, :], scalar=1.0 / C, in1=lns[:, 3, :],
                                            op0=ALU.mult, op1=ALU.add))
                V.tensor_scalar(lns[:, 3, :], lns[:, 0, :], LN_EPS, None, ALU.add).then_inc(S["ln_e"], 1)
                dve.wait_ge(S["ln_rstd"], k + 1)

            def normalise(t, slot, sem, free, n_free):
                when(dve, free, n_free)
                for i in range(2):
                    b = t * 2 + i
                    ins = V.tensor_scalar(xn[:, slot, i, :], image(h, b), mean[:, bass.ds(b, 1)],
                                          rstd[:, bass.ds(b, 1)], ALU.subtract, ALU.mult)
                ins.then_inc(sem, 1)

            finish_stats(0, S["ln0_stat"], B // 4)
            dve.wait_ge(S["load_att"], 64)
            mask4 = mask[0:HC, :].rearrange("p (a c) -> p a c", a=1)

            def att_rest(t, slot):
                dve.wait_ge(S["att_out"], t + 1)
                V.tensor_tensor(h[:, bass.ds(t * 2, 2), :], bank[3][0:N, 0:2 * C].rearrange("p (i c) -> p i c", i=2),
                                h[:, bass.ds(t * 2, 2), :], ALU.add).then_inc(S["att_h"], 1)
                dve.wait_ge(S["att_h"], t + 1)
                for i in range(2):
                    ins = V.bn_stats(image(stats, t * 2 + i), image(h, t * 2 + i))
                ins.then_inc(S["att_stat"], 1)

            def att_divide(t, slot):
                dve.wait_ge(S["att_frac"], t + 1)
                V.reciprocal(rden[:, :], wide[1][0:N, 0, 2 * C:2 * C + 2 * HEADS]).then_inc(S["att_rden"], 1)
                dve.wait_ge(S["att_rden"], t + 1)
                when(dve, S["att_oTp"], t - 1)
                V.tensor_tensor(on[:, slot].rearrange("p i h (a d) -> p (i h a) d", d=HD),
                                wide[1][0:N, 0, 0:2 * C].rearrange("p (a d) -> p a d", d=HD),
                                rden[:, :].rearrange("p (a d) -> p a d", d=1).broadcast_to([N, 2 * HEADS, HD]),
                                ALU.mult).then_inc(S["att_on"], 1)

            def attention(t, slot):
                first = isinstance(t, int) and t == 0
                dve.wait_ge(S["att_kv"], t + 1)
                when(dve, S["att_prod"], t - 1)
                V.tensor_scalar(kS[:, slot, :, :, 0:HC], wide[0][0:N, :, 0:C].rearrange("p i (h c) -> p i h c", h=2),
                                0.0, HD ** -0.5, ALU.max, ALU.add).then_inc(S["att_ks"], 1)
                if not first:
                    att_divide(t - 1, 1 - slot)
                dve.wait_ge(S["att_q"], t + 1)
                when(dve, S["att_frac"], t - 1)
                V.tensor_scalar(qT[0:HC, slot].rearrange("p h n -> p (h n)"), bank[1][0:HC, 0:4 * N],
                                0.0, HD ** -0.5, ALU.max, ALU.add).then_inc(S["att_qs"], 1)
                dve.wait_ge(S["att_prod"], t + 1)
                prod = bank[2][0:HC, 0:4 * KA].rearrange("p (a c) -> p a c", a=4)
                V.tensor_tensor(kvm[:, slot].rearrange("p i h c -> p (i h) c"), prod[:, :, 0:HC],
                                mask4.broadcast_to([HC, 4, HC]), ALU.mult)
                V.tensor_tensor(ksm[0:HC, slot].rearrange("p i h c -> p (i h) c"),
                                prod[:, :, HC:KA].broadcast_to([HC, 4, HH]),
                                mask4[:, :, 0:HC:HD].broadcast_to([HC, 4, HH]), ALU.mult).then_inc(S["att_ksm"], 1)
                if not first:
                    att_rest(t - 1, 1 - slot)
                if not (isinstance(t, int) and t + 2 >= PAIRS):
                    normalise(t + 2, slot, S["att_xn"], S["att_xT"], t + 1)

            normalise(0, 0, S["att_xn"], None, 0)
            normalise(1, 1, S["att_xn"], None, 0)
            over_pairs(dve, attention)
            att_divide(PAIRS - 1, 1)
            att_rest(PAIRS - 1, 1)

            finish_stats(1, S["att_stat"], PAIRS)

            def gate0(t, slot):
                normalise(t, slot, S["gate0_xn"], S["gate0_mean"], t - 1)

            over_pairs(dve, gate0)
            dve.wait_ge(S["gate0_mean"], PAIRS)
            dve.wait_ge(S["load_ffn"], 64)
            link(V.tensor_copy(gm[:, :, :].rearrange("p h b -> p (h b)"), bank[1][0:HC, 0:2 * B]))
            for k in range(2):
                ins = V.tensor_tensor(gprod[:, k], gm[:, k, :].rearrange("p (b a) -> p b a", a=1).broadcast_to([HC, B, E0]),
                                      wg0[:, k, :].rearrange("p (a e) -> p a e", a=1).broadcast_to([HC, B, E0]), ALU.mult)
            ins.then_inc(S["gate0_prod"], 1)
            dve.wait_ge(S["gate0_logit"], 1)
            logit = bank[2][:, 0:B * E0].rearrange("p (b e) -> p b e", e=E0)

            def spread(v, e=E0):
                return v.rearrange("p (b a) -> p b a", a=1).broadcast_to([128, B, e])

            link(V.tensor_reduce(gone[:, 0, :], logit, AX_X, ALU.max))
            V.tensor_tensor(gsm[:, 0], logit, spread(gone[:, 0, :]), ALU.subtract).then_inc(S["gate0_step"], 1)
            dve.wait_ge(S["gate0_exp"], 1)
            ex = gsm[:, 1]
            V.tensor_reduce(gone[:, 1, :], ex, AX_X, ALU.add)
            link(V.tensor_reduce(gone[:, 0, :], ex, AX_X, ALU.max))
            V.reciprocal(gone[:, 2, :], gone[:, 1, :])
            link(V.tensor_tensor(gsm[:, 0], ex, spread(gone[:, 0, :]), ALU.is_lt))
            V.tensor_tensor(gone[:, 4, :], gone[:, 2, :], gone[:, 0, :], ALU.mult)
            link(V.tensor_scalar(gone[:, 3, :], gsm[:, 0, :, 1], 1.0, None, ALU.add))
            V.tensor_tensor(sel[:, :], gone[0:1, 3, :], gsm[0:1, 0, :, 0], ALU.mult).then_inc(S["gate0_ready"], 1)

            def ffn_add(u, i):
                dve.wait_ge(S["ffn_y"], u + 1)
                V.scalar_tensor_tensor(out=image(h, u), in0=bank[3][0:N, i * 256:i * 256 + C],
                                       scalar=gone[0:N, 4, bass.ds(u, 1)], in1=image(h, u),
                                       op0=ALU.mult, op1=ALU.add).then_inc(S["ffn_h"], 1)
                dve.wait_ge(S["ffn_h"], u + 1)
                V.bn_stats(image(stats, u), image(h, u)).then_inc(S["ffn_stat"], 1)

            def ffn_hT(u, i):
                dve.wait_ge(S["ffn_hT"], u + 1)
                when(dve, S["ffn_y"], u - 1)
                V.tensor_copy(hT[:, i, 0:3, :], bank[1][:, 0:3 * N].rearrange("p (k n) -> p k n", k=3))\
                 .then_inc(S["ffn_hTv"], 1)

            def ffn(t, slot):
                for i in range(2):
                    u = t * 2 + i
                    if not first(u):
                        ffn_hT(u - 1, 1 - i)
                    if i == 0 and not (isinstance(t, int) and t + 2 >= PAIRS):
                        normalise(t + 2, slot, S["ffn_xn"], S["ffn_xT"], t + 1)
                    if not first(u):
                        ffn_add(u - 1, 1 - i)

            normalise(0, 0, S["ffn_xn"], S["gate0_mean"], PAIRS)
            normalise(1, 1, S["ffn_xn"], None, 0)
            over_pairs(dve, ffn)
            ffn_hT(B - 1, 1)
            ffn_add(B - 1, 1)

            dve.wait_ge(S["load_ttt"], 128)
            heads_of_w = w1b[:, :, :].rearrange("p m (a d) -> p (m a) d", d=HD)
            link(V.tensor_reduce(w1m[:, :], heads_of_w, AX_X, ALU.add))
            link(V.tensor_scalar(w1m[:, :], w1m[:, :], 1.0 / HD, None, ALU.mult))
            V.tensor_tensor(w1c[:, :, :].rearrange("p m (a d) -> p (m a) d", d=HD), heads_of_w,
                            w1m[:, :].rearrange("p (a d) -> p a d", d=1).broadcast_to([KA, HEADS, HD]), ALU.subtract)\
             .then_inc(S["tw_cent"], 1)
            other = wtok[:, :, 2 * C:3 * C]
            link(V.tensor_tensor(other, other, wv[:, :, :], ALU.subtract))
            link(V.tensor_tensor(other, other, gam[0:KA, :].rearrange("p (a c) -> p a c", a=1).broadcast_to([KA, 2, C]),
                                 ALU.mult))
            for i in range(2):
                V.tensor_tensor(gam2[:, i, :], gam[:, :], gam[:, :], ALU.mult)
            V.memset(kA[:, :, :, :, HC:KA], 1.0)
            for k, value in enumerate((TTT_EPS, 1.0 / (HD * N), 1.0 / HD)):
                V.memset(tc[:, k, :], value)
            dve.wait_ge(S["tw_comp"], 1)
            V.tensor_scalar(gcol[:, 0:2], gcol[:, 0:2], -1.0, None, ALU.mult)
            V.tensor_copy(wtok[0:HC, :, C:2 * C], bank[1][0:HC, 0:4 * HC].rearrange("p (k c) -> p k c", k=2))
            dve.wait_ge(S["tw_cent"], 1)
            V.tensor_copy(wtok[HC:KA, 0, C:2 * C], w1c[HC:KA, :, :].rearrange("p m c -> p (m c)"))
            V.tensor_tensor(wp[HC:KA, 0, :], bank[2][HC:KA, 0:C], wp[HC:KA, 0, :], ALU.add).then_inc(S["tw_done"], 1)
            dve.wait_ge(S["tw_done"], 1)
            finish_stats(2, S["ffn_stat"], B)

            def heads(v):
                return v.rearrange("p (a d) -> p a d", d=HD)

            def per_head(v):
                return v.rearrange("p (a d) -> p a d", d=1).broadcast_to([N, 2 * HEADS, HD])

            mask97 = mask[:, :].rearrange("p (a c) -> p a c", a=1).broadcast_to([KA, 4, HC])

            def ttt_weights(t, slot):
                dve.wait_ge(S["ttt_grad"], t + 1)
                when(dve, S["ttt_w"], t)
                V.tensor_tensor(gmk[:, :].rearrange("p (a c) -> p a c", a=4),
                                bank[2][0:KA, 0:4 * HC].rearrange("p (a c) -> p a c", a=4), mask97, ALU.mult)\
                 .then_inc(S["ttt_gm"], 1)
                dve.wait_ge(S["ttt_gm"], t + 1)
                when(dve, S["ttt_zb"], t - 1)
                V.tensor_tensor(wn[:, slot % 2].rearrange("p i m c -> p i (m c)"),
                                w1b[:, :, :].rearrange("p (a m) c -> p a (m c)", a=1).broadcast_to([KA, 2, C]),
                                gmk[:, :].rearrange("p (i c) -> p i c", i=2), ALU.subtract).then_inc(S["ttt_w"], 1)

            def ttt_centre(t, slot):
                s_ = sm[:, slot % 2]
                z = heads(wide[1][0:N, 0, 0:2 * C])
                dve.wait_ge(S["ttt_zb"], t + 1)
                V.tensor_reduce(s_[:, 4, :], z, AX_X, ALU.add).then_inc(S["ttt_zm"], 1)
                dve.wait_ge(S["ttt_zm"], t + 1)
                when(dve, S["ttt_zh"], t)
                V.scalar_tensor_tensor(out=heads(zc[:, :]), in0=per_head(s_[:, 4, :]), scalar=1.0 / HD, in1=z,
                                       op0=ALU.mult, op1=ALU.subtract).then_inc(S["ttt_zc"], 1)

            def ttt_combine(t, slot):
                dve.wait_ge(S["ttt_zT"], t + 1)
                when(dve, S["ttt_out"], t - 1)
                for k in range(2):
                    ins = V.scalar_tensor_tensor(
                        out=oT[0:HC, slot % 2, k].rearrange("p i n -> p (i n)"), in0=bank[0][0:HC, k * 2 * N:(k + 1) * 2 * N],
                        scalar=gcol[:, k:k + 1], in1=qT[0:HC, slot % 4, k, :], op0=ALU.mult, op1=ALU.add)
                ins.then_inc(S["ttt_oT"], 1)

            def ttt_add(t, slot):
                dve.wait_ge(S["ttt_out"], t + 1)
                V.tensor_tensor(h[:, bass.ds(t * 2, 2), :], wide[1][0:N, 1, 0:2 * C].rearrange("p (i c) -> p i c", i=2),
                                h[:, bass.ds(t * 2, 2), :], ALU.add).then_inc(S["ttt_h"], 1)
                dve.wait_ge(S["ttt_h"], t + 1)
                for i in range(2):
                    ins = V.bn_stats(image(stats, t * 2 + i), image(h, t * 2 + i))
                ins.then_inc(S["ttt_stat"], 1)

            def ttt(t, slot):
                fixed = isinstance(t, int)
                before = not (fixed and t == 0)
                s_ = sm[:, slot % 2]
                if not (fixed and t + 2 >= PAIRS):
                    normalise(t + 2, slot % 2, S["ttt_xn"], S["ttt_xT"], t + 1)
                if before:
                    ttt_weights(t - 1, slot - 1)
                dve.wait_ge(S["ttt_sq"], t + 1)
                V.tensor_reduce(s_[:, 0, :], heads(sq[:, :]), AX_X, ALU.add).then_inc(S["ttt_v"], 1)
                if before:
                    ttt_centre(t - 1, slot - 1)
                dve.wait_ge(S["ttt_rstd"], t + 1)
                V.tensor_tensor(xh[:, :].rearrange("p (x a d) -> p x a d", x=4, d=HD),
                                kA[:, slot % 2, :, 2:4, 0:HC].rearrange("p i m (a d) -> p i m a d", d=HD),
                                s_[:, 1, :].rearrange("p (x a d) -> p x a d", x=4, d=1).broadcast_to([N, 4, HH, HD]),
                                ALU.mult).then_inc(S["ttt_xh"], 1)
                if before:
                    dve.wait_ge(S["ttt_zsq"], t)
                    V.tensor_reduce(sm[:, (slot - 1) % 2, 5, :], heads(zsq[:, :]), AX_X, ALU.add).then_inc(S["ttt_zv"], 1)
                dve.wait_ge(S["ttt_t1"], t + 1)
                V.tensor_tensor(gg[:, :].rearrange("p (i c) -> p i c", i=2), t1[:, :].rearrange("p (i c) -> p i c", i=2),
                                dl[:, slot % 2, :, 0:C], ALU.add).then_inc(S["ttt_g"], 1)
                dve.wait_ge(S["ttt_g"], t + 1)
                V.tensor_tensor(pp[:, :], gg[:, :], xh[:, :], ALU.mult).then_inc(S["ttt_p"], 1)
                dve.wait_ge(S["ttt_p"], t + 1)
                V.tensor_reduce(s_[:, 3, :], heads(pp[:, :]), AX_X, ALU.add).then_inc(S["ttt_s"], 1)
                if before:
                    dve.wait_ge(S["ttt_zr"], t)
                    when(dve, S["ttt_zT"], t - 2)
                    V.tensor_tensor(heads(zh[:, (slot - 1) % 2, :]), heads(zc[:, :]), per_head(sm[:, (slot - 1) % 2, 6, :]),
                                    ALU.mult).then_inc(S["ttt_zh"], 1)
                dve.wait_ge(S["ttt_r"], t + 1)
                dve.wait_ge(S["ttt_s"], t + 1)
                V.tensor_tensor(heads(pp[:, :]), heads(gg[:, :]), per_head(s_[:, 2, :]), ALU.mult).then_inc(S["ttt_gr"], 1)
                dve.wait_ge(S["ttt_gr"], t + 1)
                dve.wait_ge(S["ttt_xs"], t + 1)
                when(dve, S["ttt_grad"], t - 1)
                V.tensor_tensor(zz[:, slot % 2, :], pp[:, :], xs[:, :], ALU.subtract).then_inc(S["ttt_zz"], 1)
                if before:
                    ttt_combine(t - 1, slot - 1)
                    ttt_add(t - 1, slot - 1)

            normalise(0, 0, S["ttt_xn"], None, 0)
            normalise(1, 1, S["ttt_xn"], None, 0)
            over_pairs(dve, ttt, 4)
            t, slot = PAIRS - 1, 3
            ttt_weights(t, slot)
            ttt_centre(t, slot)
            dve.wait_ge(S["ttt_zsq"], t + 1)
            V.tensor_reduce(sm[:, slot % 2, 5, :], heads(zsq[:, :]), AX_X, ALU.add).then_inc(S["ttt_zv"], 1)
            dve.wait_ge(S["ttt_zr"], t + 1)
            V.tensor_tensor(heads(zh[:, slot % 2, :]), heads(zc[:, :]), per_head(sm[:, slot % 2, 6, :]), ALU.mult)\
             .then_inc(S["ttt_zh"], 1)
            ttt_combine(t, slot)
            ttt_add(t, slot)

            dve.wait_ge(S["load_moe"], 128)
            finish_stats(3, S["ttt_stat"], PAIRS)
            link(V.tensor_tensor(lns[:, 1, :], lns[:, 0, :], rstd[:, :], ALU.mult))
            link(V.tensor_tensor(lns[:, 1, :], lns[:, 1, :], rstd[:, :], ALU.mult))
            link(V.tensor_scalar(lns[:, 1, :], lns[:, 1, :], RMS_EPS, None, ALU.add))
            V.memset(aT[HC:KA, :, :, :], 1.0)
            V.memset(xTm[HC:KA, :, :, :], 1.0).then_inc(S["rt_rms"], 1)
            dve.wait_ge(S["rt_rms"], 2)

            def rt_rows(t, slot):
                when(dve, S["rt_tT"], t - 1)
                when(dve, S["rt_row"], t - 1)
                normalise(t, slot, S["rt_xn"], None, 0)
                dve.wait_ge(S["rt_xn"], t + 1)
                for i in range(2):
                    ins = V.scalar_tensor_tensor(out=ts[:, slot, i, :], in0=xn[:, slot, i, :],
                                                 scalar=rr[:, bass.ds(t * 2 + i, 1)], in1=scale[:, :],
                                                 op0=ALU.mult, op1=ALU.mult)
                ins.then_inc(S["rt_t"], 1)
                V.tensor_tensor(h[:, bass.ds(t * 2, 2), :], h[:, bass.ds(t * 2, 2), :], xn[:, slot], ALU.add)

            def rt_choose(t, slot):
                dve.wait_ge(S["rt_logit"], t + 1)
                when(dve, S["rt_top"], t - 1)
                V.tensor_copy(gs[:, slot], bank[1][0:N, 0:2 * E1].rearrange("p (i e) -> p i e", i=2))\
                 .then_inc(S["rt_gs"], 1)
                dve.wait_ge(S["load_moe"], 128)
                dve.wait_ge(S["rt_gs"], t + 1)
                for i in range(2):
                    ins = V.max(m8[:, slot, i, :], gs[:, slot, i, :])
                ins.then_inc(S["rt_max"], 1)
                dve.wait_ge(S["load_moe"], 128)
                dve.wait_ge(S["rt_max"], t + 1)
                for i in range(2):
                    ins = V.max_index(i8[:, slot, i, :], m8[:, slot, i, :], gs[:, slot, i, :])
                ins.then_inc(S["rt_idx"], 1)
                dve.wait_ge(S["rt_idx"], t + 1)
                V.tensor_copy(topi[:, bass.ds(t * 2, 2), :], i8[:, slot, :, 0:TOPK])
                V.tensor_copy(topv[:, bass.ds(t * 2, 2), :], m8[:, slot, :, 0:TOPK]).then_inc(S["rt_top"], 1)

            def route(t, slot):
                if not last(t, PAIRS):
                    rt_rows(t + 1, 1 - slot)
                rt_choose(t, slot)

            rt_rows(0, 0)
            over_pairs(dve, route)
            dve.wait_ge(S["rt_top"], PAIRS)

            def spread(v, count=TOPK):
                return v.rearrange("p (b a) -> p b a", a=1).broadcast_to([N, v.shape[1], count])

            link(V.tensor_copy(wsum, topv[:, :, 0]))
            link(V.tensor_tensor(topv, topv, spread(wsum), ALU.subtract))
            V.memset(work[:, 1, :], 1.0).then_inc(S["rt_pre"], 1)
            iota16 = iota_e[:, :].rearrange("p (a e) -> p a e", a=1).broadcast_to([N, B, E1])
            for k in range(TOPK):
                ins = V.tensor_tensor(chosen[:, k], spread(topi[:, :, k], E1), iota16, ALU.is_equal)
            link(ins)
            three = work[:, 0, :].rearrange("p (b e) -> p b e", e=E1)
            link(V.tensor_tensor(three, chosen[:, 0], chosen[:, 1], ALU.add))
            link(V.tensor_tensor(three, three, chosen[:, 2], ALU.add))
            V.tensor_tensor(three, three, chosen[:, 3], ALU.add).then_inc(S["rt_mask"], 1)
            dve.wait_ge(S["rt_max"], PAIRS + 1)
            cnt, run = work[:, 2, :], work[:, 3, :]
            by_eb = "p (e b) -> p e b"
            link(V.tensor_copy(cnt.rearrange(by_eb, b=B), bank[3][0:N, :].rearrange("p (b e) -> p e b", e=E1)))
            V.tensor_reduce(per_e[:, 0, :], cnt.rearrange(by_eb, b=B), AX_X, ALU.add)
            link(V.tensor_tensor_scan(run, work[:, 1, :], cnt, 0.0, ALU.mult, ALU.add))
            link(V.tensor_scalar(per_ei[:, 0, :], per_e[:, 0, :], 127.0, None, ALU.add))
            link(V.tensor_scalar(per_ei[:, 1, :], per_ei[:, 0, :], 7, None, ALU.arith_shift_right))
            link(V.tensor_copy(per_e[:, 1, :], per_ei[:, 1, :]))
            link(V.tensor_tensor_scan(per_e[:, 2, :], work[:, 1, 0:E1], per_e[:, 1, :], 0.0, ALU.mult, ALU.add))
            link(V.tensor_tensor(per_e[:, 3, :], per_e[:, 2, :], per_e[:, 1, :], ALU.subtract))
            link(V.tensor_tensor(per_e[:, 4, :], per_e[:, 0, :], run.rearrange(by_eb, b=B)[:, :, B - 1], ALU.subtract))
            link(V.scalar_tensor_tensor(out=per_e[:, 5, :], in0=per_e[:, 3, :], scalar=128.0, in1=per_e[:, 4, :],
                                        op0=ALU.mult, op1=ALU.add))
            link(V.tensor_tensor(run, run, cnt, ALU.subtract))
            run3 = run.rearrange(by_eb, b=B)
            link(V.tensor_tensor(run3, run3, spread(per_e[:, 5, :], B), ALU.add))
            place = work[:, 0, :].rearrange("p (b e) -> p b e", e=E1)
            link(V.tensor_tensor(place, bank[2][0:N, :].rearrange("p (b e) -> p b e", e=E1),
                                 run.rearrange("p (e b) -> p b e", b=B), ALU.add))
            for k in range(TOPK):
                link(V.tensor_tensor(chosen[:, k], chosen[:, k], place, ALU.mult))
                link(V.tensor_reduce(slot_of[:, :, k], chosen[:, k], AX_X, ALU.add))
            link(V.tensor_copy(slot_i[:, :, :], slot_of))
            ends = per_e[0:1, 2, :].rearrange("p (a e) -> p a e", a=1).broadcast_to([1, 32, E1])
            for q in range(BLOCKS // 32):
                grid = work[0:1, 2, :].rearrange("p (j e) -> p j e", e=E1)
                link(V.tensor_tensor(grid, ends, iota_b[:, 32 * q:32 * q + 32].rearrange("p (j a) -> p j a", a=1)
                                     .broadcast_to([1, 32, E1]), ALU.is_le))
                link(V.tensor_reduce(work[0:1, 3, 32 * q:32 * q + 32], grid, AX_X, ALU.add))
            link(V.tensor_scalar(etab[:, :], work[0:1, 3, 0:BLOCKS], float(E1 - 1), None, ALU.min))
            dve.wait_ge(S["rt_exp"], 1)
            link(V.tensor_reduce(wsum, wtop, AX_X, ALU.add))
            link(V.reciprocal(wsum, wsum))
            V.tensor_tensor(wtop, wtop, spread(wsum), ALU.mult).then_inc(S["rt_done"], 1)
            dve.wait_ge(S["rt_done"], 1)

            def meta(b, slot, half):
                when(dve, S[f"dispatched{slot}"], 16 * TOPK * half)
                V.tensor_copy(rowbuf[:, slot, :, C], image(target, b))
                V.tensor_copy(rowbuf[:, slot, :, C + 1], image(wtop, b))
                V.tensor_copy(slot_s[:, slot, :], image(slot_i, b)).then_inc(S["row_meta"], 1)

            over_images(dve, meta)

            def moe_gate(j, slot, half):
                dve.wait_ge(S["moe_h"], j + 1)
                when(dve, S["moe_sig"], j - 1)
                when(dve, S["moe_p"], j - 1)
                dve.wait_ge(S[f"moe_x{slot}"], 16 * (half + 1))
                when(dve, S["moe_ys"], j - 1)
                when(dve, S[f"moe_out{slot}"], 16 * half)
                V.tensor_copy(weight[:, slot, :], xb[:, slot, C + 1:C + 2])
                V.tensor_copy(dest[:, slot, :], xb[:, slot, C:C + 1]).then_inc(S["moe_meta"], 1)
                V.tensor_scalar(al[:, slot, 0:I1], bank[1][:, 0:I1], LIMIT, None, ALU.min)
                V.tensor_scalar(al[:, slot, I1:2 * I1], bank[1][:, I1:2 * I1], -LIMIT, LIMIT, ALU.max, ALU.min)\
                 .then_inc(S["moe_al"], 1)
                dve.wait_ge(S["moe_al"], j + 1)
                when(dve, S["moe_act"], j - 1)
                V.scalar_tensor_tensor(out=pr[:, slot, :], in0=al[:, slot, I1:2 * I1], scalar=1.0, in1=al[:, slot, 0:I1],
                                       op0=ALU.add, op1=ALU.mult).then_inc(S["moe_p"], 1)

            def moe_weigh(j, slot, half):
                dve.wait_ge(S["moe_y"], j + 1)
                dve.wait_ge(S["moe_meta"], j + 1)
                when(dve, S[f"moe_out{slot}"], 16 * half)
                V.tensor_scalar(ys[:, slot, :], bank[3][:, 0:C], weight[:, slot, :], None, ALU.mult)\
                 .then_inc(S["moe_ys"], 1)

            def moe(j, slot, half):
                moe_gate(j, slot, half)
                if not first(j):
                    moe_weigh(*before(j, slot, half))

            over_blocks(dve, moe)
            moe_weigh(BLOCKS - 1, 1, BLOCKS // 2 - 1)

            def final(b, slot, half):
                dve.wait_ge(S[f"fin_y{slot}"], 16 * (half + 1))
                when(dve, S["fin_b"], b)
                V.tensor_tensor(ya[:, :], yc[:, slot, 0:2 * C], yc[:, slot, 2 * C:4 * C], ALU.add).then_inc(S["fin_a"], 1)
                dve.wait_ge(S["fin_a"], b + 1)
                when(dve, S["fin_c"], b)
                V.tensor_tensor(yb[:, :], ya[:, 0:C], ya[:, C:2 * C], ALU.add).then_inc(S["fin_b"], 1)
                dve.wait_ge(S["fin_b"], b + 1)
                when(dve, S[f"stored{slot}"], 16 * half)
                V.tensor_tensor(yo[:, slot, :], yb[:, :], image(h, b), ALU.add).then_inc(S["fin_c"], 1)

            over_images(dve, final)


def halves(w):
    return w.T.reshape(2, HC, -1).transpose(1, 0, 2)


def with_bias(w, row):
    a = np.zeros((KA, 2, w.shape[0]), np.float32)
    a[:HC] = halves(w)
    a[HC, 0] = row
    return a


def layouts(inputs):
    g = {k: np.asarray(v) for k, v in inputs.items()}
    f = np.float32

    def patches(a):
        n = a.shape[0]
        a = a.reshape(n, 3, 6, 2, 8, 6, 16).transpose(4, 6, 0, 1, 3, 2, 5)
        return a.reshape(128, n, XW)

    ids = g["x_txt"].T
    idsm = np.zeros((N, B), ids.dtype)
    idsm[NI:] = ids
    convb = np.empty((128, 12), f)
    convb[:, 0:9] = g["L0_tok_conv_w"].reshape(1, 9)
    convb[:, 9:12] = g["L0_tok_conv_b"].reshape(1, 3)
    d = {}
    d["x"] = patches(g["x"])
    d["ids"] = ids
    d["idsm"] = idsm
    d["lnwb"] = np.concatenate([patches(g["L0_tok_ln_w"][None]), patches(g["L0_tok_ln_b"][None])], axis=1)
    d["convb"] = convb
    d["projT"] = g["L0_tok_proj_w"].reshape(C, 3, 2, 8, 16).transpose(3, 4, 1, 2, 0).reshape(128, 3, 2, C)
    d["projb"] = np.broadcast_to(g["L0_tok_proj_b"], (ROWS, C))
    d["pos"] = np.concatenate([g["L0_tok_pos_emb"][0]] * GRP, axis=0)
    d["table"] = g["L0_txt_weight"]
    d["att"] = with_bias(g["L0_attn_qkv_w"], 0)
    d["attp"] = with_bias(g["L0_attn_proj_w"], g["L0_attn_proj_b"])
    d["gate0"] = halves(g["L0_ffn_Wg"])
    d["f1"] = np.stack([with_bias(g["L0_ffn_W1"][e].T, g["L0_ffn_b1"][e]) for e in range(E0)], axis=1)
    d["f2"] = g["L0_ffn_W2"].reshape(E0, FT, 128, C).transpose(2, 0, 1, 3)
    d["fb2"] = g["L0_ffn_b2"][None]
    qkv = g["L1_attn_qkv_weight"]
    d["tq"] = with_bias(qkv[:C], g["L1_attn_q_bias"])
    wtok = np.zeros((KA, 2, WTOK), f)
    wtok[:, :, 0:C] = with_bias(qkv[C:2 * C], 0)
    wtok[:, :, 2 * C:3 * C] = with_bias(qkv[C:2 * C], g["L1_attn_ttt_norm_bias"].reshape(C))
    wtok[:, :, 3 * C:] = with_bias(g["L1_attn_ttt_lr_weight"][:, 0, :], g["L1_attn_ttt_lr_bias"][:, 0])
    d["tk"] = wtok
    d["tv"] = with_bias(qkv[2 * C:], g["L1_attn_v_bias"])
    d["tkn"] = qkv[C:2 * C].reshape(2, HC, C).transpose(1, 0, 2)
    gamma = g["L1_attn_ttt_norm_weight"].reshape(C)
    d["tg"] = np.broadcast_to(gamma, (N, C))
    d["tgc"] = np.concatenate([gamma.reshape(2, HC).T, g["L1_attn_ttt_norm_bias"].reshape(2, HC).T], axis=1)
    inner = np.zeros((KA, 2, HC), f)
    for n in range(HEADS):
        m, a = n // HH, (n % HH) * HD
        inner[a:a + HD, m, a:a + HD] = g["L1_attn_W1"][n]
        inner[HC, m, a:a + HD] = g["L1_attn_b1"][n, 0]
    d["tw"] = inner
    d["tp"] = with_bias(g["L1_attn_proj_weight"], g["L1_attn_proj_bias"])
    d["scale"] = np.broadcast_to(g["L1_ffn_scale"], (N, C))
    d["gate1"] = with_bias(g["L1_ffn_gate_w"], g["L1_ffn_gate_b"])
    d["m1"] = np.stack([with_bias(g["L1_ffn_w1"][e].T, g["L1_ffn_b1"][e]) for e in range(E1)], axis=1)
    d["m2"] = np.stack([with_bias(g["L1_ffn_w2"][e].T, g["L1_ffn_b2"][e]) for e in range(E1)], axis=1)
    d["tri"] = np.triu(np.ones((N, N), f), 1)
    d["iotae"] = np.broadcast_to(np.arange(E1, dtype=f), (N, E1))
    d["iotab"] = np.arange(BLOCKS, dtype=f)[None]
    p_, b_, k_ = np.ogrid[0:N, 0:B, 0:TOPK]
    d["target"] = ((b_ * N + p_) * TOPK + k_).astype(f)
    d["dump"] = (DUMP + np.arange(128)[:, None] + 128 * np.arange(2)[None]).astype(f)
    d["ident"] = np.eye(128, dtype=f)
    m = np.ones((KA, HC), f)
    m[:HC] = np.kron(np.eye(HH, dtype=f), np.ones((HD, HD), f))
    d["mask"] = m
    return d


NAMES = """x ids idsm lnwb convb projT projb pos table att attp gate0 f1 f2 fb2 tq tk tv tkn tg tgc tw tp scale gate1 m1 m2
ident mask tri iotae iotab target dump""".split()


def kernel(**inputs):
    import concourse.bacc as _bacc
    from concourse.bass_utils import run_bass_kernel_spmd as _run

    nc = _bacc.Bacc("TRN2", target_bir_lowering=False, num_devices=1)
    d = layouts(inputs)
    arrays, args = {}, []
    for name in NAMES:
        a = np.ascontiguousarray(d[name])
        arrays[f"in_{name}"] = a
        args.append(nc.dram_tensor(f"in_{name}", a.shape, mybir.dt.from_np(a.dtype), kind="ExternalInput").ap())
    args.append(nc.dram_tensor("out_0", (B, N, C), F32, kind="ExternalOutput").ap())
    build(nc, *args)
    r = _run(nc, [arrays], core_ids=[0])
    return r.results[0]["out_0"]
```

```python
from contextlib import ExitStack

import numpy as np

import concourse.bass as bass
from concourse import mybir

F32 = mybir.dt.float32
I32 = mybir.dt.int32
U32 = mybir.dt.uint32
ALU = mybir.AluOpType
ACT = mybir.ActivationFunctionType
AX_X = mybir.AxisListType.X

B = 32
NI, NW = 36, 77
N = NI + NW
C = 192
HC = C // 2
KA = HC + 1
PAIRS = B // 2
HEADS, HD = 12, 16
HH = HEADS // 2
F0 = 768
E0 = 3
FT = F0 // 128
E1, TOPK = 16, 4
I1 = 192
VOCAB = 8000
CHUNKS = 6
XW = CHUNKS * NI
GRP = 3
ROWS = GRP * NI
BLOCKS = (TOPK * N * B + E1 * 127) // 128
CAP = N * B + 128
SPARE = 16
SLOTS = E1 * CAP + SPARE * 128
RW = C + 2
DUMP = TOPK * N * B
PADS = E1 + 2
WTOK = 3 * C + HEADS
LN_EPS = 1e-5
TTT_EPS = 1e-6
RMS_EPS = 1e-5
ALPHA, LIMIT = 1.702, 7.0

SEMS = """load_x load_tok load_idx load_att load_ffn load_ttt load_moe const_ready dve_chain gathered tok_piece0 tok_piece1
tok_stat tok_dev tok_mean tok_devavg tok_varsum tok_eps tok_rstd tok_norm tok_xg tok_mm tok_sum tok_w tok_bias_mm
tok_bias0 tok_bias clipped mask_lo mask_hi masked ln0_stat att_xn att_xT att_xTs att_q att_kv att_qs att_ks att_vs
att_prod att_ksm att_frac att_rden att_on att_oTp att_oT att_out att_h att_stat gate0_xn gate0_mean gate0_prod
gate0_logit gate0_step gate0_exp gate0_ready ffn_xn ffn_xT ffn_xTs ffn_hid ffn_gelu ffn_hT ffn_hTv ffn_hTa ffn_y
ffn_h ffn_stat tw_cent tw_comp tw_done ttt_xn ttt_xT ttt_xTs ttt_q ttt_qs ttt_tok ttt_sq ttt_kA ttt_dl ttt_sig ttt_v
root ttt_rstd ttt_xh ttt_t1 ttt_g ttt_p ttt_s ttt_r ttt_gr ttt_xs ttt_zz ttt_grad ttt_gm ttt_w ttt_zb ttt_zm ttt_zc
ttt_zsq ttt_zv ttt_zh ttt_zT ttt_oT ttt_out ttt_h ttt_stat pool_inner rt_xn rt_t rt_tT rt_tTs rt_row rt_logit rt_gs
rt_exp rt_done filled row_t row_meta dispatched0 dispatched1 going loaded0 loaded1 loaded2 loaded3 moe_xT moe_xTs
moe_h moe_al moe_sig moe_p moe_act moe_aT moe_aTs moe_y moe_ys moe_out0 moe_out1 fin_a fin_b fin_c stored0 stored1
rt_less rt_taken rt_count rt_base rt_step rt_blocks pad_ready padded""".split()


def when(eng, sem, n):
    if not isinstance(n, int) or n > 0:
        eng.wait_ge(sem, n)


def over_pairs(eng, step, unroll=2):
    step(0, 0)
    step(1, 1)
    with eng.Fori(0, (PAIRS - 4) // unroll) as turn:
        for j in range(unroll):
            step(turn * unroll + (2 + j), (2 + j) % unroll)
    step(PAIRS - 2, (PAIRS - 2) % unroll)
    step(PAIRS - 1, (PAIRS - 1) % unroll)


def over_fours(eng, step, count):
    for j in range(4):
        step(0, j)
    with eng.Fori(1, count // 4 - 1) as turn:
        for j in range(4):
            step(turn, j)
    for j in range(4):
        step(count // 4 - 1, j)


def at(turn, j):
    return turn * 4 + j, j % 4, turn * 2 + j // 2


def over_twos(eng, step, count):
    for j in range(2):
        step(0, j)
    with eng.Fori(1, count // 2 - 1) as turn:
        for j in range(2):
            step(turn, j)
    for j in range(2):
        step(count // 2 - 1, j)


def at_two(turn, j):
    return turn * 2 + j, j % 2, turn + j // 2


def over_blocks(eng, step):
    over_fours(eng, step, BLOCKS)


def over_images(eng, step):
    over_fours(eng, step, B)


def first(n):
    return isinstance(n, int) and n == 0


def last(n, count):
    return isinstance(n, int) and n == count - 1


def build(nc, x_d, ids_d, idsm_d, lnwb_d, convb_d, projT_d, projb_d, pos_d, table_d, att_d, attp_d, gate0_d,
          f1_d, f2_d, fb2_d, tq_d, tk_d, tv_d, tkn_d, tg_d, tgc_d, tw_d, tp_d, scale_d, gate1_d, m1_d, m2_d,
          ident_d, mask_d, tri_d, iota_d, target_d, dump_d, out_d):
    ctx = ExitStack()
    with ctx:
        def sb(name, shape, dt=F32):
            return ctx.enter_context(nc.sbuf_tensor(name, shape, dt))

        S = {n: ctx.enter_context(nc.semaphore(n)) for n in SEMS}
        bank = [ctx.enter_context(nc.psum_tensor(f"bank{i}", [128, 512], F32)) for i in range(4)]
        wide = [ctx.enter_context(nc.psum_tensor(f"wide{i}", [128, 2, 512], F32)) for i in range(2)]

        up = [bank[1], wide[0][:, 0, :]]

        slots_d = nc.dram_tensor("slots", [SLOTS, RW], F32, kind="Internal").ap()
        ycomb_d = nc.dram_tensor("ycomb", [DUMP + PADS * 128, C], F32, kind="Internal").ap()

        h = sb("h", [N, B, C])
        stats = sb("stats", [N, B, 6])
        mean = sb("mean", [N, B])
        rstd = sb("rstd", [N, B])
        lns = sb("lns", [N, 4, B])
        ident = sb("ident", [128, 128])
        mask = sb("mask", [KA, HC])
        ones = sb("ones", [128, 128])
        avg128 = sb("avg128", [128, 128])
        avgN = sb("avgN", [128, 1])
        xn = sb("xn", [N, 2, 2, C])
        xT = sb("xT", [KA, 2, 2, 2, N])

        def carver(name, size):
            place, taken = sb(name, [128, size]), [0]

            def carve(shape, again=False):
                if again:
                    taken[0] = 0
                n = int(np.prod(shape[1:]))
                at = taken[0]
                taken[0] += n
                assert taken[0] <= size, (name, taken[0])
                v = place[0:shape[0], at:at + n]
                names = " ".join(f"d{i}" for i in range(1, len(shape)))
                sizes = {f"d{i}": shape[i] for i in range(2, len(shape))}
                return v.rearrange(f"p ({names}) -> p {names}", **sizes) if len(shape) > 2 else v

            return carve

        rows = carver("rows", E0 * 2 * F0 + E0 * FT * C)
        X = rows([128, B, XW])
        w1 = rows([KA, E0, 2, F0], again=True)
        w2 = rows([128, E0, FT, C])
        rowbuf = rows([N, 2, 2 * TOPK, RW], again=True)
        fill = rows([128, PADS, RW])
        early = carver("early", E1 * 2 * (2 * I1 + C))
        inner = carver("inner", 12320)

        idx = sb("idx", [NW, B], I32)
        idxc = sb("idxc", [NW, B], I32)
        idxm = sb("idxm", [N, B], I32)
        dump = sb("dump", [128, PADS])
        keep = sb("keep", [N, 2, B])
        lnwb = early([128, 2, XW])
        convb = sb("convb", [128, 12])
        projT = early([128, 3, 2, C])
        convT = early([128, 3, 2, C])
        projb = early([ROWS, C])
        pos = early([ROWS, C])
        tokb = early([ROWS, C])
        tstat = early([128, B, 6])
        tsmall = early([128, 6, B])
        xg = early([128, 2, CHUNKS, ROWS])
        tok = early([ROWS, 2, C])

        watt = early([KA, 2, 3 * C])
        wattp = early([KA, 2, C])
        qT = sb("qT", [KA, 4, 2, 2 * N])
        kS = early([N, 2, 2, 2, KA])
        vS = early([N, 2, 2, 2, KA])
        kvm = early([HC, 2, 2, 2, HC])
        ksm = early([KA, 2, 2, 2, HH])
        rden = early([N, 2 * HEADS])
        on = early([N, 2, 2, 2, HC])
        oT = sb("oT", [KA, 2, 2, 2, N])

        wg0 = early([HC, 2, E0])
        wb2 = sb("wb2", [1, E0, C])
        gm = early([HC, 2, B])
        gprod = early([HC, 2, B, E0])
        gsm = early([128, 2, B, E0])
        gone = sb("gone", [128, 5, B])
        sel = sb("sel", [1, B], I32)
        hid = early([N, 2, F0])
        hT = early([128, 2, FT, N])

        wq = inner([KA, 2, C])
        wtok = inner([KA, 2, WTOK])
        wv = inner([KA, 2, C])
        wkn = inner([HC, 2, C])
        gam = inner([N, C])
        gam2 = inner([N, 2, C])
        gcol = inner([HC, 4])
        w1b = inner([KA, 2, HC])
        w1c = inner([KA, 2, HC])
        w1m = inner([KA, HEADS])
        wp = inner([KA, 2, C])
        kA = inner([N, 2, 2, 4, KA])
        dl = inner([N, 2, 2, C + HEADS])
        sig = inner([N, 2, 2 * HEADS])
        hv = inner([N, 4 * HEADS])
        irs = inner([N, 4 * HEADS])
        hw = inner([N, 4 * HEADS])
        sm = inner([N, 2, 5, 2 * HEADS])
        tc = inner([N, 3, 2 * HEADS])
        sq = inner([N, 2 * C])
        xh = inner([N, 2 * C])
        t1 = inner([N, 2 * C])
        gg = inner([N, 2 * C])
        pp = inner([N, 2 * C])
        xs = inner([N, 2 * C])
        zz = inner([N, 2, 2 * C])
        gmk = inner([KA, 4 * HC])
        wn = inner([KA, 2, 2, 2, HC])
        zc = inner([N, 2 * C])
        zsq = inner([N, 2 * C])
        zh = inner([N, 2, 2 * C])

        m1 = early([KA, E1, 2, 2 * I1], again=True)
        m2 = early([KA, E1, 2, C])
        hot = inner([N, 2, 2 * TOPK, E1], again=True)
        taken = inner([N, 2, 2, E1])
        place = inner([N, 2 * E1])
        base = inner([128, E1])
        scale = sb("scale", [N, C])
        gate1 = sb("gate1", [KA, 2, E1])
        tri = sb("tri", [N, N])
        rr = inner([N, B])
        ts = inner([N, 2, 2, C])
        gs = inner([N, 2, 2, E1])
        m8 = inner([N, 2, 2, 8])
        i8 = sb("i8", [N, 2, 2, 8], U32)
        topf = inner([N, 2, 2 * TOPK])
        wraw = inner([N, 2, 2 * TOPK])
        wexp = inner([N, 2, 2 * TOPK])
        wsum = inner([N, 2, 2])
        rowf = inner([N, 2 * TOPK])
        iota = sb("iota", [128, E1 + 1])
        per_e = inner([128, 8, E1])
        per_ei = sb("per_ei", [128, 2, E1], I32)
        slot_s = sb("slot_s", [N, 2, 2 * TOPK], I32)
        pad_f = inner([128, E1])
        pad_at = sb("pad_at", [128, E1], I32)
        block_f = inner([128, 4])
        target = sb("target", [N, B, TOPK])
        first_row = sb("first_row", [1, BLOCKS], I32)
        experts = sb("experts", [1, BLOCKS + 4])
        etab_f = sb("etab_f", [1, BLOCKS // 4])
        etab = sb("etab", [1, BLOCKS // 4], I32)
        xb = inner([128, 4, RW])
        weight = inner([128, 4, 1])
        al = inner([128, 2, 2 * I1])
        sg = inner([128, 2, I1])
        pr = inner([128, 2, I1])
        ac = inner([128, 2, I1])
        aT = inner([KA, 2, 2, 128])
        xTm = inner([KA, 2, 2, 128])
        ys = inner([128, 2, C])
        yc = inner([N, 4, TOPK * C], again=True)
        ya = inner([N, 2 * C])
        yb = inner([N, C])
        yo = inner([N, 2, C])
        dest = sb("dest", [128, 4, 1], I32)

        block = ctx.enter_context(nc.Block())

        @block.sync
        def _(sp):
            sp.dma_start(idx[:, :], ids_d).then_inc(S["load_idx"], 16)
            sp.dma_start(idxm[:, :], idsm_d).then_inc(S["load_idx"], 16)
            sp.dma_start(dump[:, :], dump_d).then_inc(S["load_idx"], 16)
            for q in range(4):
                sp.dma_start(X[:, 8 * q:8 * q + 8, :], x_d[:, 8 * q:8 * q + 8, :]).then_inc(S["load_x"], 16)
            for dst, src in ((convb[:], convb_d), (projT, projT_d), (lnwb, lnwb_d), (projb, projb_d), (pos, pos_d)):
                sp.dma_start(dst, src).then_inc(S["load_tok"], 16)
            for dst, src in ((ident[:], ident_d), (mask[:], mask_d), (watt, att_d), (wattp, attp_d)):
                sp.dma_start(dst, src).then_inc(S["load_att"], 16)

            for dst, src in ((wq, tq_d), (wtok, tk_d), (wv, tv_d), (wkn, tkn_d), (gam, tg_d), (gcol, tgc_d), (w1b, tw_d),
                             (wp, tp_d)):
                sp.dma_start(dst, src).then_inc(S["load_ttt"], 16)

            def put(g, slot, count):
                sp.wait_ge(S["tok_sum"], g + 1)
                for j in range(count):
                    sp.dma_start(h[0:NI, bass.ds(g * GRP + j, 1), :], tok[NI * j:NI * j + NI, slot, :])\
                      .then_inc(S[f"tok_piece{slot}"], 16)

            with sp.Fori(0, 5) as turn:
                put(turn * 2, 0, GRP)
                put(turn * 2 + 1, 1, GRP)
            put(10, 0, 2)
            sp.wait_ge(S["tok_xg"], 11)
            for dst, src in ((wg0, gate0_d), (w1, f1_d), (w2, f2_d), (wb2[:], fb2_d)):
                sp.dma_start(dst, src).then_inc(S["load_ffn"], 16)
            sp.wait_ge(S["filled"], 1)
            with sp.Fori(0, SPARE // 2) as turn:
                sp.dma_start(slots_d[bass.ds(turn * 256 + E1 * CAP, 256), :].rearrange("(j p) w -> p j w", p=128),
                             fill[:, E1:PADS, :]).then_inc(S["filled"], 16)
            sp.wait_ge(S["ffn_stat"], B)
            for dst, src in ((m1, m1_d), (m2, m2_d), (scale[:], scale_d), (gate1[:], gate1_d), (tri[:], tri_d),
                             (iota[:], iota_d), (target[:], target_d)):
                sp.dma_start(dst, src).then_inc(S["load_moe"], 16)

            sp.wait_ge(S["rt_done"], 1)
            sp.wait_ge(S["dispatched0"], 16 * 2 * TOPK * PAIRS // 2)
            sp.wait_ge(S["dispatched1"], 16 * 2 * TOPK * PAIRS // 2)
            sp.wait_ge(S["padded"], 16 * E1)
            sp.wait_ge(S["filled"], 1 + 16 * (SPARE // 2))

            def load_block(turn, j):
                n, slot, _ = at(turn, j)
                when(sp, S["moe_al"], n - 3)
                row = sp.value_load(first_row[0:1, bass.ds(n, 1)])
                sp.dma_start(xb[:, slot, :], slots_d[bass.ds(row, 128), :]).then_inc(S[f"loaded{slot}"], 16)

            over_blocks(sp, load_block)

            sp.wait_ge(S["moe_out0"], 16 * BLOCKS // 2)
            sp.wait_ge(S["moe_out1"], 16 * BLOCKS // 2)

            def load_choices(turn, j):
                b, slot, _ = at(turn, j)
                when(sp, S["fin_a"], b - 3)
                sp.dma_start(yc[:, slot, :], ycomb_d[bass.ds(b * (N * TOPK), N * TOPK), :].rearrange("(p k) c -> p (k c)", k=TOPK))\
                  .then_inc(S[f"loaded{slot}"], 16)

            over_images(sp, load_choices)
            sp.wait_ge(S["stored0"], 16 * B // 2)
            sp.wait_ge(S["stored1"], 16 * B // 2)

        @block.gpsimd
        def _(pool):
            pool.wait_ge(S["clipped"], 1)
            for b in range(B):
                nc.gpsimd.indirect_dma_start(
                    out=h[NI:N, b, :], out_offset=None, in_=table_d,
                    in_offset=bass.IndirectOffsetOnAxis(ap=idxc[:, b:b + 1], axis=0)).then_inc(S["gathered"], 16)
            G = nc.gpsimd

            def heads(v):
                return v.rearrange("p (a d) -> p a d", d=HD)

            def per_head(v):
                return v.rearrange("p (a d) -> p a d", d=1).broadcast_to([N, 2 * HEADS, HD])

            def ttt(t, slot):
                s_ = sm[:, slot % 2]
                step = S["pool_inner"]
                pool.wait_ge(S["ttt_sig"], t + 1)
                pool.wait_ge(S["ttt_rstd"], t + 1)
                G.tensor_tensor(s_[:, 2, :], irs[:, 0:2 * HEADS], tc[:, 1, :], ALU.mult).then_inc(step, 1)
                pool.wait_ge(step, 3 * t + 1)
                G.tensor_tensor(s_[:, 2, :], s_[:, 2, :], sig[:, slot % 2, :], ALU.mult).then_inc(S["ttt_r"], 1)
                pool.wait_ge(S["ttt_xh"], t + 1)
                G.tensor_tensor(t1[:, :], xh[:, :], gam2[:, :, :].rearrange("p i c -> p (i c)"), ALU.mult)\
                 .then_inc(S["ttt_t1"], 1)
                pool.wait_ge(S["ttt_s"], t + 1)
                pool.wait_ge(S["ttt_r"], t + 1)
                G.tensor_tensor(s_[:, 3, :], s_[:, 3, :], tc[:, 2, :], ALU.mult).then_inc(step, 1)
                pool.wait_ge(step, 3 * t + 2)
                G.tensor_tensor(s_[:, 3, :], s_[:, 3, :], s_[:, 2, :], ALU.mult).then_inc(step, 1)
                pool.wait_ge(step, 3 * t + 3)
                when(pool, S["ttt_zz"], t)
                G.tensor_tensor(heads(xs[:, :]), heads(xh[:, :]), per_head(s_[:, 3, :]), ALU.mult)\
                 .then_inc(S["ttt_xs"], 1)

            over_pairs(pool, ttt, 4)

            def dispatch(turn, j):
                t, slot, _ = at_two(turn, j)
                pool.wait_ge(S["row_t"], t + 1)
                pool.wait_ge(S["row_meta"], t + 1)
                pool.sem_inc(S["going"], 1)
                for k in range(2 * TOPK):
                    G.indirect_dma_start(
                        out=slots_d, out_offset=bass.IndirectOffsetOnAxis(ap=slot_s[:, slot, k:k + 1], axis=0),
                        in_=rowbuf[:, slot, k, :], in_offset=None).then_inc(S[f"dispatched{slot}"], 16)

            over_twos(pool, dispatch, PAIRS)
            pool.wait_ge(S["pad_ready"], 1)
            for e in range(E1):
                G.indirect_dma_start(
                    out=slots_d, out_offset=bass.IndirectOffsetOnAxis(ap=pad_at[:, e:e + 1], axis=0),
                    in_=fill[:, e, :], in_offset=None).then_inc(S["padded"], 16)

            def send_back(turn, j):
                n, slot, _ = at(turn, j)
                pool.wait_ge(S["moe_ys"], n + 1)
                pool.sem_inc(S["going"], 1)
                G.indirect_dma_start(
                    out=ycomb_d, out_offset=bass.IndirectOffsetOnAxis(ap=dest[:, slot, :], axis=0),
                    in_=ys[:, slot % 2, :], in_offset=None).then_inc(S[f"moe_out{slot % 2}"], 16)

            def moe(turn, j):
                n, slot, _ = at(turn, j)
                pool.wait_ge(S["moe_p"], n + 1)
                pool.wait_ge(S["moe_sig"], n + 1)
                when(pool, S["moe_aT"], n - 1)
                G.tensor_tensor(ac[:, slot % 2, :], pr[:, slot % 2, :], sg[:, slot % 2, :], ALU.mult)\
                 .then_inc(S["moe_act"], 1)
                if not (first(turn) and j < 2):
                    send_back(turn, j - 2)

            over_blocks(pool, moe)
            send_back(BLOCKS // 4 - 1, 2)
            send_back(BLOCKS // 4 - 1, 3)


        @block.scalar
        def _(act):
            act.wait_ge(S["const_ready"], 1)
            act.wait_ge(S["load_att"], 64)

            def attention(t, slot):
                act.wait_ge(S["att_xT"], t + 1)
                when(act, S["att_q"], t - 1)
                nc.scalar.copy(xT[0:HC, slot].rearrange("p h i n -> p (h i n)"), bank[0][0:HC, 0:4 * N])\
                    .then_inc(S["att_xTs"], 1)
                act.wait_ge(S["att_ks"], t + 1)
                when(act, S["att_prod"], t - 1)
                nc.scalar.copy(vS[:, slot, :, :, 0:HC].rearrange("p i h c -> p i h c"),
                               wide[0][0:N, :, C:2 * C].rearrange("p i (h c) -> p i h c", h=2))\
                    .then_inc(S["att_vs"], 1)

                if not first(t):
                    att_oT(t - 1, 1 - slot)

            def att_oT(t, slot):
                act.wait_ge(S["att_oTp"], t + 1)
                when(act, S["att_out"], t - 1)
                nc.scalar.copy(oT[0:HC, slot].rearrange("p h i n -> p (h i n)"), wide[1][0:HC, 1, 0:4 * N])\
                    .then_inc(S["att_oT"], 1)

            over_pairs(act, attention)
            att_oT(PAIRS - 1, 1)

            act.wait_ge(S["gate0_step"], 1)
            nc.scalar.activation(gsm[:, 1].rearrange("p b e -> p (b e)"), gsm[:, 0].rearrange("p b e -> p (b e)"),
                                 ACT.Exp).then_inc(S["gate0_exp"], 1)

            def ffn_xT(t, slot):
                act.wait_ge(S["ffn_xT"], t + 1)
                when(act, S["ffn_hid"], 2 * t - 2)
                nc.scalar.copy(xT[0:HC, slot].rearrange("p h i n -> p (h i n)"), bank[0][0:HC, 0:4 * N])\
                    .then_inc(S["ffn_xTs"], 1)

            def ffn_hT(u, i):
                act.wait_ge(S["ffn_hT"], u + 1)
                when(act, S["ffn_y"], u - 1)
                nc.scalar.copy(hT[:, i, 3:6, :], bank[2][:, 0:3 * N].rearrange("p (k n) -> p k n", k=3))\
                    .then_inc(S["ffn_hTa"], 1)

            def ffn(t, slot):
                for i in range(2):
                    u = t * 2 + i
                    if not first(u):
                        ffn_hT(u - 1, 1 - i)
                    act.wait_ge(S["ffn_hid"], u + 1)
                    when(act, S["ffn_hT"], u - 1)
                    for n in range(2):
                        ins = nc.scalar.activation(hid[:, i, 384 * n:384 * n + 384], wide[i][0:N, n, 0:384], ACT.Gelu)
                    ins.then_inc(S["ffn_gelu"], 1)
                    if i == 0 and not (isinstance(t, int) and t == PAIRS - 1):
                        ffn_xT(t + 1, 1 - slot)

            ffn_xT(0, 0)
            over_pairs(act, ffn)
            ffn_hT(B - 1, 1)

            def ttt_xT(t, slot):
                act.wait_ge(S["ttt_xT"], t + 1)
                when(act, S["ttt_tok"], t - 1)
                nc.scalar.copy(xT[0:HC, slot % 2].rearrange("p h i n -> p (h i n)"), bank[0][0:HC, 0:4 * N])\
                    .then_inc(S["ttt_xTs"], 1)

            def ttt_q(t, slot):
                act.wait_ge(S["ttt_q"], t + 1)
                when(act, S["ttt_oT"], t - 3)
                nc.scalar.copy(qT[0:HC, slot % 4].rearrange("p h n -> p (h n)"), bank[1][0:HC, 0:4 * N])\
                    .then_inc(S["ttt_qs"], 1)

            def ttt_tok(t, slot):
                act.wait_ge(S["ttt_tok"], t + 1)
                when(act, S["ttt_grad"], t - 1)
                when(act, S["ttt_xh"], t - 1)
                when(act, S["ttt_sq"], t - 1)
                nc.scalar.copy(kA[:, slot % 2, :, :, 0:HC], wide[0][0:N, :, 0:2 * C].rearrange("p i (a c) -> p i a c", a=4))\
                    .then_inc(S["ttt_kA"], 1)
                when(act, S["ttt_g"], t - 1)
                when(act, S["ttt_sig"], t - 1)
                nc.scalar.copy(dl[:, slot % 2], bank[3][0:N, 0:2 * (C + HEADS)].rearrange("p (i c) -> p i c", i=2))\
                    .then_inc(S["ttt_dl"], 1)
                act.wait_ge(S["ttt_kA"], t + 1)
                when(act, S["ttt_v"], t)
                nc.scalar.activation(sq[:, :].rearrange("p (i a c) -> p i a c", i=2, a=2), kA[:, slot % 2, :, 2:4, 0:HC],
                                     ACT.Square, scale=HD ** -0.5)\
                    .then_inc(S["ttt_sq"], 1)
                act.wait_ge(S["ttt_dl"], t + 1)
                when(act, S["ttt_r"], t - 1)
                nc.scalar.activation(sig[:, slot % 2, :].rearrange("p (i a) -> p i a", i=2),
                                     dl[:, slot % 2, :, C:C + HEADS], ACT.Sigmoid).then_inc(S["ttt_sig"], 1)

            def ttt_zsq(t):
                act.wait_ge(S["ttt_zc"], t + 1)
                when(act, S["ttt_zv"], t)
                nc.scalar.activation(zsq[:, :], zc[:, :], ACT.Square, scale=HD ** -0.5).then_inc(S["ttt_zsq"], 1)

            def ttt(t, slot):
                fixed = isinstance(t, int)
                if not (fixed and t >= PAIRS - 2):
                    ttt_xT(t + 2, slot + 2)
                if not (fixed and t == 0):
                    ttt_zsq(t - 1)
                if not (fixed and t == PAIRS - 1):
                    ttt_q(t + 1, slot + 1)
                if not (fixed and t == PAIRS - 1):
                    ttt_tok(t + 1, slot + 1)

            ttt_xT(0, 0)
            ttt_q(0, 0)
            ttt_tok(0, 0)
            ttt_xT(1, 1)
            over_pairs(act, ttt, 4)
            ttt_zsq(PAIRS - 1)

            def rt_copy(turn, j):
                t, slot, _ = at_two(turn, j)
                act.wait_ge(S["rt_tT"], t + 1)
                when(act, S["rt_logit"], t - 1)
                nc.scalar.copy(xT[0:HC, slot].rearrange("p h i n -> p (h i n)"), bank[0][0:HC, 0:4 * N])\
                    .then_inc(S["rt_tTs"], 1)

            def rt_exp(turn, j):
                t, slot, _ = at_two(turn, j)
                act.wait_ge(S["rt_less"], t + 1)
                when(act, S["row_meta"], t - 1)
                nc.scalar.activation(wexp[:, slot, :], wraw[:, slot, :], ACT.Exp).then_inc(S["rt_exp"], 1)

            def rt_rows(turn, j):
                t, slot, half = at_two(turn, j)
                when(act, S[f"dispatched{slot}"], 16 * 2 * TOPK * half)
                for i in range(2):
                    ins = nc.scalar.copy(rowbuf[:, slot, TOPK * i:TOPK * (i + 1), 0:C],
                                         ts[:, slot, i:i + 1, :].broadcast_to([N, TOPK, C]))
                ins.then_inc(S["row_t"], 1)

            def route(turn, j):
                if not (last(turn, PAIRS // 2) and j == 1):
                    rt_copy(turn, j + 1)
                rt_exp(turn, j)
                rt_rows(turn, j)

            rt_copy(0, 0)
            over_twos(act, route, PAIRS)

            def moe_xTs(turn, j):
                n, slot, _ = at(turn, j)
                act.wait_ge(S["moe_xT"], n + 1)
                when(act, S["moe_h"], n - 1)
                nc.scalar.copy(xTm[0:HC, slot % 2].rearrange("p h n -> p (h n)"), bank[0][0:HC, 0:256])\
                    .then_inc(S["moe_xTs"], 1)

            def moe_sigmoid(turn, j):
                n, slot, _ = at(turn, j)
                act.wait_ge(S["moe_al"], n + 1)
                when(act, S["moe_act"], n - 1)
                nc.scalar.activation(sg[:, slot % 2, :], al[:, slot % 2, 0:I1], ACT.Sigmoid, scale=ALPHA)\
                    .then_inc(S["moe_sig"], 1)

            def moe_aTs(turn, j):
                n, slot, _ = at(turn, j)
                act.wait_ge(S["moe_aT"], n + 1)
                when(act, S["moe_y"], n - 1)
                nc.scalar.copy(aT[0:HC, slot % 2].rearrange("p h n -> p (h n)"), bank[2][0:HC, 0:256])\
                    .then_inc(S["moe_aTs"], 1)

            def moe(turn, j):
                if not (last(turn, BLOCKS // 4) and j == 3):
                    moe_xTs(turn, j + 1)
                moe_sigmoid(turn, j)
                if not (first(turn) and j == 0):
                    moe_aTs(turn, j - 1)

            moe_xTs(0, 0)
            over_blocks(act, moe)
            moe_aTs(BLOCKS // 4 - 1, 3)

            def store(turn, j):
                b, slot, _ = at(turn, j)
                act.wait_ge(S["fin_c"], b + 1)
                act.dma_start(out_d[bass.ds(b, 1), :, :].rearrange("a n c -> n (a c)"), yo[:, slot % 2, :])\
                   .then_inc(S[f"stored{slot % 2}"], 16)

            over_images(act, store)

        @block.tensor
        def _(pe):
            pe.wait_ge(S["const_ready"], 1)
            pe.wait_ge(S["tok_stat"], 1)
            pe.matmul(bank[0][:, 0:B], avg128[:, :], tsmall[:, 0, :], start=True, stop=True).then_inc(S["tok_mean"], 1)
            pe.wait_ge(S["tok_varsum"], 1)
            pe.matmul(bank[1][:, 0:B], avg128[:, :], tsmall[:, 3, :], start=True, stop=True).then_inc(S["tok_devavg"], 1)
            pe.wait_ge(S["tok_w"], 1)
            for k in range(CHUNKS):
                pe.matmul(bank[2][0:ROWS, 0:C], xg[:, 1, k, :], convT[:, k // 2, k % 2, :],
                          start=(k == 0), stop=False)
            for k in range(CHUNKS):
                ins = pe.matmul(bank[2][0:ROWS, 0:C], xg[:, 0, k, :], projT[:, k // 2, k % 2, :],
                                start=False, stop=(k == CHUNKS - 1))
            ins.then_inc(S["tok_bias_mm"], 1)

            def patches(g, slot, count):
                pe.wait_ge(S["tok_xg"], g + 1)
                when(pe, S["tok_sum"], g - 1)
                for k in range(CHUNKS):
                    ins = pe.matmul(bank[slot][0:NI * count, 0:C], xg[:, slot, k, 0:NI * count],
                                    convT[:, k // 2, k % 2, :], start=(k == 0), stop=(k == CHUNKS - 1))
                ins.then_inc(S["tok_mm"], 1)

            patches(0, 0, GRP)
            patches(1, 1, GRP)
            with pe.Fori(1, 5) as turn:
                patches(turn * 2, 0, GRP)
                patches(turn * 2 + 1, 1, GRP)
            patches(10, 0, 2)

            def turn_rows(slot, xn_ready, count, psum_free, n_free, done):
                pe.wait_ge(xn_ready, count)
                when(pe, psum_free, n_free)
                for i in range(2):
                    for k in range(2):
                        ins = pe.transpose(bank[0][0:HC, (2 * k + i) * N:(2 * k + i + 1) * N],
                                           xn[:, slot, i, k * HC:k * HC + HC], ident[0:N, 0:N])
                ins.then_inc(done, 1)

            pe.wait_ge(S["load_att"], 64)
            pe.wait_ge(S["tok_sum"], 11)

            def att_turn(t, slot):
                turn_rows(slot, S["att_xn"], t + 1, S["att_xTs"], t, S["att_xT"])

            def att_weights(t, slot):
                pe.wait_ge(S["att_xTs"], t + 1)
                when(pe, S["att_ks"], t)
                when(pe, S["att_vs"], t)
                for i in range(2):
                    for k in range(2):
                        ins = pe.matmul(wide[0][0:N, i, 0:2 * C], xT[0:HC, slot, k, i, :], watt[0:HC, k, C:3 * C],
                                        start=(k == 0), stop=(k == 1))
                ins.then_inc(S["att_kv"], 1)
                when(pe, S["att_qs"], t)
                for m in range(2):
                    for k in range(2):
                        ins = pe.matmul(bank[1][0:HC, m * 2 * N:(m + 1) * 2 * N], watt[0:HC, k, m * HC:m * HC + HC],
                                        xT[0:HC, slot, k].rearrange("p i n -> p (i n)"), start=(k == 0), stop=(k == 1))
                ins.then_inc(S["att_q"], 1)

            def att_product(t, slot):
                pe.wait_ge(S["att_ks"], t + 1)
                pe.wait_ge(S["att_vs"], t + 1)
                when(pe, S["att_ksm"], t)
                for i in range(2):
                    for k in range(2):
                        ins = pe.matmul(bank[2][0:HC, (2 * i + k) * KA:(2 * i + k + 1) * KA], kS[:, slot, i, k, 0:HC],
                                        vS[:, slot, i, k, :], start=True, stop=True)
                ins.then_inc(S["att_prod"], 1)

            def att_fraction(t, slot):
                pe.wait_ge(S["att_qs"], t + 1)
                pe.wait_ge(S["att_ksm"], t + 1)
                when(pe, S["att_on"], t)
                for i in range(2):
                    for k in range(2):
                        q = qT[:, slot, k, i * N:i * N + N]
                        a = 2 * i + k
                        pe.matmul(wide[1][0:N, 0, a * HC:a * HC + HC], q[0:HC], kvm[:, slot, i, k, :],
                                  start=True, stop=True)
                        ins = pe.matmul(wide[1][0:N, 0, 2 * C + a * HH:2 * C + a * HH + HH], q, ksm[:, slot, i, k, :],
                                        start=True, stop=True)
                ins.then_inc(S["att_frac"], 1)

            def att_turn_back(t, slot):
                pe.wait_ge(S["att_on"], t + 1)
                when(pe, S["att_oT"], t)
                for k in range(2):
                    for i in range(2):
                        ins = pe.transpose(wide[1][0:HC, 1, (2 * k + i) * N:(2 * k + i + 1) * N], on[:, slot, i, k, :],
                                           ident[0:N, 0:N])
                ins.then_inc(S["att_oTp"], 1)

            def att_project(t, slot):
                pe.wait_ge(S["att_oT"], t + 1)
                when(pe, S["att_h"], t)
                for i in range(2):
                    for k in range(2):
                        rows = KA if k == 0 else HC
                        ins = pe.matmul(bank[3][0:N, i * C:i * C + C], oT[0:rows, slot, k, i, :], wattp[0:rows, k, :],
                                        start=(k == 0), stop=(k == 1))
                ins.then_inc(S["att_out"], 1)

            def attention(t, slot):
                att_weights(t, slot)
                first = isinstance(t, int) and t == 0
                if not first:
                    att_fraction(t - 1, 1 - slot)
                if not last(t, PAIRS):
                    att_turn(t + 1, 1 - slot)
                att_product(t, slot)
                if not first:
                    att_turn_back(t - 1, 1 - slot)
                    att_project(t - 1, 1 - slot)

            att_turn(0, 0)
            over_pairs(pe, attention)
            att_fraction(PAIRS - 1, 1)
            att_turn_back(PAIRS - 1, 1)
            att_project(PAIRS - 1, 1)

            pe.wait_ge(S["att_h"], PAIRS)
            pe.wait_ge(S["att_qs"], PAIRS)

            def gate0(t, slot):
                pe.wait_ge(S["gate0_xn"], t + 1)
                for i in range(2):
                    for k in range(2):
                        ins = pe.matmul(bank[1][0:HC, bass.ds(t * 2 + (i + B * k), 1)],
                                        xn[:, slot, i, k * HC:k * HC + HC], avgN[0:N, :], start=True, stop=True)
                ins.then_inc(S["gate0_mean"], 1)

            over_pairs(pe, gate0)
            pe.wait_ge(S["gate0_prod"], 1)
            for k in range(2):
                ins = pe.matmul(bank[2][:, 0:B * E0], ones[0:HC, :], gprod[:, k].rearrange("p b e -> p (b e)"),
                                start=(k == 0), stop=(k == 1))
            ins.then_inc(S["gate0_logit"], 1)

            pe.wait_ge(S["load_ffn"], 64)
            pe.wait_ge(S["gate0_ready"], 1)

            def ffn_turn(t, slot):
                turn_rows(slot, S["ffn_xn"], t + 1, S["ffn_xTs"], t, S["ffn_xT"])

            def ffn_up(slot, i, n, e):
                for k in range(2):
                    rows = KA if k == 0 else HC
                    ins = pe.matmul(wide[i][0:N, n, 0:384], xT[0:rows, slot, k, i, :],
                                    w1[0:rows, bass.ds(e, 1), k, 384 * n:384 * n + 384], start=(k == 0), stop=(k == 1))
                return ins

            def ffn_transpose(u, i):
                pe.wait_ge(S["ffn_gelu"], u + 1)
                when(pe, S["ffn_hTv"], u)
                when(pe, S["ffn_hTa"], u)
                for k in range(FT):
                    ins = pe.transpose(bank[1 + k // 3][:, (k % 3) * N:(k % 3 + 1) * N], hid[:, i, 128 * k:128 * k + 128],
                                       ident[0:N, 0:N])
                ins.then_inc(S["ffn_hT"], 1)

            def ffn_down(u, i, e):
                pe.wait_ge(S["ffn_hTv"], u + 1)
                pe.wait_ge(S["ffn_hTa"], u + 1)
                when(pe, S["ffn_h"], u)
                for k in range(FT):
                    pe.matmul(bank[3][0:N, i * 256:i * 256 + C], hT[:, i, k, :], w2[:, bass.ds(e, 1), k, :],
                              start=(k == 0), stop=False)
                pe.matmul(bank[3][0:N, i * 256:i * 256 + C], ones[0:1, 0:N], wb2[0:1, bass.ds(e, 1), :],
                          start=False, stop=True).then_inc(S["ffn_y"], 1)

            def ffn(t, slot):
                pe.wait_ge(S["ffn_xTs"], t + 1)
                for i in range(2):
                    u = t * 2 + i
                    lag = not (isinstance(u, int) and u == 0)
                    e = pe.value_load(sel[0:1, bass.ds(u, 1)])
                    when(pe, S["ffn_gelu"], u - 1)
                    ffn_up(slot, i, 0, e)
                    if lag:
                        ffn_transpose(u - 1, 1 - i)
                    ffn_up(slot, i, 1, e).then_inc(S["ffn_hid"], 1)
                    if lag:
                        ffn_down(u - 1, 1 - i, pe.value_load(sel[0:1, bass.ds(u - 1, 1)]))
                    if i == 0 and not (isinstance(t, int) and t == PAIRS - 1):
                        ffn_turn(t + 1, 1 - slot)

            ffn_turn(0, 0)
            over_pairs(pe, ffn)
            ffn_transpose(B - 1, 1)
            ffn_down(B - 1, 1, pe.value_load(sel[0:1, B - 1:B]))

            pe.wait_ge(S["load_ttt"], 128)
            pe.wait_ge(S["tw_cent"], 1)
            for k in range(2):
                for m in range(2):
                    pe.matmul(bank[1][0:HC, (2 * k + m) * HC:(2 * k + m + 1) * HC], wkn[:, m, k * HC:k * HC + HC],
                              w1c[0:HC, m, :], start=True, stop=True)
            for k in range(2):
                ins = pe.matmul(bank[2][HC:KA, 0:C], gcol[:, 2 + k:3 + k], wp[0:HC, k, :], start=(k == 0), stop=(k == 1))
            ins.then_inc(S["tw_comp"], 1)
            pe.wait_ge(S["tw_done"], 1)

            def ttt_turn(t, slot):
                pe.wait_ge(S["ttt_xn"], t + 1)
                when(pe, S["ttt_oT"], t - 3)
                if isinstance(t, int):
                    when(pe, S["ttt_xTs"], t)
                for i in range(2):
                    for k in range(2):
                        ins = pe.transpose(bank[0][0:HC, (2 * k + i) * N:(2 * k + i + 1) * N],
                                           xn[:, slot % 2, i, k * HC:k * HC + HC], ident[0:N, 0:N])
                ins.then_inc(S["ttt_xT"], 1)

            def ttt_query(t, slot):
                pe.wait_ge(S["ttt_xTs"], t + 1)
                when(pe, S["ttt_qs"], t)
                for m in range(2):
                    for k in range(2):
                        rows = KA if k == 0 else HC
                        ins = pe.matmul(bank[1][0:HC, m * 2 * N:(m + 1) * 2 * N], wq[0:rows, k, m * HC:m * HC + HC],
                                        xT[0:rows, slot % 2, k].rearrange("p i n -> p (i n)"),
                                        start=(k == 0), stop=(k == 1))
                ins.then_inc(S["ttt_q"], 1)

            def ttt_token(t, slot):
                when(pe, S["ttt_kA"], t)
                when(pe, S["ttt_dl"], t)
                for i in range(2):
                    for k in range(2):
                        rows = KA if k == 0 else HC
                        x_ = xT[0:rows, slot % 2, k, i, :]
                        pe.matmul(wide[0][0:N, i, 0:2 * C], x_, wtok[0:rows, k, 0:2 * C], start=(k == 0), stop=(k == 1))
                    for k in range(2):
                        rows = KA if k == 0 else HC
                        x_ = xT[0:rows, slot % 2, k, i, :]
                        ins = pe.matmul(bank[3][0:N, i * (C + HEADS):(i + 1) * (C + HEADS)], x_, wtok[0:rows, k, 2 * C:WTOK],
                                        start=(k == 0), stop=(k == 1))
                ins.then_inc(S["ttt_tok"], 1)

            def ttt_grad(t, slot):
                pe.wait_ge(S["ttt_zz"], t + 1)
                when(pe, S["ttt_gm"], t)
                for i in range(2):
                    for k in range(2):
                        a = 2 * i + k
                        ins = pe.matmul(bank[2][0:KA, a * HC:a * HC + HC], kA[:, slot % 2, i, k, :],
                                        zz[:, slot % 2, a * HC:a * HC + HC], start=True, stop=True)
                ins.then_inc(S["ttt_grad"], 1)

            def ttt_updated(t, slot):
                pe.wait_ge(S["ttt_w"], t + 1)
                pe.wait_ge(S["ttt_qs"], t + 1)
                when(pe, S["ttt_zc"], t)
                for i in range(2):
                    for k in range(2):
                        a = 2 * i + k
                        ins = pe.matmul(wide[1][0:N, 0, a * HC:a * HC + HC], qT[:, slot % 4, k, i * N:i * N + N],
                                        wn[:, slot % 2, i, k, :], start=True, stop=True)
                ins.then_inc(S["ttt_zb"], 1)

            def ttt_turn_back(t, slot):
                pe.wait_ge(S["ttt_zh"], t + 1)
                pe.wait_ge(S["ttt_xTs"], min(t + 4, PAIRS) if isinstance(t, int) else t + 4)
                for i in range(2):
                    for k in range(2):
                        a = 2 * i + k
                        ins = pe.transpose(bank[0][0:HC, (2 * k + i) * N:(2 * k + i + 1) * N],
                                           zh[:, slot % 2, a * HC:a * HC + HC], ident[0:N, 0:N])
                ins.then_inc(S["ttt_zT"], 1)

            def ttt_project(t, slot):
                pe.wait_ge(S["ttt_oT"], t + 1)
                when(pe, S["ttt_h"], t)
                for i in range(2):
                    for k in range(2):
                        rows = KA if k == 0 else HC
                        ins = pe.matmul(wide[1][0:N, 1, i * C:i * C + C], oT[0:rows, slot % 2, k, i, :], wp[0:rows, k, :],
                                        start=(k == 0), stop=(k == 1))
                ins.then_inc(S["ttt_out"], 1)

            def ttt(t, slot):
                fixed = isinstance(t, int)
                before, after = not (fixed and t == 0), not (fixed and t == PAIRS - 1)
                if before:
                    ttt_grad(t - 1, slot - 1)
                if not (fixed and t >= PAIRS - 2):
                    ttt_turn(t + 2, slot + 2)
                if before:
                    ttt_updated(t - 1, slot - 1)
                if after:
                    ttt_query(t + 1, slot + 1)
                    ttt_token(t + 1, slot + 1)
                if before:
                    ttt_turn_back(t - 1, slot - 1)
                    ttt_project(t - 1, slot - 1)

            ttt_turn(0, 0)
            ttt_query(0, 0)
            ttt_token(0, 0)
            ttt_turn(1, 1)
            over_pairs(pe, ttt, 4)
            ttt_grad(PAIRS - 1, 3)
            ttt_updated(PAIRS - 1, 3)
            ttt_turn_back(PAIRS - 1, 3)
            ttt_project(PAIRS - 1, 3)

            pe.wait_ge(S["load_moe"], 112)
            pe.wait_ge(S["ttt_oT"], PAIRS)

            def rt_turn(turn, j):
                t, slot, _ = at_two(turn, j)
                pe.wait_ge(S["rt_t"], t + 1)
                when(pe, S["rt_tTs"], t)
                for i in range(2):
                    for k in range(2):
                        ins = pe.transpose(bank[0][0:HC, (2 * k + i) * N:(2 * k + i + 1) * N],
                                           ts[:, slot, i, k * HC:k * HC + HC], ident[0:N, 0:N])
                ins.then_inc(S["rt_tT"], 1)

            def rt_logits(turn, j):
                t, slot, _ = at_two(turn, j)
                pe.wait_ge(S["rt_tTs"], t + 1)
                when(pe, S["rt_gs"], t)
                for i in range(2):
                    for k in range(2):
                        nrow = KA if k == 0 else HC
                        ins = pe.matmul(bank[1][0:N, i * E1:i * E1 + E1], xT[0:nrow, slot, k, i, :], gate1[0:nrow, k, :],
                                        start=(k == 0), stop=(k == 1))
                ins.then_inc(S["rt_logit"], 1)

            def rt_count(turn, j):
                t, slot, _ = at_two(turn, j)
                pe.wait_ge(S["rt_taken"], t + 1)
                when(pe, S["rt_base"], t)
                a, b = taken[:, slot, 0, :], taken[:, slot, 1, :]
                pe.matmul(bank[2][0:N, 0:E1], tri[:, :], a, start=True, stop=True)
                pe.matmul(bank[2][0:N, E1:2 * E1], tri[:, :], b, start=True, stop=False)
                pe.matmul(bank[2][0:N, E1:2 * E1], ones[0:N, 0:N], a, start=False, stop=True)
                pe.matmul(bank[2][:, 2 * E1:3 * E1], ones[0:N, :], a, start=True, stop=False)
                pe.matmul(bank[2][:, 2 * E1:3 * E1], ones[0:N, :], b, start=False, stop=True).then_inc(S["rt_count"], 1)

            def route(turn, j):
                if not (last(turn, PAIRS // 2) and j == 1):
                    rt_turn(turn, j + 1)
                rt_logits(turn, j)
                rt_count(turn, j)

            rt_turn(0, 0)
            over_twos(pe, route, PAIRS)
            pe.wait_ge(S["rt_blocks"], 1)
            for k in range(2):
                ins = pe.matmul(bank[3][0:1, k * BLOCKS:(k + 1) * BLOCKS], block_f[:, k:k + 1], ident[:, :],
                                start=True, stop=True)
            ins.then_inc(S["rt_row"], 1)

            def moe_turn(turn, j):
                n, slot, _ = at(turn, j)
                pe.wait_ge(S[f"loaded{slot}"], 16 * (turn + j // 4 + 1))
                when(pe, S["moe_xTs"], n)
                for k in range(2):
                    ins = pe.transpose(bank[0][0:HC, k * 128:k * 128 + 128], xb[:, slot, k * HC:k * HC + HC], ident[:, :])
                ins.then_inc(S["moe_xT"], 1)

            def moe_up(turn, j, e):
                n, slot, _ = at(turn, j)
                pe.wait_ge(S["moe_xTs"], n + 1)
                when(pe, S["moe_al"], n - 1)
                for k in range(2):
                    nrow = KA if k == 0 else HC
                    ins = pe.matmul(up[slot % 2][:, 0:2 * I1], xTm[0:nrow, slot % 2, k, :], m1[0:nrow, bass.ds(e, 1), k, :],
                                    start=(k == 0), stop=(k == 1))
                ins.then_inc(S["moe_h"], 1)

            def moe_turn_back(turn, j):
                n, slot, _ = at(turn, j)
                pe.wait_ge(S["moe_act"], n + 1)
                when(pe, S["moe_aTs"], n)
                for k in range(2):
                    ins = pe.transpose(bank[2][0:HC, k * 128:k * 128 + 128], ac[:, slot % 2, k * HC:k * HC + HC],
                                       ident[:, :])
                ins.then_inc(S["moe_aT"], 1)

            def moe_down(turn, j, e):
                n, slot, _ = at(turn, j)
                pe.wait_ge(S["moe_aTs"], n + 1)
                when(pe, S["moe_ys"], n)
                for k in range(2):
                    nrow = KA if k == 0 else HC
                    ins = pe.matmul(bank[3][:, 0:C], aT[0:nrow, slot % 2, k, :], m2[0:nrow, bass.ds(e, 1), k, :],
                                    start=(k == 0), stop=(k == 1))
                ins.then_inc(S["moe_y"], 1)

            def moe(turn, j):
                if j == 0:
                    word = pe.value_load(etab[0:1, bass.ds(turn, 1)])
                    for i in range(-2, 4):
                        expert[i] = (word // E1 ** (i + 2)) % E1
                moe_up(turn, j, expert[j])
                if not (last(turn, BLOCKS // 4) and j == 3):
                    moe_turn(turn, j + 1)
                if not (first(turn) and j == 0):
                    moe_turn_back(turn, j - 1)
                if not (first(turn) and j < 2):
                    moe_down(turn, j - 2, expert[j - 2])

            expert = {}
            pe.wait_ge(S["rt_done"], 1)
            moe_turn(0, 0)
            over_blocks(pe, moe)
            moe_turn_back(BLOCKS // 4 - 1, 3)
            moe_down(BLOCKS // 4 - 1, 2, expert[2])
            moe_down(BLOCKS // 4 - 1, 3, expert[3])

        @block.vector
        def _(dve):
            V = nc.vector
            chained = [0]

            def link(ins):
                chained[0] += 1
                ins.then_inc(S["dve_chain"], 1)
                dve.wait_ge(S["dve_chain"], chained[0])

            def rsqrt(y, v, w, then):
                then(V.tensor_scalar(y.bitcast(I32), v.bitcast(I32), -0.5, float(0x5F3759DF), ALU.mult, ALU.add))
                for i in range(3):
                    then(V.scalar_tensor_tensor(out=w, in0=y, scalar=-0.5, in1=y, op0=ALU.mult, op1=ALU.mult))
                    then(V.tensor_tensor(w, w, v, ALU.mult))
                    last_one = V.scalar_tensor_tensor(out=y, in0=w, scalar=1.5, in1=y, op0=ALU.add, op1=ALU.mult)
                    if i < 2:
                        then(last_one)
                return last_one

            V.memset(ones[:, :], 1.0)
            V.memset(avg128[:, :], 1.0 / 128)
            V.memset(avgN[:, :], 1.0 / N)
            V.memset(xT[HC:KA, :, :, :, :], 1.0)
            V.memset(qT[HC:KA, :, :, :], 1.0)
            V.memset(oT[HC:KA, :, :, :, :], 1.0)
            V.memset(kS[:, :, :, :, HC:KA], 1.0)
            V.memset(vS[:, :, :, :, HC:KA], 1.0)
            V.memset(ksm[HC:KA, :, :, :, :], TTT_EPS).then_inc(S["const_ready"], 1)
            dve.wait_ge(S["load_idx"], 48)
            V.tensor_scalar(idxc[:, :], idx[:, :], 0, VOCAB - 1, ALU.max, ALU.min).then_inc(S["clipped"], 1)
            V.tensor_scalar(keep[:, 0, :], idxm[:, :], 0, None, ALU.is_ge).then_inc(S["mask_lo"], 1)
            V.tensor_scalar(keep[:, 1, :], idxm[:, :], VOCAB - 1, None, ALU.is_le).then_inc(S["mask_hi"], 1)
            dve.wait_ge(S["mask_lo"], 1)
            dve.wait_ge(S["mask_hi"], 1)
            V.tensor_tensor(keep[:, 0, :], keep[:, 0, :], keep[:, 1, :], ALU.mult).then_inc(S["mask_lo"], 1)

            dve.wait_ge(S["load_x"], 64)
            with dve.Fori(0, B // 4) as turn:
                for j in range(4):
                    ins = V.bn_stats(tstat[:, bass.ds(turn * 4 + j, 1), :].rearrange("p a s -> p (a s)"),
                                     X[:, bass.ds(turn * 4 + j, 1), :].rearrange("p a w -> p (a w)"))
                ins.then_inc(S["tok_dev"], 1)
            dve.wait_ge(S["load_tok"], 80)
            for c in range(3):
                V.tensor_scalar(convT[:, c], projT[:, 0], convb[:, c:c + 1], None, ALU.mult).then_inc(S["tok_bias0"], 1)
            for o in (1, 2):
                for c in range(3):
                    dve.wait_ge(S["tok_bias0"], 3 * o + c - 2)
                    V.scalar_tensor_tensor(out=convT[:, c], in0=projT[:, o], scalar=convb[:, 3 * o + c:3 * o + c + 1],
                                           in1=convT[:, c], op0=ALU.mult, op1=ALU.add).then_inc(S["tok_bias0"], 1)
            dve.wait_ge(S["const_ready"], 1)
            for j in range(GRP):
                V.tensor_copy(xg[:, 1, :, j * NI:j * NI + NI], lnwb[:, 1, :].rearrange("p (k l) -> p k l", k=CHUNKS))
            for k in range(CHUNKS):
                ins = V.tensor_scalar(xg[:, 0, k, :], ones[:, 0:ROWS], convb[:, 9 + k // 2:10 + k // 2], None, ALU.mult)
            dve.wait_ge(S["tok_bias0"], 9)
            ins.then_inc(S["tok_w"], 1)
            dve.wait_ge(S["tok_dev"], B // 4)
            n_half = XW // 2
            T = tsmall
            link(V.tensor_tensor(T[:, 0, :], tstat[:, :, 1], tstat[:, :, 4], ALU.add))
            V.tensor_scalar(T[:, 0, :], T[:, 0, :], 0.5, None, ALU.mult).then_inc(S["tok_stat"], 1)
            dve.wait_ge(S["tok_mean"], 1)
            link(V.tensor_copy(T[:, 1, :], bank[0][:, 0:B]))
            for q, src in ((2, 1), (4, 4)):
                link(V.tensor_tensor(T[:, q, :], tstat[:, :, src], T[:, 1, :], ALU.subtract))
                link(V.tensor_tensor(T[:, q, :], T[:, q, :], T[:, q, :], ALU.mult))
            link(V.tensor_tensor(T[:, 2, :], T[:, 2, :], T[:, 4, :], ALU.add))
            link(V.tensor_tensor(T[:, 4, :], tstat[:, :, 2], tstat[:, :, 5], ALU.add))
            V.scalar_tensor_tensor(out=T[:, 3, :], in0=T[:, 4, :], scalar=1.0 / n_half, in1=T[:, 2, :],
                                   op0=ALU.mult, op1=ALU.add).then_inc(S["tok_varsum"], 1)
            dve.wait_ge(S["tok_devavg"], 1)
            V.tensor_scalar(T[:, 4, :], bank[1][:, 0:B], 0.5, LN_EPS, ALU.mult, ALU.add).then_inc(S["tok_eps"], 1)
            dve.wait_ge(S["tok_eps"], 1)
            rsqrt(T[:, 5, :], T[:, 4, :], T[:, 2, :], link).then_inc(S["tok_rstd"], 1)
            dve.wait_ge(S["tok_bias_mm"], 1)
            V.tensor_tensor(tokb[:, :], bank[2][0:ROWS, 0:C], projb[:, :], ALU.add).then_inc(S["tok_bias"], 1)
            dve.wait_ge(S["tok_bias"], 1)
            V.tensor_tensor(tokb[:, :], tokb[:, :], pos[:, :], ALU.add).then_inc(S["tok_bias"], 1)
            dve.wait_ge(S["tok_rstd"], 1)

            def patch_scale(g, slot, count):
                when(dve, S["tok_mm"], g - 1)
                for j in range(count):
                    b = g * GRP + j
                    ins = V.tensor_scalar(X[:, bass.ds(b, 1), :].rearrange("p a w -> p (a w)"),
                                          X[:, bass.ds(b, 1), :].rearrange("p a w -> p (a w)"),
                                          T[:, 1, bass.ds(b, 1)], T[:, 5, bass.ds(b, 1)], ALU.subtract, ALU.mult)
                ins.then_inc(S["tok_norm"], 1)
                dve.wait_ge(S["tok_norm"], g + 1)
                for j in range(count):
                    ins = V.tensor_tensor(xg[:, slot, :, j * NI:j * NI + NI],
                                          X[:, bass.ds(g * GRP + j, 1), :].rearrange("p a (k l) -> p (a k) l", k=CHUNKS),
                                          lnwb[:, 0, :].rearrange("p (k l) -> p k l", k=CHUNKS), ALU.mult)
                ins.then_inc(S["tok_xg"], 1)

            def patch_add(g, slot, count, uses):
                dve.wait_ge(S["tok_mm"], g + 1)
                dve.wait_ge(S["tok_bias"], 2)
                when(dve, S[f"tok_piece{slot}"], 16 * GRP * uses)
                rows = NI * count
                V.tensor_tensor(tok[0:rows, slot, :], bank[slot][0:rows, 0:C], tokb[0:rows, :], ALU.add)\
                 .then_inc(S["tok_sum"], 1)

            patch_scale(0, 0, GRP)
            patch_scale(1, 1, GRP)
            patch_add(0, 0, GRP, 0)
            patch_scale(2, 0, GRP)
            patch_add(1, 1, GRP, 0)
            patch_scale(3, 1, GRP)
            with dve.Fori(1, 4) as turn:
                patch_add(turn * 2, 0, GRP, turn)
                patch_scale(turn * 2 + 2, 0, GRP)
                patch_add(turn * 2 + 1, 1, GRP, turn)
                patch_scale(turn * 2 + 3, 1, GRP)
            patch_add(8, 0, GRP, 4)
            patch_scale(10, 0, 2)
            patch_add(9, 1, GRP, 4)
            patch_add(10, 0, 2, 5)

            dve.wait_ge(S["mask_lo"], 2)
            dve.wait_ge(S["tok_piece0"], 16 * (5 * GRP + 2))
            dve.wait_ge(S["tok_piece1"], 16 * 5 * GRP)
            dve.wait_ge(S["gathered"], 16 * B)

            def image(t_, b, i=1):
                return t_[:, bass.ds(b, 1), :].rearrange("p a c -> p (a c)")

            with dve.Fori(0, B // 4) as turn:
                for j in range(4):
                    b = turn * 4 + j
                    ins = V.tensor_scalar(image(h, b), image(h, b), keep[:, 0, bass.ds(b, 1)], None, ALU.mult)
                ins.then_inc(S["masked"], 1)
                dve.wait_ge(S["masked"], turn + 1)
                for j in range(4):
                    ins = V.bn_stats(image(stats, turn * 4 + j), image(h, turn * 4 + j))
                ins.then_inc(S["ln0_stat"], 1)

            def finish_stats(sem, count):
                dve.wait_ge(sem, count)
                V.tensor_tensor(lns[:, 0, :], stats[:, :, 1], stats[:, :, 4], ALU.add)
                V.tensor_tensor(lns[:, 1, :], stats[:, :, 1], stats[:, :, 4], ALU.subtract)
                link(V.tensor_tensor(lns[:, 2, :], stats[:, :, 2], stats[:, :, 5], ALU.add))
                V.tensor_scalar(mean[:, :], lns[:, 0, :], 0.5, None, ALU.mult)
                link(V.scalar_tensor_tensor(out=lns[:, 3, :], in0=lns[:, 1, :], scalar=0.25, in1=lns[:, 1, :],
                                            op0=ALU.mult, op1=ALU.mult))
                link(V.scalar_tensor_tensor(out=lns[:, 0, :], in0=lns[:, 2, :], scalar=1.0 / C, in1=lns[:, 3, :],
                                            op0=ALU.mult, op1=ALU.add))
                link(V.tensor_scalar(lns[:, 3, :], lns[:, 0, :], LN_EPS, None, ALU.add))
                link(rsqrt(rstd[:, :], lns[:, 3, :], lns[:, 1, :], link))

            def normalise(t, slot, sem, free, n_free):
                when(dve, free, n_free)
                for i in range(2):
                    b = t * 2 + i
                    ins = V.tensor_scalar(xn[:, slot, i, :], image(h, b), mean[:, bass.ds(b, 1)],
                                          rstd[:, bass.ds(b, 1)], ALU.subtract, ALU.mult)
                ins.then_inc(sem, 1)

            finish_stats(S["ln0_stat"], B // 4)
            dve.wait_ge(S["load_att"], 64)
            mask4 = mask[0:HC, :].rearrange("p (a c) -> p a c", a=1)

            def att_rest(t, slot):
                dve.wait_ge(S["att_out"], t + 1)
                V.tensor_tensor(h[:, bass.ds(t * 2, 2), :], bank[3][0:N, 0:2 * C].rearrange("p (i c) -> p i c", i=2),
                                h[:, bass.ds(t * 2, 2), :], ALU.add).then_inc(S["att_h"], 1)
                dve.wait_ge(S["att_h"], t + 1)
                for i in range(2):
                    ins = V.bn_stats(image(stats, t * 2 + i), image(h, t * 2 + i))
                ins.then_inc(S["att_stat"], 1)

            def att_divide(t, slot):
                dve.wait_ge(S["att_frac"], t + 1)
                V.reciprocal(rden[:, :], wide[1][0:N, 0, 2 * C:2 * C + 2 * HEADS]).then_inc(S["att_rden"], 1)
                dve.wait_ge(S["att_rden"], t + 1)
                when(dve, S["att_oTp"], t - 1)
                V.tensor_tensor(on[:, slot].rearrange("p i h (a d) -> p (i h a) d", d=HD),
                                wide[1][0:N, 0, 0:2 * C].rearrange("p (a d) -> p a d", d=HD),
                                rden[:, :].rearrange("p (a d) -> p a d", d=1).broadcast_to([N, 2 * HEADS, HD]),
                                ALU.mult).then_inc(S["att_on"], 1)

            def attention(t, slot):
                first = isinstance(t, int) and t == 0
                dve.wait_ge(S["att_kv"], t + 1)
                when(dve, S["att_prod"], t - 1)
                V.tensor_scalar(kS[:, slot, :, :, 0:HC], wide[0][0:N, :, 0:C].rearrange("p i (h c) -> p i h c", h=2),
                                0.0, HD ** -0.5, ALU.max, ALU.add).then_inc(S["att_ks"], 1)
                if not first:
                    att_divide(t - 1, 1 - slot)
                dve.wait_ge(S["att_q"], t + 1)
                when(dve, S["att_frac"], t - 1)
                V.tensor_scalar(qT[0:HC, slot].rearrange("p h n -> p (h n)"), bank[1][0:HC, 0:4 * N],
                                0.0, HD ** -0.5, ALU.max, ALU.add).then_inc(S["att_qs"], 1)
                dve.wait_ge(S["att_prod"], t + 1)
                prod = bank[2][0:HC, 0:4 * KA].rearrange("p (a c) -> p a c", a=4)
                V.tensor_tensor(kvm[:, slot].rearrange("p i h c -> p (i h) c"), prod[:, :, 0:HC],
                                mask4.broadcast_to([HC, 4, HC]), ALU.mult)
                V.tensor_tensor(ksm[0:HC, slot].rearrange("p i h c -> p (i h) c"),
                                prod[:, :, HC:KA].broadcast_to([HC, 4, HH]),
                                mask4[:, :, 0:HC:HD].broadcast_to([HC, 4, HH]), ALU.mult).then_inc(S["att_ksm"], 1)
                if not first:
                    att_rest(t - 1, 1 - slot)
                if not (isinstance(t, int) and t + 2 >= PAIRS):
                    normalise(t + 2, slot, S["att_xn"], S["att_xT"], t + 1)

            normalise(0, 0, S["att_xn"], None, 0)
            normalise(1, 1, S["att_xn"], None, 0)
            over_pairs(dve, attention)
            att_divide(PAIRS - 1, 1)
            att_rest(PAIRS - 1, 1)

            finish_stats(S["att_stat"], PAIRS)

            def gate0(t, slot):
                normalise(t, slot, S["gate0_xn"], S["gate0_mean"], t - 1)

            over_pairs(dve, gate0)
            dve.wait_ge(S["gate0_mean"], PAIRS)
            dve.wait_ge(S["load_ffn"], 64)
            link(V.tensor_copy(gm[:, :, :].rearrange("p h b -> p (h b)"), bank[1][0:HC, 0:2 * B]))
            for k in range(2):
                ins = V.tensor_tensor(gprod[:, k], gm[:, k, :].rearrange("p (b a) -> p b a", a=1).broadcast_to([HC, B, E0]),
                                      wg0[:, k, :].rearrange("p (a e) -> p a e", a=1).broadcast_to([HC, B, E0]), ALU.mult)
            ins.then_inc(S["gate0_prod"], 1)
            dve.wait_ge(S["gate0_logit"], 1)
            logit = bank[2][:, 0:B * E0].rearrange("p (b e) -> p b e", e=E0)

            def spread(v, e=E0):
                return v.rearrange("p (b a) -> p b a", a=1).broadcast_to([128, B, e])

            link(V.tensor_reduce(gone[:, 0, :], logit, AX_X, ALU.max))
            V.tensor_tensor(gsm[:, 0], logit, spread(gone[:, 0, :]), ALU.subtract).then_inc(S["gate0_step"], 1)
            dve.wait_ge(S["gate0_exp"], 1)
            ex = gsm[:, 1]
            V.tensor_reduce(gone[:, 1, :], ex, AX_X, ALU.add)
            link(V.tensor_reduce(gone[:, 0, :], ex, AX_X, ALU.max))
            V.reciprocal(gone[:, 2, :], gone[:, 1, :])
            link(V.tensor_tensor(gsm[:, 0], ex, spread(gone[:, 0, :]), ALU.is_lt))
            V.tensor_tensor(gone[:, 4, :], gone[:, 2, :], gone[:, 0, :], ALU.mult)
            link(V.tensor_scalar(gone[:, 3, :], gsm[:, 0, :, 1], 1.0, None, ALU.add))
            V.tensor_tensor(sel[:, :], gone[0:1, 3, :], gsm[0:1, 0, :, 0], ALU.mult).then_inc(S["gate0_ready"], 1)

            def ffn_add(u, i):
                dve.wait_ge(S["ffn_y"], u + 1)
                V.scalar_tensor_tensor(out=image(h, u), in0=bank[3][0:N, i * 256:i * 256 + C],
                                       scalar=gone[0:N, 4, bass.ds(u, 1)], in1=image(h, u),
                                       op0=ALU.mult, op1=ALU.add).then_inc(S["ffn_h"], 1)
                dve.wait_ge(S["ffn_h"], u + 1)
                V.bn_stats(image(stats, u), image(h, u)).then_inc(S["ffn_stat"], 1)

            def ffn_hT(u, i):
                dve.wait_ge(S["ffn_hT"], u + 1)
                when(dve, S["ffn_y"], u - 1)
                V.tensor_copy(hT[:, i, 0:3, :], bank[1][:, 0:3 * N].rearrange("p (k n) -> p k n", k=3))\
                 .then_inc(S["ffn_hTv"], 1)

            def ffn(t, slot):
                for i in range(2):
                    u = t * 2 + i
                    if not first(u):
                        ffn_hT(u - 1, 1 - i)
                    if i == 0 and not (isinstance(t, int) and t + 2 >= PAIRS):
                        normalise(t + 2, slot, S["ffn_xn"], S["ffn_xT"], t + 1)
                    if not first(u):
                        ffn_add(u - 1, 1 - i)

            normalise(0, 0, S["ffn_xn"], S["gate0_mean"], PAIRS)
            normalise(1, 1, S["ffn_xn"], None, 0)
            over_pairs(dve, ffn)
            ffn_hT(B - 1, 1)
            ffn_add(B - 1, 1)

            dve.wait_ge(S["load_ttt"], 128)
            heads_of_w = w1b[:, :, :].rearrange("p m (a d) -> p (m a) d", d=HD)
            link(V.tensor_reduce(w1m[:, :], heads_of_w, AX_X, ALU.add))
            link(V.tensor_scalar(w1m[:, :], w1m[:, :], 1.0 / HD, None, ALU.mult))
            V.tensor_tensor(w1c[:, :, :].rearrange("p m (a d) -> p (m a) d", d=HD), heads_of_w,
                            w1m[:, :].rearrange("p (a d) -> p a d", d=1).broadcast_to([KA, HEADS, HD]), ALU.subtract)\
             .then_inc(S["tw_cent"], 1)
            other = wtok[:, :, 2 * C:3 * C]
            link(V.tensor_tensor(other, other, wv[:, :, :], ALU.subtract))
            link(V.tensor_tensor(other, other, gam[0:KA, :].rearrange("p (a c) -> p a c", a=1).broadcast_to([KA, 2, C]),
                                 ALU.mult))
            for i in range(2):
                V.tensor_tensor(gam2[:, i, :], gam[:, :], gam[:, :], ALU.mult)
            V.memset(kA[:, :, :, :, HC:KA], 1.0)
            for k, value in enumerate((TTT_EPS, 1.0 / (HD * N), 1.0 / HD)):
                V.memset(tc[:, k, :], value)
            dve.wait_ge(S["tw_comp"], 1)
            V.tensor_scalar(gcol[:, 0:2], gcol[:, 0:2], -1.0, None, ALU.mult)
            V.tensor_copy(wtok[0:HC, :, C:2 * C], bank[1][0:HC, 0:4 * HC].rearrange("p (k c) -> p k c", k=2))
            dve.wait_ge(S["tw_cent"], 1)
            V.tensor_copy(wtok[HC:KA, 0, C:2 * C], w1c[HC:KA, :, :].rearrange("p m c -> p (m c)"))
            V.tensor_tensor(wp[HC:KA, 0, :], bank[2][HC:KA, 0:C], wp[HC:KA, 0, :], ALU.add).then_inc(S["tw_done"], 1)
            dve.wait_ge(S["tw_done"], 1)
            finish_stats(S["ffn_stat"], B)
            V.memset(fill[:, :, 0:C], 0.0)
            V.memset(fill[:, :, C + 1:RW], 0.0)
            V.tensor_copy(fill[:, :, C], dump[:, :]).then_inc(S["filled"], 1)

            def heads(v):
                return v.rearrange("p (a d) -> p a d", d=HD)

            def per_head(v):
                return v.rearrange("p (a d) -> p a d", d=1).broadcast_to([N, 2 * HEADS, HD])

            mask97 = mask[:, :].rearrange("p (a c) -> p a c", a=1).broadcast_to([KA, 4, HC])

            def ttt_weights(t, slot):
                dve.wait_ge(S["ttt_grad"], t + 1)
                when(dve, S["ttt_w"], t)
                V.tensor_tensor(gmk[:, :].rearrange("p (a c) -> p a c", a=4),
                                bank[2][0:KA, 0:4 * HC].rearrange("p (a c) -> p a c", a=4), mask97, ALU.mult)\
                 .then_inc(S["ttt_gm"], 1)
                dve.wait_ge(S["ttt_gm"], t + 1)
                when(dve, S["ttt_zb"], t - 1)
                V.tensor_tensor(wn[:, slot % 2].rearrange("p i m c -> p i (m c)"),
                                w1b[:, :, :].rearrange("p (a m) c -> p a (m c)", a=1).broadcast_to([KA, 2, C]),
                                gmk[:, :].rearrange("p (i c) -> p i c", i=2), ALU.subtract).then_inc(S["ttt_w"], 1)

            def ttt_centre(t, slot):
                s_ = sm[:, slot % 2]
                z = heads(wide[1][0:N, 0, 0:2 * C])
                dve.wait_ge(S["ttt_zb"], t + 1)
                V.tensor_reduce(s_[:, 4, :], z, AX_X, ALU.add).then_inc(S["ttt_zm"], 1)
                dve.wait_ge(S["ttt_zm"], t + 1)
                when(dve, S["ttt_zh"], t)
                V.scalar_tensor_tensor(out=heads(zc[:, :]), in0=per_head(s_[:, 4, :]), scalar=1.0 / HD, in1=z,
                                       op0=ALU.mult, op1=ALU.subtract).then_inc(S["ttt_zc"], 1)

            def spread_of_outer(t):
                dve.wait_ge(S["ttt_zsq"], t + 1)
                V.tensor_reduce(hv[:, 2 * HEADS:], heads(zsq[:, :]), AX_X, ALU.add).then_inc(S["ttt_zv"], 1)

            def root(turn, a, b):
                c = slice(a * 2 * HEADS, b * 2 * HEADS)
                done = [0]

                def then(ins):
                    done[0] += 1
                    ins.then_inc(S["root"], 1)
                    dve.wait_ge(S["root"], 10 * turn + done[0])

                if a == 0:
                    dve.wait_ge(S["ttt_v"], turn + 1)
                if b == 2:
                    dve.wait_ge(S["ttt_zv"], turn)
                when(dve, S["ttt_r"], turn)
                then(V.tensor_scalar(hv[:, c], hv[:, c], TTT_EPS, None, ALU.add))
                return rsqrt(irs[:, c], hv[:, c], hw[:, c], then)

            def normalised_outer(t, slot):
                dve.wait_ge(S["ttt_rstd"], t + 2)
                when(dve, S["ttt_zT"], t - 1)
                V.tensor_tensor(heads(zh[:, slot % 2, :]), heads(zc[:, :]), per_head(irs[:, 2 * HEADS:]), ALU.mult)\
                 .then_inc(S["ttt_zh"], 1)

            def ttt_combine(t, slot):
                dve.wait_ge(S["ttt_zT"], t + 1)
                when(dve, S["ttt_out"], t - 1)
                for k in range(2):
                    ins = V.scalar_tensor_tensor(
                        out=oT[0:HC, slot % 2, k].rearrange("p i n -> p (i n)"), in0=bank[0][0:HC, k * 2 * N:(k + 1) * 2 * N],
                        scalar=gcol[:, k:k + 1], in1=qT[0:HC, slot % 4, k, :], op0=ALU.mult, op1=ALU.add)
                ins.then_inc(S["ttt_oT"], 1)

            def ttt_add(t, slot):
                dve.wait_ge(S["ttt_out"], t + 1)
                V.tensor_tensor(h[:, bass.ds(t * 2, 2), :], wide[1][0:N, 1, 0:2 * C].rearrange("p (i c) -> p i c", i=2),
                                h[:, bass.ds(t * 2, 2), :], ALU.add).then_inc(S["ttt_h"], 1)
                dve.wait_ge(S["ttt_h"], t + 1)
                for i in range(2):
                    ins = V.bn_stats(image(stats, t * 2 + i), image(h, t * 2 + i))
                ins.then_inc(S["ttt_stat"], 1)

            def ttt(t, slot):
                fixed = isinstance(t, int)
                before = not (fixed and t == 0)
                s_ = sm[:, slot % 2]
                if not (fixed and t < 2):
                    ttt_add(t - 2, slot - 2)
                if not (fixed and t + 2 >= PAIRS):
                    normalise(t + 2, slot % 2, S["ttt_xn"], S["ttt_xT"], t + 1)
                if before:
                    ttt_weights(t - 1, slot - 1)
                dve.wait_ge(S["ttt_sq"], t + 1)
                V.tensor_reduce(hv[:, 0:2 * HEADS], heads(sq[:, :]), AX_X, ALU.add).then_inc(S["ttt_v"], 1)
                if before:
                    ttt_centre(t - 1, slot - 1)
                    spread_of_outer(t - 1)
                root(t, 0, 2 if before else 1).then_inc(S["ttt_rstd"], 1)
                dve.wait_ge(S["ttt_rstd"], t + 1)
                V.tensor_tensor(xh[:, :].rearrange("p (x a d) -> p x a d", x=4, d=HD),
                                kA[:, slot % 2, :, 2:4, 0:HC].rearrange("p i m (a d) -> p i m a d", d=HD),
                                irs[:, 0:2 * HEADS].rearrange("p (x a d) -> p x a d", x=4, d=1).broadcast_to([N, 4, HH, HD]),
                                ALU.mult).then_inc(S["ttt_xh"], 1)
                if before:
                    normalised_outer(t - 1, slot - 1)
                dve.wait_ge(S["ttt_t1"], t + 1)
                V.tensor_tensor(gg[:, :].rearrange("p (i c) -> p i c", i=2), t1[:, :].rearrange("p (i c) -> p i c", i=2),
                                dl[:, slot % 2, :, 0:C], ALU.add).then_inc(S["ttt_g"], 1)
                dve.wait_ge(S["ttt_g"], t + 1)
                V.tensor_tensor(pp[:, :], gg[:, :], xh[:, :], ALU.mult).then_inc(S["ttt_p"], 1)
                dve.wait_ge(S["ttt_p"], t + 1)
                V.tensor_reduce(s_[:, 3, :], heads(pp[:, :]), AX_X, ALU.add).then_inc(S["ttt_s"], 1)
                if before:
                    ttt_combine(t - 1, slot - 1)
                dve.wait_ge(S["ttt_r"], t + 1)
                dve.wait_ge(S["ttt_s"], t + 1)
                V.tensor_tensor(heads(pp[:, :]), heads(gg[:, :]), per_head(s_[:, 2, :]), ALU.mult).then_inc(S["ttt_gr"], 1)
                dve.wait_ge(S["ttt_gr"], t + 1)
                dve.wait_ge(S["ttt_xs"], t + 1)
                when(dve, S["ttt_grad"], t - 1)
                V.tensor_tensor(zz[:, slot % 2, :], pp[:, :], xs[:, :], ALU.subtract).then_inc(S["ttt_zz"], 1)

            normalise(0, 0, S["ttt_xn"], None, 0)
            normalise(1, 1, S["ttt_xn"], None, 0)
            over_pairs(dve, ttt, 4)
            t, slot = PAIRS - 1, 3
            ttt_add(t - 1, slot - 1)
            ttt_weights(t, slot)
            ttt_centre(t, slot)
            spread_of_outer(t)
            root(PAIRS, 1, 2).then_inc(S["ttt_rstd"], 1)
            normalised_outer(t, slot)
            ttt_combine(t, slot)
            ttt_add(t, slot)

            dve.wait_ge(S["load_moe"], 112)
            finish_stats(S["ttt_stat"], PAIRS)
            link(V.tensor_tensor(lns[:, 1, :], lns[:, 0, :], rstd[:, :], ALU.mult))
            link(V.tensor_tensor(lns[:, 1, :], lns[:, 1, :], rstd[:, :], ALU.mult))
            link(V.tensor_scalar(lns[:, 1, :], lns[:, 1, :], RMS_EPS, None, ALU.add))
            V.memset(aT[HC:KA, :, :, :], 1.0)
            V.memset(xTm[HC:KA, :, :, :], 1.0)
            link(rsqrt(rr, lns[:, 1, :], lns[:, 2, :], link))
            link(V.tensor_scalar(base, iota[:, 0:E1], float(CAP), None, ALU.mult))

            def rt_rows(turn, j):
                t, slot, _ = at_two(turn, j)
                when(dve, S["rt_tT"], t - 1)
                when(dve, S["row_t"], t - 1)
                normalise(t, slot, S["rt_xn"], None, 0)
                dve.wait_ge(S["rt_xn"], t + 1)
                for i in range(2):
                    ins = V.scalar_tensor_tensor(out=ts[:, slot, i, :], in0=xn[:, slot, i, :],
                                                 scalar=rr[:, bass.ds(t * 2 + i, 1)], in1=scale[:, :],
                                                 op0=ALU.mult, op1=ALU.mult)
                ins.then_inc(S["rt_t"], 1)
                V.tensor_tensor(h[:, bass.ds(t * 2, 2), :], h[:, bass.ds(t * 2, 2), :], xn[:, slot], ALU.add)

            def spread(v, count):
                return v.rearrange("p (b a) -> p b a", a=1).broadcast_to([v.shape[0], v.shape[1], count])

            def rt_choose(turn, j):
                t, slot, half = at_two(turn, j)
                done = [0]

                def then(ins):
                    done[0] += 1
                    ins.then_inc(S["rt_step"], 1)
                    dve.wait_ge(S["load_moe"], 112)
                    dve.wait_ge(S["rt_step"], 9 * t + done[0])

                dve.wait_ge(S["rt_logit"], t + 1)
                V.tensor_copy(gs[:, slot], bank[1][0:N, 0:2 * E1].rearrange("p (i e) -> p i e", i=2))\
                 .then_inc(S["rt_gs"], 1)
                dve.wait_ge(S["load_moe"], 112)
                dve.wait_ge(S["rt_gs"], t + 1)
                for i in range(2):
                    ins = V.max(m8[:, slot, i, :], gs[:, slot, i, :])
                then(ins)
                when(dve, S["rt_exp"], t - 1)
                V.tensor_tensor(wraw[:, slot, :].rearrange("p (i k) -> p i k", i=2), m8[:, slot, :, 0:TOPK],
                                m8[:, slot, :, 0:1].broadcast_to([N, 2, TOPK]), ALU.subtract).then_inc(S["rt_less"], 1)
                for i in range(2):
                    ins = V.max_index(i8[:, slot, i, :], m8[:, slot, i, :], gs[:, slot, i, :])
                then(ins)
                then(V.tensor_copy(topf[:, slot, :].rearrange("p (i k) -> p i k", i=2), i8[:, slot, :, 0:TOPK]))
                then(V.tensor_tensor(hot[:, slot], spread(topf[:, slot, :], E1),
                                     iota[0:N, 0:E1].rearrange("p (a e) -> p a e", a=1).broadcast_to([N, 2 * TOPK, E1]),
                                     ALU.is_equal))
                V.tensor_reduce(taken[:, slot], hot[:, slot].rearrange("p (i k) e -> p i e k", i=2), AX_X, ALU.add)\
                 .then_inc(S["rt_taken"], 1)
                when(dve, S[f"dispatched{slot}"], 16 * 2 * TOPK * half)
                V.tensor_copy(rowbuf[:, slot, :, C].rearrange("p (i k) -> p i k", i=2), target[:, bass.ds(t * 2, 2), :])
                dve.wait_ge(S["rt_exp"], t + 1)
                then(V.tensor_reduce(wsum[:, slot, :], wexp[:, slot, :].rearrange("p (i k) -> p i k", i=2), AX_X,
                                     ALU.add))
                then(V.reciprocal(wsum[:, slot, :], wsum[:, slot, :]))
                V.tensor_tensor(rowbuf[:, slot, :, C + 1].rearrange("p (i k) -> p i k", i=2),
                                wexp[:, slot, :].rearrange("p (i k) -> p i k", i=2), spread(wsum[:, slot, :], TOPK),
                                ALU.mult)
                dve.wait_ge(S["rt_count"], t + 1)
                then(V.tensor_tensor(place.rearrange("p (i e) -> p i e", i=2),
                                     bank[2][0:N, 0:2 * E1].rearrange("p (i e) -> p i e", i=2),
                                     base[0:N, :].rearrange("p (a e) -> p a e", a=1).broadcast_to([N, 2, E1]),
                                     ALU.add))
                V.tensor_tensor(base, bank[2][:, 2 * E1:3 * E1], base, ALU.add).then_inc(S["rt_base"], 1)
                hot4 = hot[:, slot].rearrange("p (i k) e -> p i k e", i=2)
                then(V.tensor_tensor(hot4, hot4, place.rearrange("p (i a e) -> p i a e", i=2, a=1)
                                     .broadcast_to([N, 2, TOPK, E1]), ALU.mult))
                then(V.tensor_reduce(rowf, hot[:, slot], AX_X, ALU.add))
                V.tensor_copy(slot_s[:, slot, :], rowf).then_inc(S["row_meta"], 1)
                dve.wait_ge(S["rt_base"], t + 1)

            def route(turn, j):
                if not (last(turn, PAIRS // 2) and j == 1):
                    rt_rows(turn, j + 1)
                rt_choose(turn, j)

            rt_rows(0, 0)
            over_twos(dve, route, PAIRS)

            link(V.tensor_scalar(pad_f, base, iota[:, E1:E1 + 1], None, ALU.add))
            V.tensor_copy(pad_at[:, :], pad_f).then_inc(S["pad_ready"], 1)
            count, blocks, ends, ended, one = (per_e[:, k, :] for k in range(5))
            link(V.memset(one, 1.0))
            link(V.scalar_tensor_tensor(out=count, in0=iota[:, 0:E1], scalar=float(-CAP), in1=base, op0=ALU.mult, op1=ALU.add))
            link(V.tensor_scalar(per_ei[:, 0, :], count, 127.0, None, ALU.add))
            link(V.tensor_scalar(per_ei[:, 1, :], per_ei[:, 0, :], 7, None, ALU.arith_shift_right))
            link(V.tensor_copy(blocks, per_ei[:, 1, :]))
            link(V.tensor_tensor_scan(ends, one, blocks, 0.0, ALU.mult, ALU.add))
            link(V.tensor_scalar(ended, ends, iota[:, E1:E1 + 1], None, ALU.is_le))
            link(V.tensor_reduce(block_f[:, 2:3], ended, AX_X, ALU.add))
            link(V.tensor_tensor(ended, ended, blocks, ALU.mult))
            link(V.tensor_reduce(block_f[:, 3:4], ended, AX_X, ALU.add))
            link(V.tensor_scalar(block_f[:, 0:1], block_f[:, 2:3], float(E1 - 1), None, ALU.min))
            link(V.tensor_tensor(block_f[:, 3:4], iota[:, E1:E1 + 1], block_f[:, 3:4], ALU.subtract))
            link(V.tensor_scalar(block_f[:, 3:4], block_f[:, 3:4], 128.0, None, ALU.mult))
            V.scalar_tensor_tensor(out=block_f[:, 1:2], in0=block_f[:, 2:3], scalar=float(CAP), in1=block_f[:, 3:4],
                                   op0=ALU.mult, op1=ALU.add).then_inc(S["rt_blocks"], 1)
            V.memset(experts[:, 0:4], 0.0)
            dve.wait_ge(S["rt_row"], 1)
            link(V.tensor_copy(experts[:, 4:4 + BLOCKS], bank[3][0:1, 0:BLOCKS]))
            V.tensor_copy(first_row[:, :], bank[3][0:1, BLOCKS:2 * BLOCKS])
            digit = experts[:, :].rearrange("p (t j) -> p j t", j=4)
            link(V.tensor_copy(etab_f[:, :], digit[:, 2, 0:BLOCKS // 4]))
            for k in range(1, 6):
                q, j = divmod(k + 2, 4)
                link(V.scalar_tensor_tensor(out=etab_f[:, :], in0=digit[:, j, q:q + BLOCKS // 4], scalar=float(E1 ** k),
                                            in1=etab_f[:, :], op0=ALU.mult, op1=ALU.add))
            V.tensor_copy(etab[:, :], etab_f[:, :]).then_inc(S["rt_done"], 1)

            def moe_gate(turn, j):
                n, four, half = at(turn, j)
                slot = four % 2
                dve.wait_ge(S["moe_h"], n + 1)
                dve.wait_ge(S[f"loaded{four}"], 16 * (turn + 1))
                when(dve, S["moe_sig"], n - 1)
                when(dve, S["moe_p"], n - 1)
                when(dve, S["moe_ys"], n - 3)
                when(dve, S[f"moe_out{slot}"], 16 * (half - 1))
                V.tensor_copy(weight[:, four, :], xb[:, four, C + 1:C + 2])
                V.tensor_copy(dest[:, four, :], xb[:, four, C:C + 1])
                V.tensor_scalar(al[:, slot, 0:I1], up[slot][:, 0:I1], LIMIT, None, ALU.min)
                V.tensor_scalar(al[:, slot, I1:2 * I1], up[slot][:, I1:2 * I1], -LIMIT, LIMIT, ALU.max, ALU.min)\
                 .then_inc(S["moe_al"], 1)
                dve.wait_ge(S["moe_al"], n + 1)
                when(dve, S["moe_act"], n - 1)
                V.scalar_tensor_tensor(out=pr[:, slot, :], in0=al[:, slot, I1:2 * I1], scalar=1.0, in1=al[:, slot, 0:I1],
                                       op0=ALU.add, op1=ALU.mult).then_inc(S["moe_p"], 1)

            def moe_weigh(turn, j):
                n, slot, half = at(turn, j)
                dve.wait_ge(S["moe_y"], n + 1)
                when(dve, S[f"moe_out{slot % 2}"], 16 * half)
                V.tensor_scalar(ys[:, slot % 2, :], bank[3][:, 0:C], weight[:, slot, :], None, ALU.mult)\
                 .then_inc(S["moe_ys"], 1)

            def moe(turn, j):
                moe_gate(turn, j)
                if not (first(turn) and j < 2):
                    moe_weigh(turn, j - 2)

            over_blocks(dve, moe)
            moe_weigh(BLOCKS // 4 - 1, 2)
            moe_weigh(BLOCKS // 4 - 1, 3)

            def final(turn, j):
                b, slot, half = at(turn, j)
                dve.wait_ge(S[f"loaded{slot}"], 16 * (BLOCKS // 4 + turn + 1))
                when(dve, S["fin_b"], b)
                V.tensor_tensor(ya[:, :], yc[:, slot, 0:2 * C], yc[:, slot, 2 * C:4 * C], ALU.add).then_inc(S["fin_a"], 1)
                dve.wait_ge(S["fin_a"], b + 1)
                when(dve, S["fin_c"], b)
                V.tensor_tensor(yb[:, :], ya[:, 0:C], ya[:, C:2 * C], ALU.add).then_inc(S["fin_b"], 1)
                dve.wait_ge(S["fin_b"], b + 1)
                when(dve, S[f"stored{slot % 2}"], 16 * half)
                V.tensor_tensor(yo[:, slot % 2, :], yb[:, :], image(h, b), ALU.add).then_inc(S["fin_c"], 1)

            over_images(dve, final)


def halves(w):
    return w.T.reshape(2, HC, -1).transpose(1, 0, 2)


def with_bias(w, row):
    a = np.zeros((KA, 2, w.shape[0]), np.float32)
    a[:HC] = halves(w)
    a[HC, 0] = row
    return a


def layouts(inputs):
    g = {k: np.asarray(v) for k, v in inputs.items()}
    f = np.float32

    def patches(a):
        n = a.shape[0]
        a = a.reshape(n, 3, 6, 2, 8, 6, 16).transpose(4, 6, 0, 1, 3, 2, 5)
        return a.reshape(128, n, XW)

    ids = g["x_txt"].T
    idsm = np.zeros((N, B), ids.dtype)
    idsm[NI:] = ids
    convb = np.empty((128, 12), f)
    convb[:, 0:9] = g["L0_tok_conv_w"].reshape(1, 9)
    convb[:, 9:12] = g["L0_tok_conv_b"].reshape(1, 3)
    d = {}
    d["x"] = patches(g["x"])
    d["ids"] = ids
    d["idsm"] = idsm
    d["lnwb"] = np.concatenate([patches(g["L0_tok_ln_w"][None]), patches(g["L0_tok_ln_b"][None])], axis=1)
    d["convb"] = convb
    d["projT"] = g["L0_tok_proj_w"].reshape(C, 3, 2, 8, 16).transpose(3, 4, 1, 2, 0).reshape(128, 3, 2, C)
    d["projb"] = np.broadcast_to(g["L0_tok_proj_b"], (ROWS, C))
    d["pos"] = np.concatenate([g["L0_tok_pos_emb"][0]] * GRP, axis=0)
    d["table"] = g["L0_txt_weight"]
    d["att"] = with_bias(g["L0_attn_qkv_w"], 0)
    d["attp"] = with_bias(g["L0_attn_proj_w"], g["L0_attn_proj_b"])
    d["gate0"] = halves(g["L0_ffn_Wg"])
    d["f1"] = np.stack([with_bias(g["L0_ffn_W1"][e].T, g["L0_ffn_b1"][e]) for e in range(E0)], axis=1)
    d["f2"] = g["L0_ffn_W2"].reshape(E0, FT, 128, C).transpose(2, 0, 1, 3)
    d["fb2"] = g["L0_ffn_b2"][None]
    qkv = g["L1_attn_qkv_weight"]
    d["tq"] = with_bias(qkv[:C], g["L1_attn_q_bias"])
    wtok = np.zeros((KA, 2, WTOK), f)
    wtok[:, :, 0:C] = with_bias(qkv[C:2 * C], 0)
    wtok[:, :, 2 * C:3 * C] = with_bias(qkv[C:2 * C], g["L1_attn_ttt_norm_bias"].reshape(C))
    wtok[:, :, 3 * C:] = with_bias(g["L1_attn_ttt_lr_weight"][:, 0, :], g["L1_attn_ttt_lr_bias"][:, 0])
    d["tk"] = wtok
    d["tv"] = with_bias(qkv[2 * C:], g["L1_attn_v_bias"])
    d["tkn"] = qkv[C:2 * C].reshape(2, HC, C).transpose(1, 0, 2)
    gamma = g["L1_attn_ttt_norm_weight"].reshape(C)
    d["tg"] = np.broadcast_to(gamma, (N, C))
    d["tgc"] = np.concatenate([gamma.reshape(2, HC).T, g["L1_attn_ttt_norm_bias"].reshape(2, HC).T], axis=1)
    inner = np.zeros((KA, 2, HC), f)
    for n in range(HEADS):
        m, a = n // HH, (n % HH) * HD
        inner[a:a + HD, m, a:a + HD] = g["L1_attn_W1"][n]
        inner[HC, m, a:a + HD] = g["L1_attn_b1"][n, 0]
    d["tw"] = inner
    d["tp"] = with_bias(g["L1_attn_proj_weight"], g["L1_attn_proj_bias"])
    d["scale"] = np.broadcast_to(g["L1_ffn_scale"], (N, C))
    d["gate1"] = with_bias(g["L1_ffn_gate_w"], g["L1_ffn_gate_b"])
    d["m1"] = np.stack([with_bias(g["L1_ffn_w1"][e].T, g["L1_ffn_b1"][e]) for e in range(E1)], axis=1)
    d["m2"] = np.stack([with_bias(g["L1_ffn_w2"][e].T, g["L1_ffn_b2"][e]) for e in range(E1)], axis=1)
    d["tri"] = np.triu(np.ones((N, N), f), 1)
    d["iota"] = np.concatenate([np.broadcast_to(np.arange(E1, dtype=f), (128, E1)), np.arange(128, dtype=f)[:, None]], axis=1)
    p_, b_, k_ = np.ogrid[0:N, 0:B, 0:TOPK]
    d["target"] = ((b_ * N + p_) * TOPK + k_).astype(f)
    d["dump"] = (DUMP + np.arange(128)[:, None] + 128 * np.arange(PADS)[None]).astype(f)
    d["ident"] = np.eye(128, dtype=f)
    m = np.ones((KA, HC), f)
    m[:HC] = np.kron(np.eye(HH, dtype=f), np.ones((HD, HD), f))
    d["mask"] = m
    return d


NAMES = """x ids idsm lnwb convb projT projb pos table att attp gate0 f1 f2 fb2 tq tk tv tkn tg tgc tw tp scale gate1 m1 m2
ident mask tri iota target dump""".split()


def kernel(**inputs):
    import concourse.bacc as _bacc
    from concourse.bass_utils import run_bass_kernel_spmd as _run

    nc = _bacc.Bacc("TRN2", target_bir_lowering=False, num_devices=1)
    d = layouts(inputs)
    arrays, args = {}, []
    for name in NAMES:
        a = np.ascontiguousarray(d[name])
        arrays[f"in_{name}"] = a
        args.append(nc.dram_tensor(f"in_{name}", a.shape, mybir.dt.from_np(a.dtype), kind="ExternalInput").ap())
    args.append(nc.dram_tensor("out_0", (B, N, C), F32, kind="ExternalOutput").ap())
    build(nc, *args)
    r = _run(nc, [arrays], core_ids=[0])
    return r.results[0]["out_0"]
```

```python
from contextlib import ExitStack

import numpy as np

import concourse.bass as bass
from concourse import mybir

F32 = mybir.dt.float32
I32 = mybir.dt.int32
U32 = mybir.dt.uint32
ALU = mybir.AluOpType
ACT = mybir.ActivationFunctionType
AX_X = mybir.AxisListType.X

B = 32
NI, NW = 36, 77
N = NI + NW
C = 192
HC = C // 2
KA = HC + 1
PAIRS = B // 2
HEADS, HD = 12, 16
HH = HEADS // 2
F0 = 768
E0 = 3
FT = F0 // 128
E1, TOPK = 16, 4
I1 = 192
VOCAB = 8000
CHUNKS = 6
XW = CHUNKS * NI
GRP = 3
ROWS = GRP * NI
BLOCKS = (TOPK * N * B + E1 * 127) // 128
CAP = N * B + 128
SPARE = 16
SLOTS = E1 * CAP + SPARE * 128
RW = C + 2
DUMP = TOPK * N * B
PADS = E1 + 2
WTOK = 3 * C + HEADS
LN_EPS = 1e-5
TTT_EPS = 1e-6
RMS_EPS = 1e-5
ALPHA, LIMIT = 1.702, 7.0

SEMS = """load_x0 load_x1 load_tok load_idx load_att load_ffn load_ttt load_moe const_ready dve_chain gathered
tok_piece0 tok_piece1
tok_stat tok_dev tok_mean tok_devavg tok_varsum tok_eps tok_rstd tok_norm tok_xg tok_mm tok_sum tok_w tok_bias_mm
tok_bias0 tok_bias clipped mask masked ln0_stat att_xn att_xT att_xTs att_q att_kv att_qs att_ks att_vs
att_prod att_ksm att_frac att_rden att_on att_oTp att_oT att_out att_h att_stat gate0_xn gate0_mean gate0_prod
gate0_logit gate0_step gate0_exp gate0_ready ffn_xn ffn_xT ffn_xTs ffn_hid ffn_gelu ffn_hT ffn_hTv ffn_hTa ffn_y
ffn_h ffn_stat tw_cent tw_comp tw_done ttt_xn ttt_xT ttt_xTs ttt_q ttt_qs ttt_tok ttt_sq ttt_kA ttt_dl ttt_sig ttt_v
root ttt_rstd ttt_xh ttt_t1 ttt_g ttt_p ttt_s ttt_r ttt_gr ttt_xs ttt_zz ttt_grad ttt_w ttt_zb ttt_zm ttt_zc ttt_zsq
ttt_zv ttt_zh ttt_zT ttt_oT ttt_out ttt_h ttt_stat pool_inner rt_xn rt_t rt_tT rt_tTs rt_row rt_logit rt_gs rt_exp
rt_done filled row_t row_meta dispatched0 dispatched1 going loaded0 loaded1 loaded2 loaded3 moe_xT moe_xTs moe_h
moe_al moe_sig moe_p moe_act moe_aT moe_aTs moe_y moe_ys moe_out0 moe_out1 fin_a fin_b fin_c stored0 stored1 rt_less
rt_taken rt_count rt_base rt_step rt_blocks pad_ready padded ln_ready masked_odd going_act ttt_sum tok_prod""".split()


def when(eng, sem, n):
    if not isinstance(n, int) or n > 0:
        eng.wait_ge(sem, n)


def over_pairs(eng, step, unroll=2):
    start, tail = (4, 2) if unroll == 2 else (5, 3)
    for t in range(start):
        step(t, t % unroll)
    with eng.Fori(0, (PAIRS - tail - start) // unroll) as turn:
        for j in range(unroll):
            step(turn * unroll + (start + j), (start + j) % unroll)
    for t in range(PAIRS - tail, PAIRS):
        step(t, t % unroll)


def over_fours(eng, step, count):
    for j in range(4):
        step(0, j)
    with eng.Fori(1, count // 4 - 1) as turn:
        for j in range(4):
            step(turn, j)
    for j in range(4):
        step(count // 4 - 1, j)


def at(turn, j):
    return turn * 4 + j, j % 4, turn * 2 + j // 2


def over_twos(eng, step, count):
    for j in range(2):
        step(0, j)
    with eng.Fori(1, count // 2 - 1) as turn:
        for j in range(2):
            step(turn, j)
    for j in range(2):
        step(count // 2 - 1, j)


def at_two(turn, j):
    return turn * 2 + j, j % 2, turn + j // 2


def over_blocks(eng, step):
    over_fours(eng, step, BLOCKS)


def first(n):
    return isinstance(n, int) and n == 0


def last(n, count):
    return isinstance(n, int) and n == count - 1


def build(nc, x_d, ids_d, idsm_d, lnwb_d, convb_d, projT_d, projb_d, pos_d, table_d, att_d, attp_d, gate0_d,
          f1_d, f2_d, fb2_d, tq_d, tk_d, tv_d, tkn_d, tg_d, tgc_d, tw_d, tp_d, scale_d, gate1_d, m1_d, m2_d,
          ident_d, mask_d, tri_d, iota_d, target_d, dump_d, out_d):
    ctx = ExitStack()
    with ctx:
        def sb(name, shape, dt=F32):
            return ctx.enter_context(nc.sbuf_tensor(name, shape, dt))

        S = {n: ctx.enter_context(nc.semaphore(n)) for n in SEMS}
        bank = [ctx.enter_context(nc.psum_tensor(f"bank{i}", [128, 512], F32)) for i in range(4)]
        wide = [ctx.enter_context(nc.psum_tensor(f"wide{i}", [128, 2, 512], F32)) for i in range(2)]

        up = [bank[1], wide[0][:, 0, :]]

        slots_d = nc.dram_tensor("slots", [SLOTS, RW], F32, kind="Internal").ap()
        ycomb_d = nc.dram_tensor("ycomb", [DUMP + PADS * 128, C], F32, kind="Internal").ap()

        h = sb("h", [N, B, C])
        stats = sb("stats", [N, B, 6])
        mean = sb("mean", [N, B])
        rstd = sb("rstd", [N, B])
        shift = sb("shift", [N, B])
        lns = sb("lns", [N, 4, B])
        ident = sb("ident", [128, 128])
        mask = sb("mask", [KA, HC])
        ones = sb("ones", [128, 128])
        avg128 = sb("avg128", [128, 128])
        avgN = sb("avgN", [128, 1])
        xn = sb("xn", [N, 2, 2, C])
        xT = sb("xT", [KA, 2, 2, 2, N])

        def carver(name, size):
            place, taken = sb(name, [128, size]), [0]

            def carve(shape, again=False):
                if again:
                    taken[0] = 0
                n = int(np.prod(shape[1:]))
                at = taken[0]
                taken[0] += n
                assert taken[0] <= size, (name, taken[0])
                v = place[0:shape[0], at:at + n]
                names = " ".join(f"d{i}" for i in range(1, len(shape)))
                sizes = {f"d{i}": shape[i] for i in range(2, len(shape))}
                return v.rearrange(f"p ({names}) -> p {names}", **sizes) if len(shape) > 2 else v

            return carve

        rows = carver("rows", E0 * 2 * F0 + E0 * FT * C)
        X = rows([128, B, XW])
        w1 = rows([KA, E0, 2, F0], again=True)
        w2 = rows([128, E0, FT, C])
        rowbuf = rows([N, 2, 2 * TOPK, RW], again=True)
        fill = rows([128, PADS, RW])
        early = carver("early", E1 * 2 * (2 * I1 + C))
        inner = carver("inner", 12388)

        idx = sb("idx", [NW, B], I32)
        idxc = sb("idxc", [NW, B], I32)
        idxm = sb("idxm", [N, B], I32)
        dump = sb("dump", [128, PADS])
        keep = sb("keep", [N, 2, B])
        lnwb = early([128, 2, XW])
        convb = sb("convb", [128, 12])
        projT = early([128, 3, 2, C])
        convT = early([128, 3, 2, C])
        parts = early([128, 2, 3, 2, C])
        projb = early([ROWS, C])
        pos = early([ROWS, C])
        tokb = early([ROWS, C])
        tstat = early([128, B, 6])
        tsmall = early([128, 6, B])
        xg = early([128, 2, CHUNKS, ROWS])
        tok = early([ROWS, 2, C])

        watt = early([KA, 2, 3 * C])
        wattp = early([KA, 2, C])
        qT = sb("qT", [KA, 4, 2, 2 * N])
        kS = early([N, 2, 2, 2, KA])
        vS = early([N, 2, 2, 2, KA])
        kvs = early([KA, 2, 2, 2, HC + HH])
        rden = early([N, 2 * HEADS])
        on = early([N, 2, 2, 2, HC])
        oT = sb("oT", [KA, 2, 2, 2, N])

        wg0 = early([HC, 2, E0])
        wb2 = sb("wb2", [1, E0, C])
        gm = early([HC, 2, B])
        gprod = early([HC, 2, B, E0])
        gsm = early([128, 2, B, E0])
        gone = sb("gone", [128, 5, B])
        sel = sb("sel", [1, B], I32)
        hid = early([N, 2, F0])
        hT = early([128, 2, FT, N])

        wq = inner([KA, 2, C])
        wtok = inner([KA, 2, WTOK])
        wv = inner([KA, 2, C])
        wkn = inner([HC, 2, C])
        gam = inner([N, C])
        gam2 = inner([N, 2, C])
        gcol = inner([HC, 4])
        w1b = inner([KA, 2, HC])
        w1c = inner([KA, 2, HC])
        w1m = inner([KA, HEADS])
        wp = inner([KA, 2, C])
        zT = inner([HC, 2, 2 * N])
        kA = inner([N, 2, 2, 4, KA])
        dl = inner([N, 2, 2, C + HEADS])
        sig = inner([N, 2, 2 * HEADS])
        hv = inner([N, 4 * HEADS])
        irs = inner([N, 4 * HEADS])
        hw = inner([N, 4 * HEADS])
        sm = inner([N, 2, 5, 2 * HEADS])
        tc = inner([N, 3, 2 * HEADS])
        sq = inner([N, 2 * C])
        xh = inner([N, 2 * C])
        t1 = inner([N, 2 * C])
        gg = inner([N, 2 * C])
        pp = inner([N, 2 * C])
        xs = inner([N, 2 * C])
        zz = inner([N, 2, 2 * C])
        wn = inner([KA, 2, 2, 2, HC])
        zc = inner([N, 2 * C])
        zsq = inner([N, 2 * C])
        zh = inner([N, 2, 2 * C])

        m1 = early([KA, E1, 2, 2 * I1], again=True)
        m2 = early([KA, E1, 2, C])
        hot = inner([N, 2, 2 * TOPK, E1], again=True)
        taken = inner([N, 2, 2, E1])
        place = inner([N, 2 * E1])
        base = inner([128, E1])
        scale = sb("scale", [N, C])
        gate1 = sb("gate1", [KA, 2, E1])
        tri = sb("tri", [N, N])
        rr = inner([N, B])
        ts = inner([N, 2, 2, C])
        gs = inner([N, 2, 2, E1])
        m8 = inner([N, 2, 2, 8])
        i8 = sb("i8", [N, 2, 2, 8], U32)
        topf = inner([N, 2, 2 * TOPK])
        wraw = inner([N, 2, 2 * TOPK])
        wexp = inner([N, 2, 2 * TOPK])
        wsum = inner([N, 2, 2])
        rowf = inner([N, 2 * TOPK])
        iota = sb("iota", [128, E1 + 1])
        per_e = inner([128, 8, E1])
        per_ei = sb("per_ei", [128, 2, E1], I32)
        slot_s = sb("slot_s", [N, 2, 2 * TOPK], I32)
        pad_at = sb("pad_at", [1, E1], I32)
        block_f = inner([128, 4])
        target = sb("target", [N, B, TOPK])
        first_row = sb("first_row", [1, BLOCKS], I32)
        experts = sb("experts", [1, BLOCKS + 4])
        etab_f = sb("etab_f", [1, BLOCKS // 4])
        etab = sb("etab", [1, BLOCKS // 4], I32)
        xb = inner([128, 4, RW])
        weight = inner([128, 4, 1])
        al = inner([128, 2, 2 * I1])
        sg = inner([128, 2, I1])
        pr = inner([128, 2, I1])
        ac = inner([128, 2, I1])
        aT = inner([KA, 2, 2, 128])
        xTm = inner([KA, 2, 2, 128])
        ys = inner([128, 2, C])
        yc = inner([N, 4, 2, TOPK * C], again=True)
        ya = inner([N, 2, 2 * C])
        yb = inner([N, 2, C])
        yo = inner([N, 2, 2, C])
        dest = sb("dest", [128, 4, 1], I32)

        block = ctx.enter_context(nc.Block())

        def pad(eng, low, high):
            eng.wait_ge(S["pad_ready"], 1)
            with eng.Fori(low, high) as e:
                row = eng.value_load(pad_at[0:1, bass.ds(e, 1)])
                eng.dma_start(slots_d[bass.ds(row, 128), :], fill[:, bass.ds(e, 1), :].rearrange("p a w -> p (a w)"))\
                   .then_inc(S["padded"], 16)

        @block.sync
        def _(sp):
            sp.dma_start(idx[:, :], ids_d).then_inc(S["load_idx"], 16)
            sp.dma_start(idxm[:, :], idsm_d).then_inc(S["load_idx"], 16)
            sp.dma_start(dump[:, :], dump_d).then_inc(S["load_idx"], 16)
            for q in (0, 1):
                sp.dma_start(X[:, 8 * q:8 * q + 8, :], x_d[:, 8 * q:8 * q + 8, :]).then_inc(S["load_x0"], 16)
            for dst, src in ((convb[:], convb_d), (projT, projT_d), (lnwb, lnwb_d), (projb, projb_d), (pos, pos_d)):
                sp.dma_start(dst, src).then_inc(S["load_tok"], 16)
            for q in (2, 3):
                sp.dma_start(X[:, 8 * q:8 * q + 8, :], x_d[:, 8 * q:8 * q + 8, :]).then_inc(S["load_x1"], 16)
            for dst, src in ((ident[:], ident_d), (mask[:], mask_d), (watt, att_d), (wattp, attp_d)):
                sp.dma_start(dst, src).then_inc(S["load_att"], 16)

            for dst, src in ((wq, tq_d), (wtok, tk_d), (wv, tv_d), (wkn, tkn_d), (gam, tg_d), (gcol, tgc_d), (w1b, tw_d),
                             (wp, tp_d)):
                sp.dma_start(dst, src).then_inc(S["load_ttt"], 16)

            def put(g, slot, count):
                sp.wait_ge(S["tok_sum"], g + 1)
                for j in range(count):
                    sp.dma_start(h[0:NI, bass.ds(g * GRP + j, 1), :], tok[NI * j:NI * j + NI, slot, :])\
                      .then_inc(S[f"tok_piece{slot}"], 16)

            with sp.Fori(0, 5) as turn:
                put(turn * 2, 0, GRP)
                put(turn * 2 + 1, 1, GRP)
            put(10, 0, 2)
            sp.wait_ge(S["tok_xg"], 11)
            for dst, src in ((wg0, gate0_d), (w1, f1_d), (w2, f2_d), (wb2[:], fb2_d)):
                sp.dma_start(dst, src).then_inc(S["load_ffn"], 16)
            sp.wait_ge(S["filled"], 1)
            with sp.Fori(0, SPARE // 2) as turn:
                sp.dma_start(slots_d[bass.ds(turn * 256 + E1 * CAP, 256), :].rearrange("(j p) w -> p j w", p=128),
                             fill[:, E1:PADS, :]).then_inc(S["filled"], 16)
            sp.wait_ge(S["ffn_stat"], B)
            for dst, src in ((m1, m1_d), (m2, m2_d), (scale[:], scale_d), (gate1[:], gate1_d), (tri[:], tri_d),
                             (iota[:], iota_d), (target[:], target_d)):
                sp.dma_start(dst, src).then_inc(S["load_moe"], 16)

            pad(sp, 0, E1 // 2)

            sp.wait_ge(S["rt_done"], 1)
            sp.wait_ge(S["dispatched0"], 16 * 2 * TOPK * PAIRS // 2)
            sp.wait_ge(S["dispatched1"], 16 * 2 * TOPK * PAIRS // 2)
            sp.wait_ge(S["padded"], 16 * E1)
            sp.wait_ge(S["filled"], 1 + 16 * (SPARE // 2))

            def load_block(turn, j):
                n, slot, _ = at(turn, j)
                when(sp, S["moe_al"], n - 3)
                row = sp.value_load(first_row[0:1, bass.ds(n, 1)])
                sp.dma_start(xb[:, slot, :], slots_d[bass.ds(row, 128), :]).then_inc(S[f"loaded{slot}"], 16)

            over_blocks(sp, load_block)

            sp.wait_ge(S["moe_out0"], 16 * BLOCKS // 2)
            sp.wait_ge(S["moe_out1"], 16 * BLOCKS // 2)

            def load_choices(turn, j):
                t, slot, _ = at(turn, j)
                when(sp, S["fin_a"], t - 3)
                sp.dma_start(yc[:, slot], ycomb_d[bass.ds(t * (2 * N * TOPK), 2 * N * TOPK), :]
                             .rearrange("(i p k) c -> p i (k c)", i=2, k=TOPK)).then_inc(S[f"loaded{slot}"], 16)

            over_fours(sp, load_choices, PAIRS)
            sp.wait_ge(S["stored0"], 16 * PAIRS // 2)
            sp.wait_ge(S["stored1"], 16 * PAIRS // 2)

        @block.gpsimd
        def _(pool):
            def gather(b):
                nc.gpsimd.indirect_dma_start(
                    out=h[NI:N, b, :], out_offset=None, in_=table_d,
                    in_offset=bass.IndirectOffsetOnAxis(ap=idxc[:, b:b + 1], axis=0)).then_inc(S["gathered"], 16)

            pool.wait_ge(S["clipped"], 1)
            for b in range(B // 4):
                gather(b)
            pool.wait_ge(S["tok_prod"], 1)
            for o in (1, 2):
                nc.gpsimd.tensor_tensor(convT[:, :, :, :], convT[:, :, :, :], parts[:, o - 1], ALU.add)\
                    .then_inc(S["tok_bias0"], 1)
                pool.wait_ge(S["tok_bias0"], o)
            for b in range(B // 4, B):
                gather(b)
            G = nc.gpsimd
            pool.wait_ge(S["load_idx"], 48)
            pool.wait_ge(S["ffn_stat"], B)
            G.memset(fill[:, :, 0:C], 0.0)
            G.memset(fill[:, :, C + 1:RW], 0.0)
            G.tensor_copy(fill[:, :, C], dump[:, :]).then_inc(S["filled"], 1)


            def heads(v):
                return v.rearrange("p (a d) -> p a d", d=HD)

            def per_head(v):
                return v.rearrange("p (a d) -> p a d", d=1).broadcast_to([N, 2 * HEADS, HD])

            def ttt_sum(t, slot):
                pool.wait_ge(S["ttt_oT"], t + 1)
                when(pool, S["ttt_out"], t - 1)
                G.tensor_tensor(oT[0:HC, slot % 2].rearrange("p h i n -> p h (i n)"), zT[:, :, :],
                                qT[0:HC, slot % 4, :, :], ALU.add).then_inc(S["ttt_sum"], 1)

            def ttt(t, slot):
                s_ = sm[:, slot % 2]
                step = S["pool_inner"]
                pool.wait_ge(S["ttt_sig"], t + 1)
                pool.wait_ge(S["ttt_rstd"], t + 1)
                G.tensor_tensor(s_[:, 2, :], irs[:, 0:2 * HEADS], tc[:, 1, :], ALU.mult).then_inc(step, 1)
                pool.wait_ge(step, 3 * t + 1)
                G.tensor_tensor(s_[:, 2, :], s_[:, 2, :], sig[:, slot % 2, :], ALU.mult).then_inc(S["ttt_r"], 1)
                pool.wait_ge(S["ttt_xh"], t + 1)
                G.tensor_tensor(t1[:, :], xh[:, :], gam2[:, :, :].rearrange("p i c -> p (i c)"), ALU.mult)\
                 .then_inc(S["ttt_t1"], 1)
                pool.wait_ge(S["ttt_s"], t + 1)
                pool.wait_ge(S["ttt_r"], t + 1)
                G.tensor_tensor(s_[:, 3, :], s_[:, 3, :], tc[:, 2, :], ALU.mult).then_inc(step, 1)
                pool.wait_ge(step, 3 * t + 2)
                G.tensor_tensor(s_[:, 3, :], s_[:, 3, :], s_[:, 2, :], ALU.mult).then_inc(step, 1)
                pool.wait_ge(step, 3 * t + 3)
                when(pool, S["ttt_zz"], t)
                G.tensor_tensor(heads(xs[:, :]), heads(xh[:, :]), per_head(s_[:, 3, :]), ALU.mult)\
                 .then_inc(S["ttt_xs"], 1)
                if not first(t):
                    ttt_sum(t - 1, slot - 1)

            over_pairs(pool, ttt, 4)
            ttt_sum(PAIRS - 1, 3)

            def dispatch(turn, j):
                t, slot, _ = at_two(turn, j)
                pool.wait_ge(S["row_t"], t + 1)
                pool.wait_ge(S["row_meta"], t + 1)
                pool.sem_inc(S["going"], 1)
                for k in range(2 * TOPK):
                    G.indirect_dma_start(
                        out=slots_d, out_offset=bass.IndirectOffsetOnAxis(ap=slot_s[:, slot, k:k + 1], axis=0),
                        in_=rowbuf[:, slot, k, :], in_offset=None).then_inc(S[f"dispatched{slot}"], 16)

            over_twos(pool, dispatch, PAIRS)
            def send_back(turn, j):
                n, slot, _ = at(turn, j)
                pool.wait_ge(S["moe_ys"], n + 1)
                pool.sem_inc(S["going"], 1)
                G.indirect_dma_start(
                    out=ycomb_d, out_offset=bass.IndirectOffsetOnAxis(ap=dest[:, slot, :], axis=0),
                    in_=ys[:, slot % 2, :], in_offset=None).then_inc(S[f"moe_out{slot % 2}"], 16)

            def moe(turn, j):
                n, slot, _ = at(turn, j)
                pool.wait_ge(S["moe_p"], n + 1)
                pool.wait_ge(S["moe_sig"], n + 1)
                when(pool, S["moe_aT"], n - 1)
                G.tensor_tensor(ac[:, slot % 2, :], pr[:, slot % 2, :], sg[:, slot % 2, :], ALU.mult)\
                 .then_inc(S["moe_act"], 1)
                if not (first(turn) and j < 2):
                    send_back(turn, j - 2)

            over_blocks(pool, moe)
            send_back(BLOCKS // 4 - 1, 2)
            send_back(BLOCKS // 4 - 1, 3)


        @block.scalar
        def _(act):
            act.wait_ge(S["const_ready"], 1)
            act.wait_ge(S["load_tok"], 80)
            for o in range(3):
                for c in range(3):
                    ins = nc.scalar.activation(convT[:, c] if o == 0 else parts[:, o - 1, c], projT[:, o], ACT.Identity,
                                               scale=convb[:, 3 * o + c:3 * o + c + 1])
            ins.then_inc(S["tok_prod"], 1)
            for j in range(GRP):
                nc.scalar.copy(xg[:, 1, :, j * NI:j * NI + NI], lnwb[:, 1, :].rearrange("p (k l) -> p k l", k=CHUNKS))
            for k in range(CHUNKS):
                ins = nc.scalar.activation(xg[:, 0, k, :], ones[:, 0:ROWS], ACT.Identity,
                                           scale=convb[:, 9 + k // 2:10 + k // 2])
            ins.then_inc(S["tok_w"], 1)

            act.wait_ge(S["tok_rstd"], 1)

            def patch_normalise(g, count):
                for j in range(count):
                    b = g * GRP + j
                    v = X[:, bass.ds(b, 1), :].rearrange("p a w -> p (a w)")
                    ins = nc.scalar.activation(v, v, ACT.Identity, bias=tsmall[:, 0, bass.ds(b, 1)],
                                               scale=tsmall[:, 5, bass.ds(b, 1)])
                ins.then_inc(S["tok_norm"], 1)

            with act.Fori(0, 10) as g:
                patch_normalise(g, GRP)
            patch_normalise(10, 2)

            act.wait_ge(S["mask"], 3)
            act.wait_ge(S["tok_piece0"], 16 * (5 * GRP + 2))
            act.wait_ge(S["tok_piece1"], 16 * 5 * GRP)
            act.wait_ge(S["gathered"], 16 * B)
            with act.Fori(0, B // 4) as turn:
                for j in (1, 3):
                    b = turn * 4 + j
                    v = h[:, bass.ds(b, 1), :].rearrange("p a c -> p (a c)")
                    ins = nc.scalar.activation(v, v, ACT.Identity, scale=keep[:, 0, bass.ds(b, 1)])
                ins.then_inc(S["masked_odd"], 1)

            act.wait_ge(S["load_att"], 64)

            def normalise(t, slot, sem):
                for i in range(2):
                    b = t * 2 + i
                    ins = nc.scalar.activation(xn[:, slot, i, :], h[:, bass.ds(b, 1), :].rearrange("p a c -> p (a c)"),
                                               ACT.Identity, bias=shift[:, bass.ds(b, 1)], scale=rstd[:, bass.ds(b, 1)])
                ins.then_inc(sem, 1)

            act.wait_ge(S["ln_ready"], 1)
            normalise(0, 0, S["att_xn"])
            normalise(1, 1, S["att_xn"])

            def att_xT(t, slot):
                act.wait_ge(S["att_xT"], t + 1)
                when(act, S["att_q"], t - 1)
                nc.scalar.copy(xT[0:HC, slot].rearrange("p h i n -> p (h i n)"), bank[0][0:HC, 0:4 * N])\
                    .then_inc(S["att_xTs"], 1)

            def attention(t, slot):
                act.wait_ge(S["att_ks"], t + 1)
                when(act, S["att_prod"], t - 1)
                nc.scalar.copy(vS[:, slot, :, :, 0:HC].rearrange("p i h c -> p i h c"),
                               wide[0][0:N, :, C:2 * C].rearrange("p i (h c) -> p i h c", h=2))\
                    .then_inc(S["att_vs"], 1)
                if not last(t, PAIRS):
                    att_xT(t + 1, 1 - slot)
                if not first(t):
                    att_oT(t - 1, 1 - slot)
                if not (isinstance(t, int) and t + 2 >= PAIRS):
                    normalise(t + 2, slot, S["att_xn"])

            def att_oT(t, slot):
                act.wait_ge(S["att_oTp"], t + 1)
                when(act, S["att_out"], t - 1)
                nc.scalar.copy(oT[0:HC, slot].rearrange("p h i n -> p (h i n)"), wide[1][0:HC, 1, 0:4 * N])\
                    .then_inc(S["att_oT"], 1)

            att_xT(0, 0)
            over_pairs(act, attention)
            att_oT(PAIRS - 1, 1)

            act.wait_ge(S["ln_ready"], 2)

            def gate0(t, slot):
                when(act, S["gate0_mean"], t - 1)
                if not (isinstance(t, int) and t < 2):
                    act.sem_inc(S["going_act"], 1)
                normalise(t, slot, S["gate0_xn"])

            over_pairs(act, gate0)
            act.wait_ge(S["gate0_step"], 1)
            nc.scalar.activation(gsm[:, 1].rearrange("p b e -> p (b e)"), gsm[:, 0].rearrange("p b e -> p (b e)"),
                                 ACT.Exp).then_inc(S["gate0_exp"], 1)

            def ffn_xT(t, slot):
                act.wait_ge(S["ffn_xT"], t + 1)
                when(act, S["ffn_hid"], 2 * t - 2)
                nc.scalar.copy(xT[0:HC, slot].rearrange("p h i n -> p (h i n)"), bank[0][0:HC, 0:4 * N])\
                    .then_inc(S["ffn_xTs"], 1)

            def ffn_hT(u, i):
                act.wait_ge(S["ffn_hT"], u + 1)
                when(act, S["ffn_y"], u - 1)
                nc.scalar.copy(hT[:, i, 3:6, :], bank[2][:, 0:3 * N].rearrange("p (k n) -> p k n", k=3))\
                    .then_inc(S["ffn_hTa"], 1)

            def ffn(t, slot):
                for i in range(2):
                    u = t * 2 + i
                    if not first(u):
                        ffn_hT(u - 1, 1 - i)
                    act.wait_ge(S["ffn_hid"], u + 1)
                    when(act, S["ffn_hT"], u - 1)
                    for n in range(2):
                        ins = nc.scalar.activation(hid[:, i, 384 * n:384 * n + 384], wide[i][0:N, n, 0:384], ACT.Gelu)
                    ins.then_inc(S["ffn_gelu"], 1)
                    if i == 0 and not (isinstance(t, int) and t == PAIRS - 1):
                        ffn_xT(t + 1, 1 - slot)

            ffn_xT(0, 0)
            over_pairs(act, ffn)
            ffn_hT(B - 1, 1)

            def ttt_xT(t, slot):
                act.wait_ge(S["ttt_xT"], t + 1)
                when(act, S["ttt_tok"], t - 1)
                nc.scalar.copy(xT[0:HC, slot % 2].rearrange("p h i n -> p (h i n)"), bank[0][0:HC, 0:4 * N])\
                    .then_inc(S["ttt_xTs"], 1)

            def ttt_q(t, slot):
                act.wait_ge(S["ttt_q"], t + 1)
                when(act, S["ttt_out"], t - 3)
                nc.scalar.copy(qT[0:HC, slot % 4].rearrange("p h n -> p (h n)"), bank[1][0:HC, 0:4 * N])\
                    .then_inc(S["ttt_qs"], 1)

            def ttt_tok(t, slot):
                act.wait_ge(S["ttt_tok"], t + 1)
                when(act, S["ttt_grad"], t - 1)
                when(act, S["ttt_xh"], t - 1)
                when(act, S["ttt_sq"], t - 1)
                nc.scalar.copy(kA[:, slot % 2, :, :, 0:HC], wide[0][0:N, :, 0:2 * C].rearrange("p i (a c) -> p i a c", a=4))\
                    .then_inc(S["ttt_kA"], 1)
                when(act, S["ttt_g"], t - 1)
                when(act, S["ttt_sig"], t - 1)
                nc.scalar.copy(dl[:, slot % 2], bank[3][0:N, 0:2 * (C + HEADS)].rearrange("p (i c) -> p i c", i=2))\
                    .then_inc(S["ttt_dl"], 1)
                act.wait_ge(S["ttt_kA"], t + 1)
                when(act, S["ttt_v"], t)
                nc.scalar.activation(sq[:, :].rearrange("p (i a c) -> p i a c", i=2, a=2), kA[:, slot % 2, :, 2:4, 0:HC],
                                     ACT.Square, scale=HD ** -0.5)\
                    .then_inc(S["ttt_sq"], 1)
                act.wait_ge(S["ttt_dl"], t + 1)
                when(act, S["ttt_r"], t - 1)
                nc.scalar.activation(sig[:, slot % 2, :].rearrange("p (i a) -> p i a", i=2),
                                     dl[:, slot % 2, :, C:C + HEADS], ACT.Sigmoid).then_inc(S["ttt_sig"], 1)

            def ttt_oT(t, slot):
                act.wait_ge(S["ttt_zT"], t + 1)
                when(act, S["ttt_sum"], t)
                for k in range(2):
                    ins = nc.scalar.activation(zT[:, k, :], bank[0][0:HC, 2 * k * N:2 * (k + 1) * N], ACT.Identity,
                                               scale=gcol[:, k:k + 1])
                ins.then_inc(S["ttt_oT"], 1)

            def ttt_zsq(t):
                act.wait_ge(S["ttt_zc"], t + 1)
                when(act, S["ttt_zv"], t)
                nc.scalar.activation(zsq[:, :], zc[:, :], ACT.Square, scale=HD ** -0.5).then_inc(S["ttt_zsq"], 1)

            def ttt(t, slot):
                fixed = isinstance(t, int)
                if not (fixed and t >= PAIRS - 2):
                    ttt_xT(t + 2, slot + 2)
                if not (fixed and t == 0):
                    ttt_zsq(t - 1)
                if not (fixed and t == PAIRS - 1):
                    ttt_q(t + 1, slot + 1)
                if not (fixed and t >= PAIRS - 3):
                    normalise(t + 3, (slot + 3) % 2, S["ttt_xn"])
                if not (fixed and t == PAIRS - 1):
                    ttt_tok(t + 1, slot + 1)
                if not (fixed and t == 0):
                    ttt_oT(t - 1, slot - 1)

            act.wait_ge(S["ln_ready"], 3)
            normalise(0, 0, S["ttt_xn"])
            normalise(1, 1, S["ttt_xn"])
            ttt_xT(0, 0)
            normalise(2, 0, S["ttt_xn"])
            ttt_q(0, 0)
            ttt_tok(0, 0)
            ttt_xT(1, 1)
            over_pairs(act, ttt, 4)
            ttt_zsq(PAIRS - 1)
            ttt_oT(PAIRS - 1, 3)

            def rt_copy(turn, j):
                t, slot, _ = at_two(turn, j)
                act.wait_ge(S["rt_tT"], t + 1)
                when(act, S["rt_logit"], t - 1)
                nc.scalar.copy(xT[0:HC, slot].rearrange("p h i n -> p (h i n)"), bank[0][0:HC, 0:4 * N])\
                    .then_inc(S["rt_tTs"], 1)

            def rt_exp(turn, j):
                t, slot, _ = at_two(turn, j)
                act.wait_ge(S["rt_less"], t + 1)
                when(act, S["row_meta"], t - 1)
                nc.scalar.activation(wexp[:, slot, :], wraw[:, slot, :], ACT.Exp).then_inc(S["rt_exp"], 1)

            def rt_rows(turn, j):
                t, slot, half = at_two(turn, j)
                when(act, S[f"dispatched{slot}"], 16 * 2 * TOPK * half)
                for i in range(2):
                    ins = nc.scalar.copy(rowbuf[:, slot, TOPK * i:TOPK * (i + 1), 0:C],
                                         ts[:, slot, i:i + 1, :].broadcast_to([N, TOPK, C]))
                ins.then_inc(S["row_t"], 1)

            def route(turn, j):
                if not (last(turn, PAIRS // 2) and j == 1):
                    rt_copy(turn, j + 1)
                rt_exp(turn, j)
                rt_rows(turn, j)

            rt_copy(0, 0)
            over_twos(act, route, PAIRS)
            pad(act, E1 // 2, E1)

            def moe_xTs(turn, j):
                n, slot, _ = at(turn, j)
                act.wait_ge(S["moe_xT"], n + 1)
                when(act, S["moe_h"], n - 1)
                nc.scalar.copy(xTm[0:HC, slot % 2].rearrange("p h n -> p (h n)"), bank[0][0:HC, 0:256])\
                    .then_inc(S["moe_xTs"], 1)

            def moe_sigmoid(turn, j):
                n, slot, _ = at(turn, j)
                act.wait_ge(S["moe_al"], n + 1)
                when(act, S["moe_act"], n - 1)
                nc.scalar.activation(sg[:, slot % 2, :], al[:, slot % 2, 0:I1], ACT.Sigmoid, scale=ALPHA)\
                    .then_inc(S["moe_sig"], 1)

            def moe_aTs(turn, j):
                n, slot, _ = at(turn, j)
                act.wait_ge(S["moe_aT"], n + 1)
                when(act, S["moe_y"], n - 1)
                nc.scalar.copy(aT[0:HC, slot % 2].rearrange("p h n -> p (h n)"), bank[2][0:HC, 0:256])\
                    .then_inc(S["moe_aTs"], 1)

            def moe(turn, j):
                if not (last(turn, BLOCKS // 4) and j == 3):
                    moe_xTs(turn, j + 1)
                moe_sigmoid(turn, j)
                if not (first(turn) and j == 0):
                    moe_aTs(turn, j - 1)

            moe_xTs(0, 0)
            over_blocks(act, moe)
            moe_aTs(BLOCKS // 4 - 1, 3)

            def store(turn, j):
                t, slot, _ = at(turn, j)
                act.wait_ge(S["fin_c"], t + 1)
                act.dma_start(out_d[bass.ds(t * 2, 2), :, :].rearrange("i n c -> n i c"), yo[:, slot % 2])\
                   .then_inc(S[f"stored{slot % 2}"], 16)

            over_fours(act, store, PAIRS)

        @block.tensor
        def _(pe):
            pe.wait_ge(S["const_ready"], 1)
            pe.wait_ge(S["tok_stat"], 1)
            pe.matmul(bank[0][:, 0:B], avg128[:, :], tsmall[:, 0, :], start=True, stop=True).then_inc(S["tok_mean"], 1)
            pe.wait_ge(S["tok_varsum"], 1)
            pe.matmul(bank[1][:, 0:B], avg128[:, :], tsmall[:, 3, :], start=True, stop=True).then_inc(S["tok_devavg"], 1)
            pe.wait_ge(S["tok_w"], 1)
            pe.wait_ge(S["tok_bias0"], 2)
            for k in range(CHUNKS):
                pe.matmul(bank[2][0:ROWS, 0:C], xg[:, 1, k, :], convT[:, k // 2, k % 2, :],
                          start=(k == 0), stop=False)
            for k in range(CHUNKS):
                ins = pe.matmul(bank[2][0:ROWS, 0:C], xg[:, 0, k, :], projT[:, k // 2, k % 2, :],
                                start=False, stop=(k == CHUNKS - 1))
            ins.then_inc(S["tok_bias_mm"], 1)

            def patches(g, slot, count):
                pe.wait_ge(S["tok_xg"], g + 1)
                when(pe, S["tok_sum"], g - 1)
                for k in range(CHUNKS):
                    ins = pe.matmul(bank[slot][0:NI * count, 0:C], xg[:, slot, k, 0:NI * count],
                                    convT[:, k // 2, k % 2, :], start=(k == 0), stop=(k == CHUNKS - 1))
                ins.then_inc(S["tok_mm"], 1)

            patches(0, 0, GRP)
            patches(1, 1, GRP)
            with pe.Fori(1, 5) as turn:
                patches(turn * 2, 0, GRP)
                patches(turn * 2 + 1, 1, GRP)
            patches(10, 0, 2)

            def turn_rows(slot, xn_ready, count, psum_free, n_free, done):
                pe.wait_ge(xn_ready, count)
                when(pe, psum_free, n_free)
                for i in range(2):
                    for k in range(2):
                        ins = pe.transpose(bank[0][0:HC, (2 * k + i) * N:(2 * k + i + 1) * N],
                                           xn[:, slot, i, k * HC:k * HC + HC], ident[0:N, 0:N])
                ins.then_inc(done, 1)

            pe.wait_ge(S["load_att"], 64)
            pe.wait_ge(S["tok_sum"], 11)

            def att_turn(t, slot):
                turn_rows(slot, S["att_xn"], t + 1, S["att_xTs"], t, S["att_xT"])

            def att_weights(t, slot):
                pe.wait_ge(S["att_xTs"], t + 1)
                when(pe, S["att_ks"], t)
                when(pe, S["att_vs"], t)
                for i in range(2):
                    for k in range(2):
                        ins = pe.matmul(wide[0][0:N, i, 0:2 * C], xT[0:HC, slot, k, i, :], watt[0:HC, k, C:3 * C],
                                        start=(k == 0), stop=(k == 1))
                ins.then_inc(S["att_kv"], 1)
                when(pe, S["att_qs"], t)
                for m in range(2):
                    for k in range(2):
                        ins = pe.matmul(bank[1][0:HC, m * 2 * N:(m + 1) * 2 * N], watt[0:HC, k, m * HC:m * HC + HC],
                                        xT[0:HC, slot, k].rearrange("p i n -> p (i n)"), start=(k == 0), stop=(k == 1))
                ins.then_inc(S["att_q"], 1)

            def att_product(t, slot):
                pe.wait_ge(S["att_ks"], t + 1)
                pe.wait_ge(S["att_vs"], t + 1)
                when(pe, S["att_ksm"], t)
                for i in range(2):
                    for k in range(2):
                        ins = pe.matmul(bank[2][0:HC, (2 * i + k) * KA:(2 * i + k + 1) * KA], kS[:, slot, i, k, 0:HC],
                                        vS[:, slot, i, k, :], start=True, stop=True)
                ins.then_inc(S["att_prod"], 1)

            def att_fraction(t, slot):
                pe.wait_ge(S["att_qs"], t + 1)
                pe.wait_ge(S["att_ksm"], t + 1)
                when(pe, S["att_on"], t)
                for i in range(2):
                    for k in range(2):
                        a = (2 * i + k) * (HC + HH)
                        ins = pe.matmul(wide[1][0:N, 0, a:a + HC + HH], qT[:, slot, k, i * N:i * N + N],
                                        kvs[:, slot, i, k, :], start=True, stop=True)
                ins.then_inc(S["att_frac"], 1)

            def att_turn_back(t, slot):
                pe.wait_ge(S["att_on"], t + 1)
                when(pe, S["att_oT"], t)
                for k in range(2):
                    for i in range(2):
                        ins = pe.transpose(wide[1][0:HC, 1, (2 * k + i) * N:(2 * k + i + 1) * N], on[:, slot, i, k, :],
                                           ident[0:N, 0:N])
                ins.then_inc(S["att_oTp"], 1)

            def att_project(t, slot):
                pe.wait_ge(S["att_oT"], t + 1)
                when(pe, S["att_h"], t)
                for i in range(2):
                    for k in range(2):
                        rows = KA if k == 0 else HC
                        ins = pe.matmul(bank[3][0:N, i * C:i * C + C], oT[0:rows, slot, k, i, :], wattp[0:rows, k, :],
                                        start=(k == 0), stop=(k == 1))
                ins.then_inc(S["att_out"], 1)

            def attention(t, slot):
                att_weights(t, slot)
                first = isinstance(t, int) and t == 0
                if not first:
                    att_fraction(t - 1, 1 - slot)
                if not last(t, PAIRS):
                    att_turn(t + 1, 1 - slot)
                if not (isinstance(t, int) and t < 2):
                    att_project(t - 2, slot)
                att_product(t, slot)
                if not first:
                    att_turn_back(t - 1, 1 - slot)

            att_turn(0, 0)
            over_pairs(pe, attention)
            att_fraction(PAIRS - 1, 1)
            att_project(PAIRS - 2, 0)
            att_turn_back(PAIRS - 1, 1)
            att_project(PAIRS - 1, 1)

            pe.wait_ge(S["att_h"], PAIRS)
            pe.wait_ge(S["att_qs"], PAIRS)

            def gate0(t, slot):
                pe.wait_ge(S["gate0_xn"], t + 1)
                for i in range(2):
                    for k in range(2):
                        ins = pe.matmul(bank[1][0:HC, bass.ds(t * 2 + (i + B * k), 1)],
                                        xn[:, slot, i, k * HC:k * HC + HC], avgN[0:N, :], start=True, stop=True)
                ins.then_inc(S["gate0_mean"], 1)

            over_pairs(pe, gate0)
            pe.wait_ge(S["load_ttt"], 128)
            pe.wait_ge(S["tw_cent"], 1)
            for k in range(2):
                for m in range(2):
                    pe.matmul(bank[3][0:HC, (2 * k + m) * HC:(2 * k + m + 1) * HC], wkn[:, m, k * HC:k * HC + HC],
                              w1c[0:HC, m, :], start=True, stop=True)
            for k in range(2):
                ins = pe.matmul(bank[0][HC:KA, 0:C], gcol[:, 2 + k:3 + k], wp[0:HC, k, :], start=(k == 0), stop=(k == 1))
            ins.then_inc(S["tw_comp"], 1)
            pe.wait_ge(S["gate0_prod"], 1)
            for k in range(2):
                ins = pe.matmul(bank[2][:, 0:B * E0], ones[0:HC, :], gprod[:, k].rearrange("p b e -> p (b e)"),
                                start=(k == 0), stop=(k == 1))
            ins.then_inc(S["gate0_logit"], 1)

            pe.wait_ge(S["load_ffn"], 64)
            pe.wait_ge(S["gate0_ready"], 1)

            def ffn_turn(t, slot):
                turn_rows(slot, S["ffn_xn"], t + 1, S["ffn_xTs"], t, S["ffn_xT"])

            def ffn_up(slot, i, n, e):
                for k in range(2):
                    rows = KA if k == 0 else HC
                    ins = pe.matmul(wide[i][0:N, n, 0:384], xT[0:rows, slot, k, i, :],
                                    w1[0:rows, bass.ds(e, 1), k, 384 * n:384 * n + 384], start=(k == 0), stop=(k == 1))
                return ins

            def ffn_transpose(u, i):
                pe.wait_ge(S["ffn_gelu"], u + 1)
                when(pe, S["ffn_hTv"], u)
                when(pe, S["ffn_hTa"], u)
                for k in range(FT):
                    ins = pe.transpose(bank[1 + k // 3][:, (k % 3) * N:(k % 3 + 1) * N], hid[:, i, 128 * k:128 * k + 128],
                                       ident[0:N, 0:N])
                ins.then_inc(S["ffn_hT"], 1)

            def ffn_down(u, i, e):
                pe.wait_ge(S["ffn_hTv"], u + 1)
                pe.wait_ge(S["ffn_hTa"], u + 1)
                when(pe, S["ffn_h"], u)
                for k in range(FT):
                    pe.matmul(bank[3][0:N, i * 256:i * 256 + C], hT[:, i, k, :], w2[:, bass.ds(e, 1), k, :],
                              start=(k == 0), stop=False)
                pe.matmul(bank[3][0:N, i * 256:i * 256 + C], ones[0:1, 0:N], wb2[0:1, bass.ds(e, 1), :],
                          start=False, stop=True).then_inc(S["ffn_y"], 1)

            def ffn(t, slot):
                pe.wait_ge(S["ffn_xTs"], t + 1)
                for i in range(2):
                    u = t * 2 + i
                    lag = not (isinstance(u, int) and u == 0)
                    e = pe.value_load(sel[0:1, bass.ds(u, 1)])
                    when(pe, S["ffn_gelu"], u - 1)
                    ffn_up(slot, i, 0, e)
                    if lag:
                        ffn_transpose(u - 1, 1 - i)
                    ffn_up(slot, i, 1, e).then_inc(S["ffn_hid"], 1)
                    if lag:
                        ffn_down(u - 1, 1 - i, pe.value_load(sel[0:1, bass.ds(u - 1, 1)]))
                    if i == 0 and not (isinstance(t, int) and t == PAIRS - 1):
                        ffn_turn(t + 1, 1 - slot)

            ffn_turn(0, 0)
            pe.wait_ge(S["tw_done"], 1)
            over_pairs(pe, ffn)
            ffn_transpose(B - 1, 1)
            ffn_down(B - 1, 1, pe.value_load(sel[0:1, B - 1:B]))


            def ttt_turn(t, slot):
                pe.wait_ge(S["ttt_xn"], t + 1)
                when(pe, S["ttt_oT"], t - 3)
                if isinstance(t, int):
                    when(pe, S["ttt_xTs"], t)
                for i in range(2):
                    for k in range(2):
                        ins = pe.transpose(bank[0][0:HC, (2 * k + i) * N:(2 * k + i + 1) * N],
                                           xn[:, slot % 2, i, k * HC:k * HC + HC], ident[0:N, 0:N])
                ins.then_inc(S["ttt_xT"], 1)

            def ttt_query(t, slot):
                pe.wait_ge(S["ttt_xTs"], t + 1)
                when(pe, S["ttt_qs"], t)
                for m in range(2):
                    for k in range(2):
                        rows = KA if k == 0 else HC
                        ins = pe.matmul(bank[1][0:HC, m * 2 * N:(m + 1) * 2 * N], wq[0:rows, k, m * HC:m * HC + HC],
                                        xT[0:rows, slot % 2, k].rearrange("p i n -> p (i n)"),
                                        start=(k == 0), stop=(k == 1))
                ins.then_inc(S["ttt_q"], 1)

            def ttt_token(t, slot):
                when(pe, S["ttt_kA"], t)
                when(pe, S["ttt_dl"], t)
                for i in range(2):
                    for k in range(2):
                        rows = KA if k == 0 else HC
                        x_ = xT[0:rows, slot % 2, k, i, :]
                        pe.matmul(wide[0][0:N, i, 0:2 * C], x_, wtok[0:rows, k, 0:2 * C], start=(k == 0), stop=(k == 1))
                    for k in range(2):
                        rows = KA if k == 0 else HC
                        x_ = xT[0:rows, slot % 2, k, i, :]
                        ins = pe.matmul(bank[3][0:N, i * (C + HEADS):(i + 1) * (C + HEADS)], x_, wtok[0:rows, k, 2 * C:WTOK],
                                        start=(k == 0), stop=(k == 1))
                ins.then_inc(S["ttt_tok"], 1)

            def ttt_grad(t, slot):
                when(pe, S["ttt_w"], t)
                pe.matmul(bank[2][0:KA, 0:4 * HC].rearrange("p (i c) -> p i c", i=2), ident[0:KA, 0:KA],
                          w1b[:, :, :].rearrange("p (a m) c -> p a (m c)", a=1).broadcast_to([KA, 2, C]),
                          start=True, stop=False)
                pe.wait_ge(S["ttt_zz"], t + 1)
                for a in range(4):
                    ins = pe.matmul(bank[2][0:KA, a * HC:a * HC + HC], kA[:, slot % 2, a // 2, a % 2, :],
                                    zz[:, slot % 2, a * HC:a * HC + HC], start=False, stop=(a == 3))
                ins.then_inc(S["ttt_grad"], 1)

            def ttt_updated(t, slot):
                pe.wait_ge(S["ttt_w"], t + 1)
                pe.wait_ge(S["ttt_qs"], t + 1)
                when(pe, S["ttt_zc"], t)
                for i in range(2):
                    for k in range(2):
                        a = 2 * i + k
                        ins = pe.matmul(wide[1][0:N, 0, a * HC:a * HC + HC], qT[:, slot % 4, k, i * N:i * N + N],
                                        wn[:, slot % 2, i, k, :], start=True, stop=True)
                ins.then_inc(S["ttt_zb"], 1)

            def ttt_turn_back(t, slot):
                pe.wait_ge(S["ttt_zh"], t + 1)
                pe.wait_ge(S["ttt_xTs"], min(t + 4, PAIRS) if isinstance(t, int) else t + 4)
                for i in range(2):
                    for k in range(2):
                        a = 2 * i + k
                        ins = pe.transpose(bank[0][0:HC, (2 * k + i) * N:(2 * k + i + 1) * N],
                                           zh[:, slot % 2, a * HC:a * HC + HC], ident[0:N, 0:N])
                ins.then_inc(S["ttt_zT"], 1)

            def ttt_project(t, slot):
                pe.wait_ge(S["ttt_sum"], t + 1)
                when(pe, S["ttt_h"], t)
                for i in range(2):
                    for k in range(2):
                        rows = KA if k == 0 else HC
                        ins = pe.matmul(wide[1][0:N, 1, i * C:i * C + C], oT[0:rows, slot % 2, k, i, :], wp[0:rows, k, :],
                                        start=(k == 0), stop=(k == 1))
                ins.then_inc(S["ttt_out"], 1)

            def ttt(t, slot):
                fixed = isinstance(t, int)
                before, after = not (fixed and t == 0), not (fixed and t == PAIRS - 1)
                if before:
                    ttt_grad(t - 1, slot - 1)
                if not (fixed and t >= PAIRS - 2):
                    ttt_turn(t + 2, slot + 2)
                if before:
                    ttt_updated(t - 1, slot - 1)
                if not (fixed and t < 2):
                    ttt_project(t - 2, slot - 2)
                if after:
                    ttt_query(t + 1, slot + 1)
                    ttt_token(t + 1, slot + 1)
                if before:
                    ttt_turn_back(t - 1, slot - 1)

            ttt_turn(0, 0)
            ttt_query(0, 0)
            ttt_token(0, 0)
            ttt_turn(1, 1)
            over_pairs(pe, ttt, 4)
            ttt_grad(PAIRS - 1, 3)
            ttt_project(PAIRS - 2, 2)
            ttt_updated(PAIRS - 1, 3)
            ttt_turn_back(PAIRS - 1, 3)
            ttt_project(PAIRS - 1, 3)

            pe.wait_ge(S["load_moe"], 112)
            pe.wait_ge(S["ttt_oT"], PAIRS)

            def rt_turn(turn, j):
                t, slot, _ = at_two(turn, j)
                pe.wait_ge(S["rt_t"], t + 1)
                when(pe, S["rt_tTs"], t)
                for i in range(2):
                    for k in range(2):
                        ins = pe.transpose(bank[0][0:HC, (2 * k + i) * N:(2 * k + i + 1) * N],
                                           ts[:, slot, i, k * HC:k * HC + HC], ident[0:N, 0:N])
                ins.then_inc(S["rt_tT"], 1)

            def rt_logits(turn, j):
                t, slot, _ = at_two(turn, j)
                pe.wait_ge(S["rt_tTs"], t + 1)
                when(pe, S["rt_gs"], t)
                for i in range(2):
                    for k in range(2):
                        nrow = KA if k == 0 else HC
                        ins = pe.matmul(bank[1][0:N, i * E1:i * E1 + E1], xT[0:nrow, slot, k, i, :], gate1[0:nrow, k, :],
                                        start=(k == 0), stop=(k == 1))
                ins.then_inc(S["rt_logit"], 1)

            def rt_count(turn, j):
                t, slot, _ = at_two(turn, j)
                pe.wait_ge(S["rt_taken"], t + 1)
                when(pe, S["rt_base"], t)
                a, b = taken[:, slot, 0, :], taken[:, slot, 1, :]
                pe.matmul(bank[2][0:N, 0:E1], tri[:, :], a, start=True, stop=True)
                pe.matmul(bank[2][0:N, E1:2 * E1], tri[:, :], b, start=True, stop=False)
                pe.matmul(bank[2][0:N, E1:2 * E1], ones[0:N, 0:N], a, start=False, stop=True)
                pe.matmul(bank[2][:, 2 * E1:3 * E1], ones[0:N, :], a, start=True, stop=False)
                pe.matmul(bank[2][:, 2 * E1:3 * E1], ones[0:N, :], b, start=False, stop=True).then_inc(S["rt_count"], 1)

            def route(turn, j):
                rt_logits(turn, j)
                if not (last(turn, PAIRS // 2) and j == 1):
                    rt_turn(turn, j + 1)
                rt_count(turn, j)

            rt_turn(0, 0)
            over_twos(pe, route, PAIRS)
            pe.wait_ge(S["rt_blocks"], 1)
            for k in range(2):
                ins = pe.matmul(bank[3][0:1, k * BLOCKS:(k + 1) * BLOCKS], block_f[:, k:k + 1], ident[:, :],
                                start=True, stop=True)
            ins.then_inc(S["rt_row"], 1)

            def moe_turn(turn, j):
                n, slot, _ = at(turn, j)
                pe.wait_ge(S[f"loaded{slot}"], 16 * (turn + j // 4 + 1))
                when(pe, S["moe_xTs"], n)
                for k in range(2):
                    ins = pe.transpose(bank[0][0:HC, k * 128:k * 128 + 128], xb[:, slot, k * HC:k * HC + HC], ident[:, :])
                ins.then_inc(S["moe_xT"], 1)

            def moe_up(turn, j, e):
                n, slot, _ = at(turn, j)
                pe.wait_ge(S["moe_xTs"], n + 1)
                when(pe, S["moe_al"], n - 1)
                for k in range(2):
                    nrow = KA if k == 0 else HC
                    ins = pe.matmul(up[slot % 2][:, 0:2 * I1], xTm[0:nrow, slot % 2, k, :], m1[0:nrow, bass.ds(e, 1), k, :],
                                    start=(k == 0), stop=(k == 1))
                ins.then_inc(S["moe_h"], 1)

            def moe_turn_back(turn, j):
                n, slot, _ = at(turn, j)
                pe.wait_ge(S["moe_act"], n + 1)
                when(pe, S["moe_aTs"], n)
                for k in range(2):
                    ins = pe.transpose(bank[2][0:HC, k * 128:k * 128 + 128], ac[:, slot % 2, k * HC:k * HC + HC],
                                       ident[:, :])
                ins.then_inc(S["moe_aT"], 1)

            def moe_down(turn, j, e):
                n, slot, _ = at(turn, j)
                pe.wait_ge(S["moe_aTs"], n + 1)
                when(pe, S["moe_ys"], n)
                for k in range(2):
                    nrow = KA if k == 0 else HC
                    ins = pe.matmul(bank[3][:, 0:C], aT[0:nrow, slot % 2, k, :], m2[0:nrow, bass.ds(e, 1), k, :],
                                    start=(k == 0), stop=(k == 1))
                ins.then_inc(S["moe_y"], 1)

            def moe(turn, j):
                if j == 0:
                    word = pe.value_load(etab[0:1, bass.ds(turn, 1)])
                    for i in range(-2, 4):
                        expert[i] = (word // E1 ** (i + 2)) % E1
                moe_up(turn, j, expert[j])
                if not (last(turn, BLOCKS // 4) and j == 3):
                    moe_turn(turn, j + 1)
                if not (first(turn) and j == 0):
                    moe_turn_back(turn, j - 1)
                if not (first(turn) and j < 2):
                    moe_down(turn, j - 2, expert[j - 2])

            expert = {}
            pe.wait_ge(S["rt_done"], 1)
            moe_turn(0, 0)
            over_blocks(pe, moe)
            moe_turn_back(BLOCKS // 4 - 1, 3)
            moe_down(BLOCKS // 4 - 1, 2, expert[2])
            moe_down(BLOCKS // 4 - 1, 3, expert[3])

        @block.vector
        def _(dve):
            V = nc.vector
            chained = [0]

            def link(ins):
                chained[0] += 1
                ins.then_inc(S["dve_chain"], 1)
                dve.wait_ge(S["dve_chain"], chained[0])

            def rsqrt(y, v, w, then):
                by = 0.375 ** 0.2
                then(V.tensor_scalar(y.bitcast(I32), v.bitcast(I32), -0.5, float(0x5F3759DF), ALU.mult, ALU.add))
                then(V.scalar_tensor_tensor(out=w, in0=y, scalar=-0.5 * by, in1=y, op0=ALU.mult, op1=ALU.mult))
                then(V.tensor_tensor(w, w, v, ALU.mult))
                then(V.scalar_tensor_tensor(out=y, in0=w, scalar=1.5 * by, in1=y, op0=ALU.add, op1=ALU.mult))
                then(V.tensor_tensor(w, y, y, ALU.mult))
                then(V.tensor_tensor(w, w, v, ALU.mult))
                then(V.scalar_tensor_tensor(out=w, in0=w, scalar=-10 / 3 * by ** 2, in1=w, op0=ALU.add, op1=ALU.mult))
                return V.scalar_tensor_tensor(out=y, in0=w, scalar=5 * by ** 4, in1=y, op0=ALU.add, op1=ALU.mult)

            V.memset(ones[:, :], 1.0)
            V.memset(avg128[:, :], 1.0 / 128)
            V.memset(avgN[:, :], 1.0 / N)
            V.memset(xT[HC:KA, :, :, :, :], 1.0)
            V.memset(qT[HC:KA, :, :, :], 1.0)
            V.memset(oT[HC:KA, :, :, :, :], 1.0)
            V.memset(kS[:, :, :, :, HC:KA], 1.0)
            V.memset(vS[:, :, :, :, HC:KA], 1.0)
            V.memset(kvs[HC:KA, :, :, :, 0:HC], 0.0)
            V.memset(kvs[HC:KA, :, :, :, HC:], TTT_EPS).then_inc(S["const_ready"], 1)
            dve.wait_ge(S["load_idx"], 48)
            V.tensor_scalar(idxc[:, :], idx[:, :], 0, VOCAB - 1, ALU.max, ALU.min).then_inc(S["clipped"], 1)
            V.tensor_scalar(keep[:, 0, :], idxm[:, :], 0, None, ALU.is_ge).then_inc(S["mask"], 1)
            V.tensor_scalar(keep[:, 1, :], idxm[:, :], VOCAB - 1, None, ALU.is_le).then_inc(S["mask"], 1)
            dve.wait_ge(S["mask"], 2)
            V.tensor_tensor(keep[:, 0, :], keep[:, 0, :], keep[:, 1, :], ALU.mult).then_inc(S["mask"], 1)

            for half in range(2):
                dve.wait_ge(S[f"load_x{half}"], 32)
                for b in range(B // 2 * half, B // 2 * (half + 1)):
                    ins = V.bn_stats(tstat[:, b:b + 1, :].rearrange("p a s -> p (a s)"),
                                     X[:, b:b + 1, :].rearrange("p a w -> p (a w)"))
                ins.then_inc(S["tok_dev"], 1)
            dve.wait_ge(S["tok_dev"], 2)
            n_half = XW // 2
            T = tsmall
            link(V.tensor_tensor(T[:, 0, :], tstat[:, :, 1], tstat[:, :, 4], ALU.add))
            V.tensor_scalar(T[:, 0, :], T[:, 0, :], 0.5, None, ALU.mult).then_inc(S["tok_stat"], 1)
            dve.wait_ge(S["tok_mean"], 1)
            link(V.tensor_copy(T[:, 1, :], bank[0][:, 0:B]))
            for q, src in ((2, 1), (4, 4)):
                link(V.tensor_tensor(T[:, q, :], tstat[:, :, src], T[:, 1, :], ALU.subtract))
                link(V.tensor_tensor(T[:, q, :], T[:, q, :], T[:, q, :], ALU.mult))
            link(V.tensor_tensor(T[:, 2, :], T[:, 2, :], T[:, 4, :], ALU.add))
            link(V.tensor_tensor(T[:, 4, :], tstat[:, :, 2], tstat[:, :, 5], ALU.add))
            V.scalar_tensor_tensor(out=T[:, 3, :], in0=T[:, 4, :], scalar=1.0 / n_half, in1=T[:, 2, :],
                                   op0=ALU.mult, op1=ALU.add).then_inc(S["tok_varsum"], 1)
            dve.wait_ge(S["tok_devavg"], 1)
            V.tensor_scalar(T[:, 4, :], bank[1][:, 0:B], 0.5, LN_EPS, ALU.mult, ALU.add).then_inc(S["tok_eps"], 1)
            dve.wait_ge(S["tok_eps"], 1)
            link(rsqrt(T[:, 5, :], T[:, 4, :], T[:, 2, :], link))
            V.scalar_tensor_tensor(out=T[:, 0, :], in0=T[:, 1, :], scalar=-1.0, in1=T[:, 5, :],
                                   op0=ALU.mult, op1=ALU.mult).then_inc(S["tok_rstd"], 1)
            dve.wait_ge(S["tok_bias_mm"], 1)
            V.tensor_tensor(tokb[:, :], bank[2][0:ROWS, 0:C], projb[:, :], ALU.add).then_inc(S["tok_bias"], 1)
            dve.wait_ge(S["tok_bias"], 1)
            V.tensor_tensor(tokb[:, :], tokb[:, :], pos[:, :], ALU.add).then_inc(S["tok_bias"], 1)
            def patch_scale(g, slot, count):
                when(dve, S["tok_mm"], g - 1)
                dve.wait_ge(S["tok_norm"], g + 1)
                for j in range(count):
                    ins = V.tensor_tensor(xg[:, slot, :, j * NI:j * NI + NI],
                                          X[:, bass.ds(g * GRP + j, 1), :].rearrange("p a (k l) -> p (a k) l", k=CHUNKS),
                                          lnwb[:, 0, :].rearrange("p (k l) -> p k l", k=CHUNKS), ALU.mult)
                ins.then_inc(S["tok_xg"], 1)

            def patch_add(g, slot, count, uses):
                dve.wait_ge(S["tok_mm"], g + 1)
                dve.wait_ge(S["tok_bias"], 2)
                when(dve, S[f"tok_piece{slot}"], 16 * GRP * uses)
                rows = NI * count
                V.tensor_tensor(tok[0:rows, slot, :], bank[slot][0:rows, 0:C], tokb[0:rows, :], ALU.add)\
                 .then_inc(S["tok_sum"], 1)

            patch_scale(0, 0, GRP)
            patch_scale(1, 1, GRP)
            patch_add(0, 0, GRP, 0)
            patch_scale(2, 0, GRP)
            patch_add(1, 1, GRP, 0)
            patch_scale(3, 1, GRP)
            with dve.Fori(1, 4) as turn:
                patch_add(turn * 2, 0, GRP, turn)
                patch_scale(turn * 2 + 2, 0, GRP)
                patch_add(turn * 2 + 1, 1, GRP, turn)
                patch_scale(turn * 2 + 3, 1, GRP)
            patch_add(8, 0, GRP, 4)
            patch_scale(10, 0, 2)
            patch_add(9, 1, GRP, 4)
            patch_add(10, 0, 2, 5)

            dve.wait_ge(S["mask"], 3)
            dve.wait_ge(S["tok_piece0"], 16 * (5 * GRP + 2))
            dve.wait_ge(S["tok_piece1"], 16 * 5 * GRP)
            dve.wait_ge(S["gathered"], 16 * B)

            def image(t_, b, i=1):
                return t_[:, bass.ds(b, 1), :].rearrange("p a c -> p (a c)")

            with dve.Fori(0, 2) as turn:
                for j in range(0, B // 2, 2):
                    b = turn * (B // 2) + j
                    ins = V.tensor_scalar(image(h, b), image(h, b), keep[:, 0, bass.ds(b, 1)], None, ALU.mult)
                ins.then_inc(S["masked"], 1)
            dve.wait_ge(S["masked"], 2)
            with dve.Fori(0, 2) as turn:
                dve.wait_ge(S["masked_odd"], turn * (B // 8) + B // 8)
                for j in range(B // 2):
                    b = turn * (B // 2) + j
                    ins = V.bn_stats(image(stats, b), image(h, b))
                ins.then_inc(S["ln0_stat"], 1)

            def finish_stats(sem, count):
                dve.wait_ge(sem, count)
                V.tensor_tensor(lns[:, 0, :], stats[:, :, 1], stats[:, :, 4], ALU.add)
                V.tensor_tensor(lns[:, 1, :], stats[:, :, 1], stats[:, :, 4], ALU.subtract)
                link(V.tensor_tensor(lns[:, 2, :], stats[:, :, 2], stats[:, :, 5], ALU.add))
                V.tensor_scalar(mean[:, :], lns[:, 0, :], 0.5, None, ALU.mult)
                link(V.scalar_tensor_tensor(out=lns[:, 3, :], in0=lns[:, 1, :], scalar=0.25, in1=lns[:, 1, :],
                                            op0=ALU.mult, op1=ALU.mult))
                link(V.scalar_tensor_tensor(out=lns[:, 0, :], in0=lns[:, 2, :], scalar=1.0 / C, in1=lns[:, 3, :],
                                            op0=ALU.mult, op1=ALU.add))
                link(V.tensor_scalar(lns[:, 3, :], lns[:, 0, :], LN_EPS, None, ALU.add))
                link(rsqrt(rstd[:, :], lns[:, 3, :], lns[:, 1, :], link))
                V.scalar_tensor_tensor(out=shift[:, :], in0=mean[:, :], scalar=-1.0, in1=rstd[:, :],
                                       op0=ALU.mult, op1=ALU.mult).then_inc(S["ln_ready"], 1)

            def normalise(t, slot, sem, free, n_free):
                when(dve, free, n_free)
                for i in range(2):
                    b = t * 2 + i
                    ins = V.tensor_scalar(xn[:, slot, i, :], image(h, b), mean[:, bass.ds(b, 1)],
                                          rstd[:, bass.ds(b, 1)], ALU.subtract, ALU.mult)
                ins.then_inc(sem, 1)

            finish_stats(S["ln0_stat"], 2)
            dve.wait_ge(S["load_att"], 64)
            mask4 = mask[0:HC, :].rearrange("p (a c) -> p a c", a=1)

            def att_rest(t, slot):
                dve.wait_ge(S["att_out"], t + 1)
                V.tensor_tensor(h[:, bass.ds(t * 2, 2), :], bank[3][0:N, 0:2 * C].rearrange("p (i c) -> p i c", i=2),
                                h[:, bass.ds(t * 2, 2), :], ALU.add).then_inc(S["att_h"], 1)
                dve.wait_ge(S["att_h"], t + 1)
                for i in range(2):
                    ins = V.bn_stats(image(stats, t * 2 + i), image(h, t * 2 + i))
                ins.then_inc(S["att_stat"], 1)

            def att_divide(t, slot):
                dve.wait_ge(S["att_frac"], t + 1)
                parts = wide[1][0:N, 0, 0:4 * (HC + HH)].rearrange("p (a c) -> p a c", a=4)
                V.reciprocal(rden[:, :].rearrange("p (a c) -> p a c", a=4), parts[:, :, HC:]).then_inc(S["att_rden"], 1)
                dve.wait_ge(S["att_rden"], t + 1)
                when(dve, S["att_oTp"], t - 1)
                V.tensor_tensor(on[:, slot].rearrange("p i h (a d) -> p (i h) a d", d=HD),
                                parts[:, :, 0:HC].rearrange("p x (a d) -> p x a d", d=HD),
                                rden[:, :].rearrange("p (x a d) -> p x a d", x=4, d=1).broadcast_to([N, 4, HH, HD]),
                                ALU.mult).then_inc(S["att_on"], 1)

            def attention(t, slot):
                first = isinstance(t, int) and t == 0
                dve.wait_ge(S["att_kv"], t + 1)
                when(dve, S["att_prod"], t - 1)
                V.tensor_scalar(kS[:, slot, :, :, 0:HC], wide[0][0:N, :, 0:C].rearrange("p i (h c) -> p i h c", h=2),
                                0.0, HD ** -0.5, ALU.max, ALU.add).then_inc(S["att_ks"], 1)
                if not first:
                    att_divide(t - 1, 1 - slot)
                dve.wait_ge(S["att_q"], t + 1)
                when(dve, S["att_frac"], t - 1)
                V.tensor_scalar(qT[0:HC, slot].rearrange("p h n -> p (h n)"), bank[1][0:HC, 0:4 * N],
                                0.0, HD ** -0.5, ALU.max, ALU.add).then_inc(S["att_qs"], 1)
                dve.wait_ge(S["att_prod"], t + 1)
                prod = bank[2][0:HC, 0:4 * KA].rearrange("p (a c) -> p a c", a=4)
                V.tensor_tensor(kvs[0:HC, slot, :, :, 0:HC].rearrange("p i h c -> p (i h) c"), prod[:, :, 0:HC],
                                mask4.broadcast_to([HC, 4, HC]), ALU.mult)
                V.tensor_tensor(kvs[0:HC, slot, :, :, HC:].rearrange("p i h c -> p (i h) c"),
                                prod[:, :, HC:KA].broadcast_to([HC, 4, HH]),
                                mask4[:, :, 0:HC:HD].broadcast_to([HC, 4, HH]), ALU.mult).then_inc(S["att_ksm"], 1)
                if not (isinstance(t, int) and t < 2):
                    att_rest(t - 2, slot)

            over_pairs(dve, attention)
            att_divide(PAIRS - 1, 1)
            att_rest(PAIRS - 2, 0)
            att_rest(PAIRS - 1, 1)

            finish_stats(S["att_stat"], PAIRS)

            dve.wait_ge(S["load_ttt"], 128)
            heads_of_w = w1b[:, :, :].rearrange("p m (a d) -> p (m a) d", d=HD)
            link(V.tensor_reduce(w1m[:, :], heads_of_w, AX_X, ALU.add))
            link(V.tensor_scalar(w1m[:, :], w1m[:, :], 1.0 / HD, None, ALU.mult))
            V.tensor_tensor(w1c[:, :, :].rearrange("p m (a d) -> p (m a) d", d=HD), heads_of_w,
                            w1m[:, :].rearrange("p (a d) -> p a d", d=1).broadcast_to([KA, HEADS, HD]), ALU.subtract)\
             .then_inc(S["tw_cent"], 1)
            other = wtok[:, :, 2 * C:3 * C]
            link(V.tensor_tensor(other, other, wv[:, :, :], ALU.subtract))
            link(V.tensor_tensor(other, other, gam[0:KA, :].rearrange("p (a c) -> p a c", a=1).broadcast_to([KA, 2, C]),
                                 ALU.mult))
            for i in range(2):
                V.tensor_tensor(gam2[:, i, :], gam[:, :], gam[:, :], ALU.mult)
            V.memset(kA[:, :, :, :, HC:KA], 1.0)
            for k, value in enumerate((TTT_EPS, 1.0 / (HD * N), 1.0 / HD)):
                V.memset(tc[:, k, :], value)
            dve.wait_ge(S["gate0_mean"], PAIRS)
            dve.wait_ge(S["load_ffn"], 64)
            link(V.tensor_copy(gm[:, :, :].rearrange("p h b -> p (h b)"), bank[1][0:HC, 0:2 * B]))
            for k in range(2):
                ins = V.tensor_tensor(gprod[:, k], gm[:, k, :].rearrange("p (b a) -> p b a", a=1).broadcast_to([HC, B, E0]),
                                      wg0[:, k, :].rearrange("p (a e) -> p a e", a=1).broadcast_to([HC, B, E0]), ALU.mult)
            ins.then_inc(S["gate0_prod"], 1)
            dve.wait_ge(S["gate0_logit"], 1)
            logit = bank[2][:, 0:B * E0].rearrange("p (b e) -> p b e", e=E0)

            def spread(v, e=E0):
                return v.rearrange("p (b a) -> p b a", a=1).broadcast_to([128, B, e])

            link(V.tensor_reduce(gone[:, 0, :], logit, AX_X, ALU.max))
            V.tensor_tensor(gsm[:, 0], logit, spread(gone[:, 0, :]), ALU.subtract).then_inc(S["gate0_step"], 1)
            dve.wait_ge(S["gate0_exp"], 1)
            ex = gsm[:, 1]
            V.tensor_reduce(gone[:, 1, :], ex, AX_X, ALU.add)
            link(V.tensor_reduce(gone[:, 0, :], ex, AX_X, ALU.max))
            V.reciprocal(gone[:, 2, :], gone[:, 1, :])
            link(V.tensor_tensor(gsm[:, 0], ex, spread(gone[:, 0, :]), ALU.is_lt))
            V.tensor_tensor(gone[:, 4, :], gone[:, 2, :], gone[:, 0, :], ALU.mult)
            link(V.tensor_scalar(gone[:, 3, :], gsm[:, 0, :, 1], 1.0, None, ALU.add))
            V.tensor_tensor(sel[:, :], gone[0:1, 3, :], gsm[0:1, 0, :, 0], ALU.mult).then_inc(S["gate0_ready"], 1)

            def ffn_add(u, i):
                dve.wait_ge(S["ffn_y"], u + 1)
                V.scalar_tensor_tensor(out=image(h, u), in0=bank[3][0:N, i * 256:i * 256 + C],
                                       scalar=gone[0:N, 4, bass.ds(u, 1)], in1=image(h, u),
                                       op0=ALU.mult, op1=ALU.add).then_inc(S["ffn_h"], 1)
                dve.wait_ge(S["ffn_h"], u + 1)
                V.bn_stats(image(stats, u), image(h, u)).then_inc(S["ffn_stat"], 1)

            def ffn_hT(u, i):
                dve.wait_ge(S["ffn_hT"], u + 1)
                when(dve, S["ffn_y"], u - 1)
                V.tensor_copy(hT[:, i, 0:3, :], bank[1][:, 0:3 * N].rearrange("p (k n) -> p k n", k=3))\
                 .then_inc(S["ffn_hTv"], 1)

            def ffn(t, slot):
                for i in range(2):
                    u = t * 2 + i
                    if not first(u):
                        ffn_hT(u - 1, 1 - i)
                    if i == 0 and not (isinstance(t, int) and t + 2 >= PAIRS):
                        normalise(t + 2, slot, S["ffn_xn"], S["ffn_xT"], t + 1)
                    if not first(u):
                        ffn_add(u - 1, 1 - i)

            normalise(0, 0, S["ffn_xn"], S["gate0_mean"], PAIRS)
            dve.wait_ge(S["tw_comp"], 1)
            V.tensor_scalar(gcol[:, 0:2], gcol[:, 0:2], -1.0, None, ALU.mult)
            V.tensor_copy(wtok[0:HC, :, C:2 * C], bank[3][0:HC, 0:4 * HC].rearrange("p (k c) -> p k c", k=2))
            dve.wait_ge(S["tw_cent"], 1)
            V.tensor_copy(wtok[HC:KA, 0, C:2 * C], w1c[HC:KA, :, :].rearrange("p m c -> p (m c)"))
            V.tensor_tensor(wp[HC:KA, 0, :], bank[0][HC:KA, 0:C], wp[HC:KA, 0, :], ALU.add).then_inc(S["tw_done"], 1)
            dve.wait_ge(S["tw_done"], 1)
            normalise(1, 1, S["ffn_xn"], None, 0)
            over_pairs(dve, ffn)
            ffn_hT(B - 1, 1)
            ffn_add(B - 1, 1)

            finish_stats(S["ffn_stat"], B)

            def heads(v):
                return v.rearrange("p (a d) -> p a d", d=HD)

            def per_head(v):
                return v.rearrange("p (a d) -> p a d", d=1).broadcast_to([N, 2 * HEADS, HD])

            mask97 = mask[:, :].rearrange("p (a c) -> p a c", a=1).broadcast_to([KA, 4, HC])

            def ttt_weights(t, slot):
                dve.wait_ge(S["ttt_grad"], t + 1)
                when(dve, S["ttt_zb"], t - 1)
                V.tensor_tensor(wn[:, slot % 2].rearrange("p i m c -> p (i m) c"),
                                bank[2][0:KA, 0:4 * HC].rearrange("p (a c) -> p a c", a=4), mask97, ALU.mult)\
                 .then_inc(S["ttt_w"], 1)

            def ttt_centre(t, slot):
                s_ = sm[:, slot % 2]
                z = heads(wide[1][0:N, 0, 0:2 * C])
                dve.wait_ge(S["ttt_zb"], t + 1)
                V.tensor_reduce(s_[:, 4, :], z, AX_X, ALU.add).then_inc(S["ttt_zm"], 1)
                dve.wait_ge(S["ttt_zm"], t + 1)
                when(dve, S["ttt_zh"], t)
                V.scalar_tensor_tensor(out=heads(zc[:, :]), in0=per_head(s_[:, 4, :]), scalar=1.0 / HD, in1=z,
                                       op0=ALU.mult, op1=ALU.subtract).then_inc(S["ttt_zc"], 1)

            def spread_of_outer(t):
                dve.wait_ge(S["ttt_zsq"], t + 1)
                V.tensor_reduce(hv[:, 2 * HEADS:], heads(zsq[:, :]), AX_X, ALU.add).then_inc(S["ttt_zv"], 1)

            def root(turn, a, b):
                c = slice(a * 2 * HEADS, b * 2 * HEADS)
                done = [0]

                def then(ins):
                    done[0] += 1
                    ins.then_inc(S["root"], 1)
                    dve.wait_ge(S["root"], 8 * turn + done[0])

                if a == 0:
                    dve.wait_ge(S["ttt_v"], turn + 1)
                if b == 2:
                    dve.wait_ge(S["ttt_zv"], turn)
                when(dve, S["ttt_r"], turn)
                then(V.tensor_scalar(hv[:, c], hv[:, c], TTT_EPS, None, ALU.add))
                return rsqrt(irs[:, c], hv[:, c], hw[:, c], then)

            def normalised_outer(t, slot):
                dve.wait_ge(S["ttt_rstd"], t + 2)
                when(dve, S["ttt_zT"], t - 1)
                V.tensor_tensor(heads(zh[:, slot % 2, :]), heads(zc[:, :]), per_head(irs[:, 2 * HEADS:]), ALU.mult)\
                 .then_inc(S["ttt_zh"], 1)

            def ttt_add(t):
                dve.wait_ge(S["ttt_out"], t + 1)
                V.tensor_tensor(h[:, bass.ds(t * 2, 2), :], wide[1][0:N, 1, 0:2 * C].rearrange("p (i c) -> p i c", i=2),
                                h[:, bass.ds(t * 2, 2), :], ALU.add).then_inc(S["ttt_h"], 1)

            def ttt_stats(t):
                dve.wait_ge(S["ttt_h"], t + 1)
                for i in range(2):
                    ins = V.bn_stats(image(stats, t * 2 + i), image(h, t * 2 + i))
                ins.then_inc(S["ttt_stat"], 1)

            def ttt(t, slot):
                fixed = isinstance(t, int)
                before = not (fixed and t == 0)
                s_ = sm[:, slot % 2]
                dve.wait_ge(S["ttt_sq"], t + 1)
                V.tensor_reduce(hv[:, 0:2 * HEADS], heads(sq[:, :]), AX_X, ALU.add).then_inc(S["ttt_v"], 1)
                if before:
                    ttt_weights(t - 1, slot - 1)
                    ttt_centre(t - 1, slot - 1)
                    spread_of_outer(t - 1)
                root(t, 0, 2 if before else 1).then_inc(S["ttt_rstd"], 1)
                dve.wait_ge(S["ttt_rstd"], t + 1)
                V.tensor_tensor(xh[:, :].rearrange("p (x a d) -> p x a d", x=4, d=HD),
                                kA[:, slot % 2, :, 2:4, 0:HC].rearrange("p i m (a d) -> p i m a d", d=HD),
                                irs[:, 0:2 * HEADS].rearrange("p (x a d) -> p x a d", x=4, d=1).broadcast_to([N, 4, HH, HD]),
                                ALU.mult).then_inc(S["ttt_xh"], 1)
                if before:
                    normalised_outer(t - 1, slot - 1)
                if not (fixed and t < 2):
                    ttt_add(t - 2)
                dve.wait_ge(S["ttt_t1"], t + 1)
                V.tensor_tensor(gg[:, :].rearrange("p (i c) -> p i c", i=2), t1[:, :].rearrange("p (i c) -> p i c", i=2),
                                dl[:, slot % 2, :, 0:C], ALU.add).then_inc(S["ttt_g"], 1)
                dve.wait_ge(S["ttt_g"], t + 1)
                V.tensor_tensor(pp[:, :], gg[:, :], xh[:, :], ALU.mult).then_inc(S["ttt_p"], 1)
                dve.wait_ge(S["ttt_p"], t + 1)
                V.tensor_reduce(s_[:, 3, :], heads(pp[:, :]), AX_X, ALU.add).then_inc(S["ttt_s"], 1)
                if not (fixed and t < 2):
                    ttt_stats(t - 2)
                dve.wait_ge(S["ttt_r"], t + 1)
                dve.wait_ge(S["ttt_s"], t + 1)
                V.tensor_tensor(heads(pp[:, :]), heads(gg[:, :]), per_head(s_[:, 2, :]), ALU.mult).then_inc(S["ttt_gr"], 1)
                dve.wait_ge(S["ttt_gr"], t + 1)
                dve.wait_ge(S["ttt_xs"], t + 1)
                when(dve, S["ttt_grad"], t - 1)
                V.tensor_tensor(zz[:, slot % 2, :], xs[:, :], pp[:, :], ALU.subtract).then_inc(S["ttt_zz"], 1)

            over_pairs(dve, ttt, 4)
            t, slot = PAIRS - 1, 3
            ttt_add(t - 1)
            ttt_stats(t - 1)
            ttt_weights(t, slot)
            ttt_centre(t, slot)
            spread_of_outer(t)
            root(PAIRS, 1, 2).then_inc(S["ttt_rstd"], 1)
            normalised_outer(t, slot)
            ttt_add(t)
            ttt_stats(t)

            dve.wait_ge(S["load_moe"], 112)
            finish_stats(S["ttt_stat"], PAIRS)
            link(V.tensor_tensor(lns[:, 1, :], lns[:, 0, :], rstd[:, :], ALU.mult))
            link(V.tensor_tensor(lns[:, 1, :], lns[:, 1, :], rstd[:, :], ALU.mult))
            link(V.tensor_scalar(lns[:, 1, :], lns[:, 1, :], RMS_EPS, None, ALU.add))
            V.memset(aT[HC:KA, :, :, :], 1.0)
            V.memset(xTm[HC:KA, :, :, :], 1.0)
            link(rsqrt(rr, lns[:, 1, :], lns[:, 2, :], link))
            link(V.tensor_scalar(base, iota[:, 0:E1], float(CAP), None, ALU.mult))

            def rt_rows(turn, j):
                t, slot, _ = at_two(turn, j)
                when(dve, S["rt_tT"], t - 1)
                when(dve, S["row_t"], t - 1)
                normalise(t, slot, S["rt_xn"], None, 0)
                dve.wait_ge(S["rt_xn"], t + 1)
                for i in range(2):
                    ins = V.scalar_tensor_tensor(out=ts[:, slot, i, :], in0=xn[:, slot, i, :],
                                                 scalar=rr[:, bass.ds(t * 2 + i, 1)], in1=scale[:, :],
                                                 op0=ALU.mult, op1=ALU.mult)
                ins.then_inc(S["rt_t"], 1)

            def spread(v, count):
                return v.rearrange("p (b a) -> p b a", a=1).broadcast_to([v.shape[0], v.shape[1], count])

            def rt_choose(turn, j):
                t, slot, half = at_two(turn, j)
                done = [0]

                def then(ins):
                    done[0] += 1
                    ins.then_inc(S["rt_step"], 1)
                    dve.wait_ge(S["load_moe"], 112)
                    dve.wait_ge(S["rt_step"], 9 * t + done[0])

                dve.wait_ge(S["rt_logit"], t + 1)
                V.tensor_copy(gs[:, slot], bank[1][0:N, 0:2 * E1].rearrange("p (i e) -> p i e", i=2))\
                 .then_inc(S["rt_gs"], 1)
                dve.wait_ge(S["load_moe"], 112)
                dve.wait_ge(S["rt_gs"], t + 1)
                for i in range(2):
                    ins = V.max(m8[:, slot, i, :], gs[:, slot, i, :])
                then(ins)
                when(dve, S["rt_exp"], t - 1)
                V.tensor_tensor(wraw[:, slot, :].rearrange("p (i k) -> p i k", i=2), m8[:, slot, :, 0:TOPK],
                                m8[:, slot, :, 0:1].broadcast_to([N, 2, TOPK]), ALU.subtract).then_inc(S["rt_less"], 1)
                for i in range(2):
                    ins = V.max_index(i8[:, slot, i, :], m8[:, slot, i, :], gs[:, slot, i, :])
                then(ins)
                then(V.tensor_copy(topf[:, slot, :].rearrange("p (i k) -> p i k", i=2), i8[:, slot, :, 0:TOPK]))
                then(V.tensor_tensor(hot[:, slot], spread(topf[:, slot, :], E1),
                                     iota[0:N, 0:E1].rearrange("p (a e) -> p a e", a=1).broadcast_to([N, 2 * TOPK, E1]),
                                     ALU.is_equal))
                V.tensor_reduce(taken[:, slot], hot[:, slot].rearrange("p (i k) e -> p i e k", i=2), AX_X, ALU.add)\
                 .then_inc(S["rt_taken"], 1)
                when(dve, S[f"dispatched{slot}"], 16 * 2 * TOPK * half)
                V.tensor_copy(rowbuf[:, slot, :, C].rearrange("p (i k) -> p i k", i=2), target[:, bass.ds(t * 2, 2), :])
                dve.wait_ge(S["rt_exp"], t + 1)
                then(V.tensor_reduce(wsum[:, slot, :], wexp[:, slot, :].rearrange("p (i k) -> p i k", i=2), AX_X,
                                     ALU.add))
                then(V.reciprocal(wsum[:, slot, :], wsum[:, slot, :]))
                V.tensor_tensor(rowbuf[:, slot, :, C + 1].rearrange("p (i k) -> p i k", i=2),
                                wexp[:, slot, :].rearrange("p (i k) -> p i k", i=2), spread(wsum[:, slot, :], TOPK),
                                ALU.mult)
                V.tensor_tensor(h[:, bass.ds(t * 2, 2), :], h[:, bass.ds(t * 2, 2), :], xn[:, slot], ALU.add)
                dve.wait_ge(S["rt_count"], t + 1)
                then(V.tensor_tensor(place.rearrange("p (i e) -> p i e", i=2),
                                     bank[2][0:N, 0:2 * E1].rearrange("p (i e) -> p i e", i=2),
                                     base[0:N, :].rearrange("p (a e) -> p a e", a=1).broadcast_to([N, 2, E1]),
                                     ALU.add))
                V.tensor_tensor(base, bank[2][:, 2 * E1:3 * E1], base, ALU.add).then_inc(S["rt_base"], 1)
                hot4 = hot[:, slot].rearrange("p (i k) e -> p i k e", i=2)
                then(V.tensor_tensor(hot4, hot4, place.rearrange("p (i a e) -> p i a e", i=2, a=1)
                                     .broadcast_to([N, 2, TOPK, E1]), ALU.mult))
                then(V.tensor_reduce(rowf, hot[:, slot], AX_X, ALU.add))
                V.tensor_copy(slot_s[:, slot, :], rowf).then_inc(S["row_meta"], 1)
                dve.wait_ge(S["rt_base"], t + 1)

            def route(turn, j):
                if not (last(turn, PAIRS // 2) and j == 1):
                    rt_rows(turn, j + 1)
                rt_choose(turn, j)

            rt_rows(0, 0)
            over_twos(dve, route, PAIRS)

            V.tensor_copy(pad_at[:, :], base[0:1, :]).then_inc(S["pad_ready"], 1)
            count, blocks, ends, ended, one = (per_e[:, k, :] for k in range(5))
            link(V.memset(one, 1.0))
            link(V.scalar_tensor_tensor(out=count, in0=iota[:, 0:E1], scalar=float(-CAP), in1=base, op0=ALU.mult, op1=ALU.add))
            link(V.tensor_scalar(per_ei[:, 0, :], count, 127.0, None, ALU.add))
            link(V.tensor_scalar(per_ei[:, 1, :], per_ei[:, 0, :], 7, None, ALU.arith_shift_right))
            link(V.tensor_copy(blocks, per_ei[:, 1, :]))
            link(V.tensor_tensor_scan(ends, one, blocks, 0.0, ALU.mult, ALU.add))
            link(V.tensor_scalar(ended, ends, iota[:, E1:E1 + 1], None, ALU.is_le))
            link(V.tensor_reduce(block_f[:, 2:3], ended, AX_X, ALU.add))
            link(V.tensor_tensor(ended, ended, blocks, ALU.mult))
            link(V.tensor_reduce(block_f[:, 3:4], ended, AX_X, ALU.add))
            link(V.tensor_scalar(block_f[:, 0:1], block_f[:, 2:3], float(E1 - 1), None, ALU.min))
            link(V.tensor_tensor(block_f[:, 3:4], iota[:, E1:E1 + 1], block_f[:, 3:4], ALU.subtract))
            link(V.tensor_scalar(block_f[:, 3:4], block_f[:, 3:4], 128.0, None, ALU.mult))
            V.scalar_tensor_tensor(out=block_f[:, 1:2], in0=block_f[:, 2:3], scalar=float(CAP), in1=block_f[:, 3:4],
                                   op0=ALU.mult, op1=ALU.add).then_inc(S["rt_blocks"], 1)
            V.memset(experts[:, 0:4], 0.0)
            dve.wait_ge(S["rt_row"], 1)
            link(V.tensor_copy(experts[:, 4:4 + BLOCKS], bank[3][0:1, 0:BLOCKS]))
            V.tensor_copy(first_row[:, :], bank[3][0:1, BLOCKS:2 * BLOCKS])
            digit = experts[:, :].rearrange("p (t j) -> p j t", j=4)
            link(V.tensor_copy(etab_f[:, :], digit[:, 2, 0:BLOCKS // 4]))
            for k in range(1, 6):
                q, j = divmod(k + 2, 4)
                link(V.scalar_tensor_tensor(out=etab_f[:, :], in0=digit[:, j, q:q + BLOCKS // 4], scalar=float(E1 ** k),
                                            in1=etab_f[:, :], op0=ALU.mult, op1=ALU.add))
            V.tensor_copy(etab[:, :], etab_f[:, :]).then_inc(S["rt_done"], 1)

            def moe_gate(turn, j):
                n, four, half = at(turn, j)
                slot = four % 2
                dve.wait_ge(S["moe_h"], n + 1)
                dve.wait_ge(S[f"loaded{four}"], 16 * (turn + 1))
                when(dve, S["moe_sig"], n - 1)
                when(dve, S["moe_p"], n - 1)
                when(dve, S["moe_ys"], n - 3)
                when(dve, S[f"moe_out{slot}"], 16 * (half - 1))
                V.tensor_copy(weight[:, four, :], xb[:, four, C + 1:C + 2])
                V.tensor_copy(dest[:, four, :], xb[:, four, C:C + 1])
                V.tensor_scalar(al[:, slot, 0:I1], up[slot][:, 0:I1], LIMIT, None, ALU.min)
                V.tensor_scalar(al[:, slot, I1:2 * I1], up[slot][:, I1:2 * I1], -LIMIT, LIMIT, ALU.max, ALU.min)\
                 .then_inc(S["moe_al"], 1)
                dve.wait_ge(S["moe_al"], n + 1)
                when(dve, S["moe_act"], n - 1)
                V.scalar_tensor_tensor(out=pr[:, slot, :], in0=al[:, slot, I1:2 * I1], scalar=1.0, in1=al[:, slot, 0:I1],
                                       op0=ALU.add, op1=ALU.mult).then_inc(S["moe_p"], 1)

            def moe_weigh(turn, j):
                n, slot, half = at(turn, j)
                dve.wait_ge(S["moe_y"], n + 1)
                when(dve, S[f"moe_out{slot % 2}"], 16 * half)
                V.tensor_scalar(ys[:, slot % 2, :], bank[3][:, 0:C], weight[:, slot, :], None, ALU.mult)\
                 .then_inc(S["moe_ys"], 1)

            def moe(turn, j):
                moe_gate(turn, j)
                if not (first(turn) and j < 2):
                    moe_weigh(turn, j - 2)

            over_blocks(dve, moe)
            moe_weigh(BLOCKS // 4 - 1, 2)
            moe_weigh(BLOCKS // 4 - 1, 3)

            def final(turn, j):
                t, slot, half = at(turn, j)
                dve.wait_ge(S[f"loaded{slot}"], 16 * (BLOCKS // 4 + turn + 1))
                when(dve, S["fin_b"], t)
                V.tensor_tensor(ya[:, :, :], yc[:, slot, :, 0:2 * C], yc[:, slot, :, 2 * C:4 * C], ALU.add)\
                 .then_inc(S["fin_a"], 1)
                dve.wait_ge(S["fin_a"], t + 1)
                when(dve, S["fin_c"], t)
                V.tensor_tensor(yb[:, :, :], ya[:, :, 0:C], ya[:, :, C:2 * C], ALU.add).then_inc(S["fin_b"], 1)
                dve.wait_ge(S["fin_b"], t + 1)
                when(dve, S[f"stored{slot % 2}"], 16 * half)
                V.tensor_tensor(yo[:, slot % 2], yb[:, :, :], h[:, bass.ds(t * 2, 2), :], ALU.add)\
                 .then_inc(S["fin_c"], 1)

            over_fours(dve, final, PAIRS)


def halves(w):
    return w.T.reshape(2, HC, -1).transpose(1, 0, 2)


def with_bias(w, row):
    a = np.zeros((KA, 2, w.shape[0]), np.float32)
    a[:HC] = halves(w)
    a[HC, 0] = row
    return a


def layouts(inputs):
    g = {k: np.asarray(v) for k, v in inputs.items()}
    f = np.float32

    def patches(a):
        n = a.shape[0]
        a = a.reshape(n, 3, 6, 2, 8, 6, 16).transpose(4, 6, 0, 1, 3, 2, 5)
        return a.reshape(128, n, XW)

    ids = g["x_txt"].T
    idsm = np.zeros((N, B), ids.dtype)
    idsm[NI:] = ids
    convb = np.empty((128, 12), f)
    convb[:, 0:9] = g["L0_tok_conv_w"].reshape(1, 9)
    convb[:, 9:12] = g["L0_tok_conv_b"].reshape(1, 3)
    d = {}
    d["x"] = patches(g["x"])
    d["ids"] = ids
    d["idsm"] = idsm
    d["lnwb"] = np.concatenate([patches(g["L0_tok_ln_w"][None]), patches(g["L0_tok_ln_b"][None])], axis=1)
    d["convb"] = convb
    d["projT"] = g["L0_tok_proj_w"].reshape(C, 3, 2, 8, 16).transpose(3, 4, 1, 2, 0).reshape(128, 3, 2, C)
    d["projb"] = np.broadcast_to(g["L0_tok_proj_b"], (ROWS, C))
    d["pos"] = np.concatenate([g["L0_tok_pos_emb"][0]] * GRP, axis=0)
    d["table"] = g["L0_txt_weight"]
    d["att"] = with_bias(g["L0_attn_qkv_w"], 0)
    d["attp"] = with_bias(g["L0_attn_proj_w"], g["L0_attn_proj_b"])
    d["gate0"] = halves(g["L0_ffn_Wg"])
    d["f1"] = np.stack([with_bias(g["L0_ffn_W1"][e].T, g["L0_ffn_b1"][e]) for e in range(E0)], axis=1)
    d["f2"] = g["L0_ffn_W2"].reshape(E0, FT, 128, C).transpose(2, 0, 1, 3)
    d["fb2"] = g["L0_ffn_b2"][None]
    qkv = g["L1_attn_qkv_weight"]
    d["tq"] = with_bias(qkv[:C], g["L1_attn_q_bias"])
    wtok = np.zeros((KA, 2, WTOK), f)
    wtok[:, :, 0:C] = with_bias(qkv[C:2 * C], 0)
    wtok[:, :, 2 * C:3 * C] = with_bias(qkv[C:2 * C], g["L1_attn_ttt_norm_bias"].reshape(C))
    wtok[:, :, 3 * C:] = with_bias(g["L1_attn_ttt_lr_weight"][:, 0, :], g["L1_attn_ttt_lr_bias"][:, 0])
    d["tk"] = wtok
    d["tv"] = with_bias(qkv[2 * C:], g["L1_attn_v_bias"])
    d["tkn"] = qkv[C:2 * C].reshape(2, HC, C).transpose(1, 0, 2)
    gamma = g["L1_attn_ttt_norm_weight"].reshape(C)
    d["tg"] = np.broadcast_to(gamma, (N, C))
    d["tgc"] = np.concatenate([gamma.reshape(2, HC).T, g["L1_attn_ttt_norm_bias"].reshape(2, HC).T], axis=1)
    inner = np.zeros((KA, 2, HC), f)
    for n in range(HEADS):
        m, a = n // HH, (n % HH) * HD
        inner[a:a + HD, m, a:a + HD] = g["L1_attn_W1"][n]
        inner[HC, m, a:a + HD] = g["L1_attn_b1"][n, 0]
    d["tw"] = inner
    d["tp"] = with_bias(g["L1_attn_proj_weight"], g["L1_attn_proj_bias"])
    d["scale"] = np.broadcast_to(g["L1_ffn_scale"], (N, C))
    d["gate1"] = with_bias(g["L1_ffn_gate_w"], g["L1_ffn_gate_b"])
    d["m1"] = np.stack([with_bias(g["L1_ffn_w1"][e].T, g["L1_ffn_b1"][e]) for e in range(E1)], axis=1)
    d["m2"] = np.stack([with_bias(g["L1_ffn_w2"][e].T, g["L1_ffn_b2"][e]) for e in range(E1)], axis=1)
    d["tri"] = np.triu(np.ones((N, N), f), 1)
    d["iota"] = np.concatenate([np.broadcast_to(np.arange(E1, dtype=f), (128, E1)), np.arange(128, dtype=f)[:, None]], axis=1)
    p_, b_, k_ = np.ogrid[0:N, 0:B, 0:TOPK]
    d["target"] = ((b_ * N + p_) * TOPK + k_).astype(f)
    d["dump"] = (DUMP + np.arange(128)[:, None] + 128 * np.arange(PADS)[None]).astype(f)
    d["ident"] = np.eye(128, dtype=f)
    m = np.ones((KA, HC), f)
    m[:HC] = np.kron(np.eye(HH, dtype=f), np.ones((HD, HD), f))
    d["mask"] = m
    return d


NAMES = """x ids idsm lnwb convb projT projb pos table att attp gate0 f1 f2 fb2 tq tk tv tkn tg tgc tw tp scale gate1 m1 m2
ident mask tri iota target dump""".split()


def kernel(**inputs):
    import concourse.bacc as _bacc
    from concourse.bass_utils import run_bass_kernel_spmd as _run

    nc = _bacc.Bacc("TRN2", target_bir_lowering=False, num_devices=1)
    d = layouts(inputs)
    arrays, args = {}, []
    for name in NAMES:
        a = np.ascontiguousarray(d[name])
        arrays[f"in_{name}"] = a
        args.append(nc.dram_tensor(f"in_{name}", a.shape, mybir.dt.from_np(a.dtype), kind="ExternalInput").ap())
    args.append(nc.dram_tensor("out_0", (B, N, C), F32, kind="ExternalOutput").ap())
    build(nc, *args)
    r = _run(nc, [arrays], core_ids=[0])
    return r.results[0]["out_0"]
```
